# Optimizing a Trainium2 kernel written in Bass

```python
import numpy as np
import jax
import jax.numpy as jnp

def _softmax(x, axis=-1):
    return jax.nn.softmax(x, axis=axis)

def _gelu(x):
    return jax.nn.gelu(x, approximate=True)

def _silu(x):
    return jax.nn.silu(x)

def _sigmoid(x):
    return jax.nn.sigmoid(x)

def _layernorm(x, axis=-1, eps=1e-05):
    m = jnp.mean(x, axis=axis, keepdims=True)
    v = jnp.var(x, axis=axis, keepdims=True)
    return (x - m) / jnp.sqrt(v + eps)

def _scatter_add(tgt, idx, src, axis=0):
    return tgt.at[idx].add(src)

def _segment_sum(src, seg, n):
    return jax.ops.segment_sum(src, seg, n)
kernel_name = 'mk_audio_tower_d1_tok_audfeat768_r4_43c7cb'

def setup_inputs(seed: int=0):
    np.random.seed(seed)
    _w = jnp.asarray

    def _rec_inputs():
        import jax
        import jax.numpy as jnp
        _rk = jax.random.key(seed)
        x = -0.000183583 + 0.999963 * jax.random.normal(jax.random.fold_in(_rk, 1), (64, 256, 192), jnp.float32)
        return x
    x = _rec_inputs()

    def _L0_tok_setup():
        import jax, jax.numpy as jnp
        import numpy as np
        KEEP_RATIO = 0.7
        LN_EPS = 1e-05
        key = jax.random.key(seed)
        k1, k2 = jax.random.split(key)
        B, N, D = (16, 2048, 192)
        x = jax.random.normal(k1, (B, N, D), dtype=jnp.float32)
        gamma = jnp.ones((D,), dtype=jnp.float32)
        beta = jnp.zeros((D,), dtype=jnp.float32)
        w = jax.random.normal(k2, (D,), dtype=jnp.float32) * (1.0 / np.sqrt(D))
        b = jnp.zeros((1,), dtype=jnp.float32)
        return {'x': x, 'gamma': gamma, 'beta': beta, 'w': w, 'b': b}
    _L0_tok_all = _L0_tok_setup()
    _L0_tok_in = {k: v for k, v in _L0_tok_all.items() if k in ('gamma', 'beta', 'w', 'b')}
    del _L0_tok_all

    def _L0_attn_setup():
        import jax, jax.numpy as jnp
        import numpy as np
        NH, DK, DV, D = (8, 64, 64, 192)
        DECAY = 0.95
        WRITE_STRENGTH = 0.1
        key = jax.random.key(seed)
        ks = jax.random.split(key, 6)
        s = 0.02
        return {'x': jax.random.normal(ks[0], (4, 1024, D), dtype=jnp.float32), 'w_key': jax.random.normal(ks[1], (NH * DK, D), dtype=jnp.float32) * s, 'w_value': jax.random.normal(ks[2], (NH * DV, D), dtype=jnp.float32) * s, 'w_query': jax.random.normal(ks[3], (NH * DK, D), dtype=jnp.float32) * s, 'w_gate': jax.random.normal(ks[4], (NH, D), dtype=jnp.float32) * s, 'w_out': jax.random.normal(ks[5], (D, NH * DV), dtype=jnp.float32) * s}
    _L0_attn_all = _L0_attn_setup()
    _L0_attn_in = {k: v for k, v in _L0_attn_all.items() if k in ('w_key', 'w_value', 'w_query', 'w_gate', 'w_out')}
    del _L0_attn_all

    def _L0_ffn_setup():
        import jax, jax.numpy as jnp
        import numpy as np
        DIM = 192
        HID = 128
        E = 16
        G = 8
        TOPK_G = 4
        TOPK_E = 4
        SCALE = 2.5
        B, S = (2, 512)
        key = jax.random.key(seed)
        ks = jax.random.split(key, 9)
        init = lambda k, shape: jax.random.normal(k, shape, dtype=jnp.float32) * 0.02
        z = lambda shape: jnp.zeros(shape, jnp.float32)
        return {'x': jax.random.normal(ks[0], (B, S, DIM), dtype=jnp.float32), 'gate_w': init(ks[1], (DIM, E)), 'gate_b': z((E,)), 'bias': z((E,)), 'Wu': init(ks[2], (E, DIM, HID)), 'bu': z((E, HID)), 'Wg': init(ks[3], (E, DIM, HID)), 'bg': z((E, HID)), 'Wd': init(ks[4], (E, HID, DIM)), 'bd': z((E, DIM)), 'sWu': init(ks[5], (DIM, HID)), 'sbu': z((HID,)), 'sWg': init(ks[6], (DIM, HID)), 'sbg': z((HID,)), 'sWd': init(ks[7], (HID, DIM)), 'sbd': z((DIM,))}
    _L0_ffn_all = _L0_ffn_setup()
    _L0_ffn_in = {k: v for k, v in _L0_ffn_all.items() if k in ('gate_w', 'gate_b', 'bias', 'Wu', 'bu', 'Wg', 'bg', 'Wd', 'bd', 'sWu', 'sbu', 'sWg', 'sbg', 'sWd', 'sbd')}
    del _L0_ffn_all
    return {'x': x, 'L0_tok_gamma': _L0_tok_in['gamma'], 'L0_tok_beta': _L0_tok_in['beta'], 'L0_tok_w': _L0_tok_in['w'], 'L0_tok_b': _L0_tok_in['b'], 'L0_attn_w_key': _L0_attn_in['w_key'], 'L0_attn_w_value': _L0_attn_in['w_value'], 'L0_attn_w_query': _L0_attn_in['w_query'], 'L0_attn_w_gate': _L0_attn_in['w_gate'], 'L0_attn_w_out': _L0_attn_in['w_out'], 'L0_ffn_gate_w': _L0_ffn_in['gate_w'], 'L0_ffn_gate_b': _L0_ffn_in['gate_b'], 'L0_ffn_bias': _L0_ffn_in['bias'], 'L0_ffn_Wu': _L0_ffn_in['Wu'], 'L0_ffn_bu': _L0_ffn_in['bu'], 'L0_ffn_Wg': _L0_ffn_in['Wg'], 'L0_ffn_bg': _L0_ffn_in['bg'], 'L0_ffn_Wd': _L0_ffn_in['Wd'], 'L0_ffn_bd': _L0_ffn_in['bd'], 'L0_ffn_sWu': _L0_ffn_in['sWu'], 'L0_ffn_sbu': _L0_ffn_in['sbu'], 'L0_ffn_sWg': _L0_ffn_in['sWg'], 'L0_ffn_sbg': _L0_ffn_in['sbg'], 'L0_ffn_sWd': _L0_ffn_in['sWd'], 'L0_ffn_sbd': _L0_ffn_in['sbd']}

def reference(x, L0_tok_gamma, L0_tok_beta, L0_tok_w, L0_tok_b, L0_attn_w_key, L0_attn_w_value, L0_attn_w_query, L0_attn_w_gate, L0_attn_w_out, L0_ffn_gate_w, L0_ffn_gate_b, L0_ffn_bias, L0_ffn_Wu, L0_ffn_bu, L0_ffn_Wg, L0_ffn_bg, L0_ffn_Wd, L0_ffn_bd, L0_ffn_sWu, L0_ffn_sbu, L0_ffn_sWg, L0_ffn_sbg, L0_ffn_sWd, L0_ffn_sbd):
    import jax
    import jax.numpy as jnp

    def _L0_tok_ref(x, gamma, beta, w, b):
        import jax, jax.numpy as jnp
        import numpy as np
        KEEP_RATIO = 0.7
        LN_EPS = 1e-05
        B, N, D = x.shape
        mu = jnp.mean(x, axis=-1, keepdims=True)
        var = jnp.mean(jnp.square(x - mu), axis=-1, keepdims=True)
        xn = (x - mu) * jax.lax.rsqrt(var + LN_EPS) * gamma + beta
        scores = jnp.einsum('bnd,d->bn', xn, w) + b[0]
        k = int(N * KEEP_RATIO)
        _, idx = jax.lax.top_k(scores, k)
        x_kept = jnp.take_along_axis(x, idx[..., None], axis=1)
        return x_kept

    def _L0_attn_ref(x, w_key, w_value, w_query, w_gate, w_out):
        import jax, jax.numpy as jnp
        import numpy as np
        NH, DK, DV, D = (8, 64, 64, 192)
        DECAY = 0.95
        WRITE_STRENGTH = 0.1
        B, S, _ = x.shape
        k = (x @ w_key.T).reshape(B, S, NH, DK)
        v = (x @ w_value.T).reshape(B, S, NH, DV)
        q = (x @ w_query.T).reshape(B, S, NH, DK)
        gate = jax.nn.sigmoid(x @ w_gate.T)
        k0 = k[0]
        v0 = v[0]
        g0 = gate[0]

        def step(fw, inp):
            q_t, k0_t, v0_t, g0_t = inp
            retrieved = jnp.einsum('bhk,hkv->bhv', q_t, fw)
            write = (WRITE_STRENGTH * g0_t)[:, None, None] * (k0_t[:, :, None] * v0_t[:, None, :])
            fw_new = DECAY * fw + jax.lax.stop_gradient(write)
            return (fw_new, retrieved)
        fw0 = jnp.zeros((NH, DK, DV), dtype=x.dtype)
        inputs = (q.transpose(1, 0, 2, 3), k0, v0, g0)
        _, retrieved = jax.lax.scan(step, fw0, inputs)
        retrieved = retrieved.transpose(1, 0, 2, 3).reshape(B, S, NH * DV)
        return x + retrieved @ w_out.T

    def _L0_ffn_ref(x, gate_w, gate_b, bias, Wu, bu, Wg, bg, Wd, bd, sWu, sbu, sWg, sbg, sWd, sbd):
        import jax, jax.numpy as jnp
        import numpy as np
        DIM = 192
        HID = 128
        E = 16
        G = 8
        TOPK_G = 4
        TOPK_E = 4
        SCALE = 2.5
        B, S = (2, 512)
        orig_shape = x.shape
        xt = x.reshape(-1, DIM)
        T = xt.shape[0]
        scores = jax.nn.softmax(xt @ gate_w + gate_b, axis=-1)
        orig_scores = jax.lax.stop_gradient(scores)
        s = scores + bias[None, :]
        s3 = s.reshape(T, G, E // G)
        group_scores = jax.lax.top_k(s3, 2)[0].sum(-1)
        gidx = jax.lax.top_k(group_scores, TOPK_G)[1]
        gmask = jnp.any(jnp.arange(G)[None, None, :] == gidx[:, :, None], axis=1)
        s_masked = jnp.where(gmask[:, :, None], s3, -jnp.inf).reshape(T, E)
        _, idx = jax.lax.top_k(s_masked, TOPK_E)
        w = jnp.take_along_axis(orig_scores, idx, axis=1) * SCALE
        w_full = jnp.zeros((T, E), xt.dtype).at[jnp.arange(T)[:, None], idx].add(w)
        up = jax.nn.silu(jnp.einsum('td,edh->teh', xt, Wu) + bu)
        gt = jnp.einsum('td,edh->teh', xt, Wg) + bg
        act = up * gt * w_full[:, :, None]
        y = jnp.einsum('teh,ehd->td', act, Wd) + w_full @ bd
        sh = jax.nn.silu(xt @ sWu + sbu) * (xt @ sWg + sbg)
        y = y + sh @ sWd + sbd
        return y.reshape(orig_shape)
    h = _L0_tok_ref(x, L0_tok_gamma, L0_tok_beta, L0_tok_w, L0_tok_b)
    h = h + _L0_attn_ref(_layernorm(h, axis=-1), L0_attn_w_key, L0_attn_w_value, L0_attn_w_query, L0_attn_w_gate, L0_attn_w_out)
    h = h + _L0_ffn_ref(_layernorm(h, axis=-1), L0_ffn_gate_w, L0_ffn_gate_b, L0_ffn_bias, L0_ffn_Wu, L0_ffn_bu, L0_ffn_Wg, L0_ffn_bg, L0_ffn_Wd, L0_ffn_bd, L0_ffn_sWu, L0_ffn_sbu, L0_ffn_sWg, L0_ffn_sbg, L0_ffn_sWd, L0_ffn_sbd)
    return h

_drawn_inputs = setup_inputs


def setup_inputs(seed=0):
    import zlib

    import numpy as np

    out = dict(_drawn_inputs(seed))
    spreads = {'L0_tok_gamma': (1.0, 0.2),
     'L0_tok_beta': (0.0, 0.1),
     'L0_ffn_gate_b': (0.0, 0.8),
     'L0_ffn_bias': (0.0, 0.371),
     'L0_ffn_bu': (0.0, 0.8),
     'L0_ffn_bg': (0.0, 0.8),
     'L0_ffn_bd': (0.0, 2.0),
     'L0_ffn_sbu': (0.0, 0.8),
     'L0_ffn_sbg': (0.0, 0.8),
     'L0_ffn_sbd': (0.0, 2.0)}
    factors = {'L0_attn_w_key': 7.778,
     'L0_attn_w_value': 7.169,
     'L0_attn_w_query': 7.139,
     'L0_attn_w_gate': 8.0,
     'L0_attn_w_out': 7.12,
     'L0_ffn_gate_w': 6.096,
     'L0_ffn_Wu': 8.0,
     'L0_ffn_Wg': 8.0,
     'L0_ffn_Wd': 8.0,
     'L0_ffn_sWu': 8.0,
     'L0_ffn_sWg': 8.0,
     'L0_ffn_sWd': 8.0}
    for name, (base, spread) in spreads.items():
        noise = np.random.default_rng([zlib.crc32(name.encode()), seed]).standard_normal(out[name].shape)
        drawn = base * np.exp(spread * noise) if base else spread * noise
        out[name] = jnp.asarray(drawn.astype(out[name].dtype))
    for name, factor in factors.items():
        out[name] = (out[name] * factor).astype(out[name].dtype)
    return out
```

```python
from contextlib import ExitStack

import concourse.bass as bass
from concourse import mybir

B, N, D = 64, 256, 192
KEEP = int(N * 0.7)
STEPS = KEEP + KEEP % 2
TILES = STEPS // 2
TPC = 6
CHUNKS = TILES // TPC
CS = 2 * TPC
NH, DK = 8, 64
E, G, HID = 16, 8, 128
TOP = 4
SCALE = 2.5
EPS = 1e-5
DECAY, WRITE = 0.95, 0.1
HD = D // 2
R = CS * NH
CT = TPC * 128
HT = CT // 2
ROUNDS = (STEPS + 7) // 8
XC = 8
XCHUNKS = 128 // XC
XBUF = 3
S0 = STEPS // 2
SPARE = 5


def tower(nc, a, out):
    f32, u32 = mybir.dt.float32, mybir.dt.uint32
    ALU, ACT, AX = mybir.AluOpType, mybir.ActivationFunctionType, mybir.AxisListType
    es = ExitStack()
    with es:
        sb = lambda name, shape, dt=f32: es.enter_context(nc.sbuf_tensor(name, shape, dt))
        pb = lambda name, p, n: es.enter_context(nc.psum_tensor(name, [p, n], f32))
        sem = lambda name: es.enter_context(nc.semaphore(name))

        h = sb("h", [128, TILES * D])
        ident = sb("ident", [128, 128])
        wu = sb("wu", [HD, 2, E * HID])
        wg = sb("wg", [HD, 2, E * HID])
        wd = sb("wd", [HID, E, D])
        swu = sb("swu", [HD, 2, HID])
        swg = sb("swg", [HD, 2, HID])
        swd = sb("swd", [HID, D])
        bu = sb("bu", [HID, E + 1])
        bg = sb("bg", [HID, E + 1])
        bd = sb("bd", [E, D])
        sbd = sb("sbd", [128, D])
        gw = sb("gw", [HD, 2, E])
        gb = sb("gb", [128, E])
        rb = sb("rb", [128, E])
        iota = sb("iota", [128, E])
        causal = sb("causal", [R, CS])
        tdecay = sb("tdecay", [128, TPC])
        AT = sb("AT", [HD, 2, STEPS * NH])
        BT = sb("BT", [HD, 2, STEPS * NH])
        W = sb("W", [HD, 2, D])
        mhalf = sb("mhalf", [128, 128])

        xin = h[:, 0:XBUF * XC * D].rearrange("p (i n) -> p i n", i=XBUF)
        xst = sb("xst", [128, 128, 6])
        xmean = sb("xmean", [128, 128])
        xscr = sb("xscr", [128, D])
        xdot = sb("xdot", [128, 128])
        xtmp = sb("xtmp", [128, 128])
        xvar = sb("xvar", [128, 128])
        xrs = sb("xrs", [128, 128])
        gam = sb("gam", [128, D])
        bet = sb("bet", [128, D])
        tw = sb("tw", [128, D])
        gamw = sb("gamw", [128, D])
        tb = sb("tb", [128, 1])
        tcon = sb("tcon", [128, 1])
        tcon2 = sb("tcon2", [128, 1])
        sc = sb("sc", [B, 2, N])
        m8 = sb("m8", [B, 8])
        idx = sb("idx", [B, ROUNDS * 8], u32)
        rowbase = sb("rowbase", [B, 1])
        rowi = sb("rowi", [B, ROUNDS * 8], u32)
        odd = sb("odd", [B, TILES], u32)
        gidx = sb("gidx", [128, TILES], u32)
        kidx = sb("kidx", [S0, 2], u32)
        kone = sb("kone", [S0, 2, 1], u32)

        spare = [SPARE * TPC * D]

        def in_h(p, x, y):
            lo = spare[0]
            spare[0] += x * y
            assert spare[0] <= TILES * D
            return h[0:p, lo:lo + x * y].rearrange("p (x y) -> p x y", x=x)

        wk, wq, wv, woT = (in_h(128, 4, D) for _ in range(4))
        wgt = sb("wgt", [HD, 2, NH])
        wgtb = sb("wgtb", [HD, 2, NH, HD])
        Gm, Hm = (in_h(HD, 2, NH * D).rearrange("p c (k d) -> p c k d", k=NH) for _ in range(2))
        x0 = sb("x0", [S0, 2, D])
        x0st = sb("x0st", [S0, 2, 6])
        x0mv = sb("x0mv", [S0, 2, 2])
        x0r = sb("x0r", [S0, 2])
        x0n = sb("x0n", [S0, 2, D])
        x0T = sb("x0T", [HD, 2, STEPS])
        wdec = sb("wdec", [HD, STEPS])
        gate = sb("gate", [HD, STEPS])

        st = sb("st", [128, TPC, 6])
        mv = sb("mv", [128, TPC, 2])
        rs = sb("rs", [128, TPC])
        xn = sb("xn", [128, TPC, D])
        xnT = sb("xnT", [HD, 2, CT])
        P = sb("P", [R, CT])
        ATc = sb("ATc", [HD, 2, R])
        BTc = sb("BTc", [HD, 2, R])
        Ac = sb("Ac", [R, D])
        Bc = sb("Bc", [R, D])
        lg = sb("lg", [128, TPC, E])
        mx = sb("mx", [128, TPC])
        ex = sb("ex", [128, TPC, E])
        rsum = sb("rsum", [128, TPC])
        rinv = sb("rinv", [128, TPC])
        prob = sb("prob", [128, TPC, E])
        sel = sb("sel", [128, TPC, E])
        gs = sb("gs", [128, TPC, G])
        g8 = sb("g8", [128, TPC, 8])
        gi = sb("gi", [128, TPC, 8], u32)
        hit = sb("hit", [128, TPC, E * TOP])
        gm = sb("gm", [128, TPC, G])
        wf = sb("wf", [128, TPC, E])
        wT = sb("wT", [E, CT])
        su = sb("su", [HID, 2, HT])
        ac = sb("ac", [HID, 2, HT])

        X = [pb("X0", 128, 512), pb("X1", 128, 512)]
        O = [pb("O0", 128, 512), pb("O1", 128, 512)]
        U = [pb("U0", 128, 512), pb("U1", 128, 512)]
        V = [pb("V0", 128, 512), pb("V1", 128, 512)]

        score_d = nc.dram_tensor("score_d", [128, 128], f32, kind="Internal").ap()
        row0_d = nc.dram_tensor("row0_d", [1, STEPS], u32, kind="Internal").ap()

        names = """weights x_loaded0 x_loaded1 x_loaded2 x_used stats_done mean_half mean_ready dot_done gamw_ready
        tcon_ready fold_ready var_ready rstd_ready score_ready score_out score_in top8 top8i top8r rowi_ready
        odd_ready odd_moved row0_out kidx_in kone_ready x0_in x0_stats x0_mv x0_rstd0 x0_rstd x0_norm x0_tp x0_copied wgtb_ready
        woT_tp woT_copied gh_mm gh_copied at_mm at_copied gate_mm gate_ready bt_scaled W_ready
        gath0 gath1 st_done_a st_done_b mv_done_a mv_done_b rs0_done_a rs0_done_b rs_done_a rs_done_b xn_done_a xn_done_b hx_done xn_tp xnT_done abT_done ab_tp ab_done
        s_mm P_done o_mm h1_done w_mm w_done lg_mm lg_done mx_done sub_done ex_done sum_done inv_done prob_done sel_done
        gs_done g8_done gi_done ghit_done gm_done pen_done msk_done e8_done ei_done ehit_done cnt_done wf_done
        wT_tp wT_done up_mm su_done ac_done y_mm y_done hs_done stored""".split()
        s = {n: sem(n) for n in names}
        block = es.enter_context(nc.Block())

        def _bc(ap, pos, n):
            shape = list(ap.shape)
            u = ap.unsqueeze(pos)
            shape.insert(pos, n)
            return u.to_broadcast(shape)

        loads = []

        def wait_alone(eng, what, count):
            eng.wait_ge(s["weights"], NLOAD)
            eng.wait_ge(what, count)

        @block.sync
        def _(sp):
            def load(dst, src):
                sp.dma_start(dst, src).then_inc(s["weights"], 16)
                loads.append(1)

            def xload(i):
                sp.dma_start(xin[:, i % XBUF, :], a["x"].rearrange("b (u n) d -> (b u) (n d)", u=2)
                             [:, i * XC * D:(i + 1) * XC * D]).then_inc(s[f"x_loaded{i % XBUF}"], 16)

            row = lambda v, p: v.rearrange("(a n) -> a n", a=1).to_broadcast([p, v.shape[0]])
            load(gam[:, :], row(a["L0_tok_gamma"], 128))
            load(tw[:, :], row(a["L0_tok_w"], 128))
            xload(0)
            xload(1)
            xload(2)
            load(bet[:, :], row(a["L0_tok_beta"], 128))
            load(tb[:, :], row(a["L0_tok_b"], 128))
            load(ident[:, :], a["c_ident"])
            load(rowbase[:, :], a["c_rowbase"])
            load(mhalf[:, :], a["c_mhalf"])
            load(wk[:, :, :], a["L0_attn_w_key"].rearrange("(c p) d -> p c d", p=128))
            load(wq[:, :, :], a["L0_attn_w_query"].rearrange("(c p) d -> p c d", p=128))
            load(wv[:, :, :], a["L0_attn_w_value"].rearrange("(c p) d -> p c d", p=128))
            load(woT[:, :, :], a["L0_attn_w_out"].rearrange("(c p) d -> p c d", p=128))
            load(wgt[:, :, :], a["L0_attn_w_gate"].rearrange("(c p) k -> p c k", p=HD))
            load(wdec[:, :], a["c_wdec"])
            load(causal[:, :], a["c_causal"])
            load(tdecay[:, :], a["c_tdecay"])
            load(iota[:, :], a["c_iota"])
            load(gw[:, :, :], a["L0_ffn_gate_w"].rearrange("(c p) e -> p c e", p=HD))
            load(gb[:, :], row(a["L0_ffn_gate_b"], 128))
            load(rb[:, :], row(a["L0_ffn_bias"], 128))
            load(sbd[:, :], row(a["L0_ffn_sbd"], 128))
            load(bd[:, :], a["L0_ffn_bd"])
            load(bu[:, 0:E], a["L0_ffn_bu"])
            load(bg[:, 0:E], a["L0_ffn_bg"])
            load(bu[:, E:E + 1], a["L0_ffn_sbu"].rearrange("(h o) -> h o", o=1))
            load(bg[:, E:E + 1], a["L0_ffn_sbg"].rearrange("(h o) -> h o", o=1))
            for c in range(2):
                load(wu[:, c, :].rearrange("p (e n) -> p e n", e=E), a["L0_ffn_Wu"][:, c * HD:(c + 1) * HD, :].rearrange("e p n -> p e n"))
                load(wg[:, c, :].rearrange("p (e n) -> p e n", e=E), a["L0_ffn_Wg"][:, c * HD:(c + 1) * HD, :].rearrange("e p n -> p e n"))
            load(wd[:, :, :], a["L0_ffn_Wd"].rearrange("e h d -> h e d"))
            load(swu[:, :, :], a["L0_ffn_sWu"].rearrange("(c p) n -> p c n", p=HD))
            load(swg[:, :, :], a["L0_ffn_sWg"].rearrange("(c p) n -> p c n", p=HD))
            load(swd[:, :], a["L0_ffn_sWd"])
            for i in range(XBUF, XCHUNKS):
                sp.wait_ge(s["x_used"], i - XBUF + 1)
                xload(i)
            sp.wait_ge(s["score_ready"], 1)
            sp.dma_start(score_d, xdot[:, :]).then_inc(s["score_out"], 16)
            sp.wait_ge(s["score_out"], 16)
            sp.dma_start(sc[:, 0, :], score_d.rearrange("(b u) n -> b (u n)", u=2)).then_inc(s["score_in"], 16)
            sp.wait_ge(s["odd_ready"], 1)
            sp.dma_start(row0_d, rowi[0:1, 0:STEPS]).then_inc(s["row0_out"], 16)
            sp.dma_start(gidx[64:128, :], odd[:, :]).then_inc(s["odd_moved"], 16)
            sp.wait_ge(s["row0_out"], 16)
            sp.dma_start(kidx[:, :], row0_d.rearrange("a (p i) -> (a p) i", i=2)).then_inc(s["kidx_in"], 16)

            hv = h[:, :].rearrange("p (t d) -> p t d", d=D)

            outp = out.rearrange("b t d -> b (t d)")
            with sp.Fori(0, CHUNKS - 1) as c:
                sp.wait_ge(s["y_done"], (c + 1) * (E + 1) * TPC)
                for u in range(2):
                    src = h[64 * u:64 * u + 64, bass.ds(c * (TPC * D), TPC * D)].rearrange("p (j d) -> p j d", d=D)
                    dst = outp[:, bass.ds(c * (CS * D), CS * D)].rearrange("b (j w d) -> b j w d", w=2, d=D)[:, :, u, :]
                    sp.dma_start(dst, src).then_inc(s["stored"], 16)
            sp.wait_ge(s["y_done"], CHUNKS * (E + 1) * TPC)
            for u in range(2):
                tiles = TPC - u
                base = (CHUNKS - 1) * CS
                src = hv[64 * u:64 * u + 64, (CHUNKS - 1) * TPC:(CHUNKS - 1) * TPC + tiles, :]
                sp.dma_start(out[:, base + u:base + u + 2 * tiles - 1:2, :], src).then_inc(s["stored"], 16)
            sp.wait_ge(s["stored"], 2 * CHUNKS * 16)

        NLOAD = 16 * len(loads)

        @block.gpsimd
        def _(pool):
            pool.wait_ge(s["weights"], NLOAD)
            pool.wait_ge(s["var_ready"], 1)
            nc.gpsimd.tensor_tensor(xrs[:, :], xvar[:, :], mhalf[:, :], ALU.pow).then_inc(s["rstd_ready"], 1)
            xrows = a["x"].rearrange("b n d -> (b n) d")
            pool.wait_ge(s["kone_ready"], 1)
            for i in range(2):
                pool.indirect_dma_start(out=x0[:, i, :], out_offset=None, in_=xrows,
                                        in_offset=bass.IndirectOffsetOnAxis(ap=kone[:, i, :], axis=0)).then_inc(s["x0_in"], 16)
            pool.wait_ge(s["x0_mv"], 1)
            nc.gpsimd.tensor_scalar(x0r[:, :], x0mv[:, :, 1], EPS, None, ALU.add).then_inc(s["x0_rstd0"], 1)
            pool.wait_ge(s["x0_rstd0"], 1)
            nc.gpsimd.tensor_tensor(x0r[:, :], x0r[:, :], mhalf[0:S0, 0:2], ALU.pow).then_inc(s["x0_rstd"], 1)
            pool.wait_ge(s["odd_moved"], 16)

            def gather(t, k):
                pool.indirect_dma_start(out=h[:, t * D:(t + 1) * D], out_offset=None, in_=xrows,
                                        in_offset=bass.IndirectOffsetOnAxis(ap=gidx[:, t:t + 1], axis=0)).then_inc(s[f"gath{k}"], 16)
            for c in range(CHUNKS):
                if c == SPARE:
                    pool.wait_ge(s["at_mm"], 4 * NH)
                if c >= 2:
                    pool.wait_ge(s[f"gath{c % 2}"], 16 * TPC * (c // 2))
                for j in range(TPC):
                    gather(c * TPC + j, c % 2)
            with pool.Fori(1, CHUNKS + 1) as nth:
                c = nth - 1
                wait_alone(pool, s["mv_done_a"], nth)
                nc.gpsimd.tensor_scalar(rs[:, :], mv[:, :, 1], EPS, None, ALU.add).then_inc(s["rs0_done_a"], 1)
                wait_alone(pool, s["rs0_done_a"], nth)
                nc.gpsimd.tensor_tensor(rs[:, :], rs[:, :], mhalf[:, 0:TPC], ALU.pow).then_inc(s["rs_done_a"], 1)
                wait_alone(pool, s["xn_done_a"], nth)
                hc = h[:, bass.ds(c * (TPC * D), TPC * D)]
                nc.gpsimd.tensor_tensor(hc, hc, xn[:, :, :].rearrange("p j d -> p (j d)"), ALU.add).then_inc(s["hx_done"], 1)
                wait_alone(pool, s["mv_done_b"], nth)
                nc.gpsimd.tensor_scalar(rs[:, :], mv[:, :, 1], EPS, None, ALU.add).then_inc(s["rs0_done_b"], 1)
                wait_alone(pool, s["rs0_done_b"], nth)
                nc.gpsimd.tensor_tensor(rs[:, :], rs[:, :], mhalf[:, 0:TPC], ALU.pow).then_inc(s["rs_done_b"], 1)
                wait_alone(pool, s["xn_done_b"], nth)
                h3 = hc.rearrange("p (j d) -> p j d", d=D)
                nc.gpsimd.tensor_tensor(h3, h3, _bc(sbd[:, :], 1, TPC), ALU.add).then_inc(s["hs_done"], 1)

        @block.vector
        def _(dve):
            v = nc.vector
            dve.wait_ge(s["weights"], NLOAD)
            v.tensor_tensor(gamw[:, :], gam[:, :], tw[:, :], ALU.mult).then_inc(s["gamw_ready"], 1)
            v.scalar_tensor_tensor(out=xscr[:, :], in0=bet[:, :], scalar=1.0, in1=tw[:, :], op0=ALU.mult, op1=ALU.mult,
                                   accum_out=tcon[:, :]).then_inc(s["tcon_ready"], 1)
            v.memset(W[:, :, :], 0.0).then_inc(s["W_ready"], 1)
            dve.wait_ge(s["tcon_ready"], 1)
            v.tensor_tensor(tcon2[:, :], tcon[:, :], tb[:, :], ALU.add).then_inc(s["tcon_ready"], 1)
            dve.wait_ge(s["gamw_ready"], 1)
            for i in range(XCHUNKS):
                dve.wait_ge(s[f"x_loaded{i % XBUF}"], 16 * (i // XBUF + 1))
                for k in range(XC):
                    xt = xin[:, i % XBUF, k * D:(k + 1) * D]
                    last = v.bn_stats(xst[:, i * XC + k, :], xt)
                last.then_inc(s["stats_done"], 1)
                r = slice(i * XC, (i + 1) * XC)
                dve.wait_ge(s["stats_done"], i + 1)
                v.tensor_tensor(xtmp[:, r], xst[:, r, 1], xst[:, r, 4], ALU.add).then_inc(s["mean_half"], 1)
                dve.wait_ge(s["mean_half"], i + 1)
                v.tensor_scalar(xmean[:, r], xtmp[:, r], 0.5, None, ALU.mult).then_inc(s["mean_ready"], 1)
                dve.wait_ge(s["mean_ready"], i + 1)
                for k in range(XC):
                    xt = xin[:, i % XBUF, k * D:(k + 1) * D]
                    n = i * XC + k
                    last = v.scalar_tensor_tensor(out=xt, in0=xt, scalar=xmean[:, n:n + 1], in1=gamw[:, :],
                                                  op0=ALU.subtract, op1=ALU.mult, accum_out=xdot[:, n:n + 1])
                last.then_inc(s["x_used"], 1)
            v.tensor_tensor(xtmp[:, :], xst[:, :, 1], xst[:, :, 4], ALU.subtract).then_inc(s["fold_ready"], 1)
            v.tensor_tensor(xvar[:, :], xst[:, :, 2], xst[:, :, 5], ALU.add).then_inc(s["fold_ready"], 1)
            dve.wait_ge(s["fold_ready"], 2)
            v.tensor_tensor(xtmp[:, :], xtmp[:, :], xtmp[:, :], ALU.mult).then_inc(s["fold_ready"], 1)
            v.tensor_scalar(xvar[:, :], xvar[:, :], 1.0 / D, EPS, ALU.mult, ALU.add).then_inc(s["fold_ready"], 1)
            dve.wait_ge(s["fold_ready"], 4)
            v.scalar_tensor_tensor(out=xvar[:, :], in0=xtmp[:, :], scalar=0.25, in1=xvar[:, :], op0=ALU.mult, op1=ALU.add)\
                .then_inc(s["var_ready"], 1)
            dve.wait_ge(s["rstd_ready"], 1)
            dve.wait_ge(s["var_ready"], 1)
            v.tensor_tensor(xtmp[:, :], xrs[:, :], xrs[:, :], ALU.mult).then_inc(s["fold_ready"], 1)
            dve.wait_ge(s["fold_ready"], 5)
            v.tensor_tensor(xtmp[:, :], xtmp[:, :], xvar[:, :], ALU.mult).then_inc(s["fold_ready"], 1)
            dve.wait_ge(s["fold_ready"], 6)
            v.tensor_scalar(xtmp[:, :], xtmp[:, :], -0.5, 1.5, ALU.mult, ALU.add).then_inc(s["fold_ready"], 1)
            dve.wait_ge(s["x_used"], XCHUNKS)
            v.tensor_tensor(xdot[:, :], xdot[:, :], xrs[:, :], ALU.mult).then_inc(s["fold_ready"], 1)
            dve.wait_ge(s["fold_ready"], 8)
            v.tensor_tensor(xdot[:, :], xdot[:, :], xtmp[:, :], ALU.mult).then_inc(s["fold_ready"], 1)
            dve.wait_ge(s["fold_ready"], 9)
            dve.wait_ge(s["tcon_ready"], 2)
            v.tensor_scalar(xdot[:, :], xdot[:, :], tcon2[:, :], None, ALU.add).then_inc(s["score_ready"], 1)
            dve.wait_ge(s["score_in"], 16)
            for r in range(ROUNDS):
                cur, nxt = sc[:, r % 2, :], sc[:, (r + 1) % 2, :]
                if r:
                    dve.wait_ge(s["top8r"], r)
                v.max(m8[:, :], cur).then_inc(s["top8"], 1)
                dve.wait_ge(s["top8"], r + 1)
                v.max_index(idx[:, 8 * r:8 * r + 8], m8[:, :], cur).then_inc(s["top8i"], 1)
                v.match_replace(nxt, m8[:, :], cur, -3.0e38).then_inc(s["top8r"], 1)
            dve.wait_ge(s["top8i"], ROUNDS)
            v.tensor_scalar(rowi[:, :], idx[:, :], rowbase[:, :], None, ALU.add).then_inc(s["rowi_ready"], 1)
            dve.wait_ge(s["rowi_ready"], 1)
            v.tensor_copy(gidx[0:64, :], rowi[:, 0:STEPS:2])
            v.tensor_copy(odd[:, :], rowi[:, 1:STEPS:2]).then_inc(s["odd_ready"], 1)
            dve.wait_ge(s["kidx_in"], 16)
            v.tensor_copy(kone[:, :, 0], kidx[:, :]).then_inc(s["kone_ready"], 1)

            dve.wait_ge(s["x0_in"], 32)
            for i in range(2):
                last = v.bn_stats(x0st[:, i, :], x0[:, i, :])
            last.then_inc(s["x0_stats"], 1)
            dve.wait_ge(s["x0_stats"], 1)
            for i in range(2):
                last = v.bn_aggr(x0mv[:, i, :], x0st[:, i, :])
            last.then_inc(s["x0_mv"], 1)
            dve.wait_ge(s["x0_mv"], 1)
            dve.wait_ge(s["x0_rstd"], 1)
            for i in range(2):
                last = v.tensor_scalar(x0n[:, i, :], x0[:, i, :], x0mv[:, i, 0:1], x0r[:, i:i + 1], ALU.subtract, ALU.mult)
            last.then_inc(s["x0_norm"], 1)
            for hh in range(NH):
                dve.wait_ge(s["gate_ready"], hh + 1)
                v.tensor_tensor(gate[:, :], gate[:, :], wdec[:, :], ALU.mult).then_inc(s["bt_scaled"], 1)
                dve.wait_ge(s["bt_scaled"], 3 * hh + 1)
                dve.wait_ge(s["at_mm"], 4 * hh + 4)
                for c in range(2):
                    dst = BT[:, c, :].rearrange("p (s k) -> p s k", k=NH)[:, :, hh]
                    v.tensor_tensor(dst, (V[c])[0:HD, 0:STEPS], gate[:, :], ALU.mult).then_inc(s["bt_scaled"], 1)

            def norm(c, nth, n):
                hc = h[:, bass.ds(c * (TPC * D), TPC * D)].rearrange("p (j d) -> p j d", d=D)
                for j in range(TPC):
                    last = v.bn_stats(st[:, j, :], hc[:, j, :])
                last.then_inc(s[f"st_done_{'ab'[n]}"], 1)
                wait_alone(dve, s[f"st_done_{'ab'[n]}"], nth)
                for j in range(TPC):
                    last = v.bn_aggr(mv[:, j, :], st[:, j, :])
                last.then_inc(s[f"mv_done_{'ab'[n]}"], 1)
                dve.wait_ge(s[f"mv_done_{'ab'[n]}"], c + 1)
                dve.wait_ge(s[f"rs_done_{'ab'[n]}"], c + 1)
                dve.wait_ge(s["xn_tp"], TPC * (2 * c + n))
                for j in range(TPC):
                    last = v.tensor_scalar(xn[:, j, :], hc[:, j, :], mv[:, j, 0:1], rs[:, j:j + 1], ALU.subtract, ALU.mult)
                last.then_inc(s[f"xn_done_{'ab'[n]}"], 1)

            for n in range(2):
                dve.wait_ge(s[f"gath{n}"], 16 * TPC * ((CHUNKS + 1 - n) // 2))
            with dve.Fori(1, CHUNKS + 1) as nth:
                c = nth - 1
                hc = h[:, bass.ds(c * (TPC * D), TPC * D)].rearrange("p (j d) -> p j d", d=D)
                norm(c, nth, 0)
                for k in range(2):
                    dve.wait_ge(s["s_mm"], 2 * c + k + 1)
                    dve.wait_ge(s["w_mm"], c)
                    dst = P[:, k * HT:(k + 1) * HT].rearrange("p (t b) -> p t b", b=64)
                    v.tensor_tensor(dst, U[k][0:R, 0:HT].rearrange("p (t b) -> p t b", b=64),
                                    _bc(causal[:, k * TPC:(k + 1) * TPC], 2, 64), ALU.mult).then_inc(s["P_done"], 1)
                dve.wait_ge(s["hx_done"], c + 1)
                for j in range(TPC):
                    dve.wait_ge(s["o_mm"], TPC * c + j + 1)
                    v.scalar_tensor_tensor(out=hc[:, j, :], in0=O[j % 2][:, 0:D], scalar=tdecay[:, j:j + 1], in1=hc[:, j, :],
                                           op0=ALU.mult, op1=ALU.add).then_inc(s["h1_done"], 1)
                dve.wait_ge(s["h1_done"], TPC * (c + 1))
                dve.wait_ge(s["w_mm"], c + 1)
                dve.wait_ge(s["W_ready"], c + 1)
                v.scalar_tensor_tensor(out=W[:, :, :].rearrange("p c d -> p (c d)"), in0=W[:, :, :].rearrange("p c d -> p (c d)"),
                                       scalar=DECAY ** CS, in1=V[0][0:HD, 0:2 * D],
                                       op0=ALU.mult, op1=ALU.add).then_inc(s["W_ready"], 1)
                norm(c, nth, 1)
                dve.wait_ge(s["lg_mm"], c + 1)
                v.tensor_tensor(lg[:, :, :], X[0][:, 0:TPC * E].rearrange("p (j e) -> p j e", e=E), _bc(gb[:, :], 1, TPC), ALU.add)\
                    .then_inc(s["lg_done"], 1)
                dve.wait_ge(s["lg_done"], c + 1)
                v.tensor_reduce(mx[:, :], lg[:, :, :], AX.X, ALU.max).then_inc(s["mx_done"], 1)
                dve.wait_ge(s["mx_done"], c + 1)
                v.tensor_tensor(lg[:, :, :], lg[:, :, :], _bc(mx[:, :], 2, E), ALU.subtract).then_inc(s["sub_done"], 1)
                dve.wait_ge(s["ex_done"], c + 1)
                v.tensor_reduce(rsum[:, :], ex[:, :, :], AX.X, ALU.add).then_inc(s["sum_done"], 1)
                dve.wait_ge(s["sum_done"], c + 1)
                v.reciprocal(rinv[:, :], rsum[:, :]).then_inc(s["inv_done"], 1)
                dve.wait_ge(s["inv_done"], c + 1)
                v.tensor_tensor(prob[:, :, :], ex[:, :, :], _bc(rinv[:, :], 2, E), ALU.mult).then_inc(s["prob_done"], 1)
                dve.wait_ge(s["prob_done"], c + 1)
                v.tensor_tensor(sel[:, :, :], prob[:, :, :], _bc(rb[:, :], 1, TPC), ALU.add).then_inc(s["sel_done"], 1)
                dve.wait_ge(s["sel_done"], c + 1)
                pair = sel[:, :, :].rearrange("p j (g u) -> p j g u", u=2)
                v.tensor_tensor(gs[:, :, :], pair[:, :, :, 0], pair[:, :, :, 1], ALU.add).then_inc(s["gs_done"], 1)
                wait_alone(dve, s["gs_done"], nth)
                for j in range(TPC):
                    last = v.max(g8[:, j, :], gs[:, j, :])
                last.then_inc(s["g8_done"], 1)
                wait_alone(dve, s["g8_done"], nth)
                for j in range(TPC):
                    last = v.max_index(gi[:, j, :], g8[:, j, :], gs[:, j, :])
                last.then_inc(s["gi_done"], 1)
                dve.wait_ge(s["gi_done"], c + 1)
                for k in range(TOP):
                    hk = hit[:, :, :].rearrange("p j (g k) -> p j g k", k=TOP)[:, :, 0:G, k]
                    last = v.tensor_tensor(hk, _bc(gi[:, :, k], 2, G), _bc(iota[:, 0:G], 1, TPC), ALU.is_equal)
                last.then_inc(s["ghit_done"], 1)
                dve.wait_ge(s["ghit_done"], c + 1)
                v.tensor_reduce(gm[:, :, :], hit[:, :, 0:G * TOP].rearrange("p j (g k) -> p j g k", k=TOP), AX.X, ALU.add)\
                    .then_inc(s["gm_done"], 1)
                dve.wait_ge(s["gm_done"], c + 1)
                v.tensor_scalar(gm[:, :, :], gm[:, :, :], -1.0, 1.0e30, ALU.add, ALU.mult).then_inc(s["pen_done"], 1)
                dve.wait_ge(s["pen_done"], c + 1)
                for u in range(2):
                    last = v.tensor_tensor(pair[:, :, :, u], pair[:, :, :, u], gm[:, :, :], ALU.add)
                last.then_inc(s["msk_done"], 1)
                wait_alone(dve, s["msk_done"], nth)
                for j in range(TPC):
                    last = v.max(g8[:, j, :], sel[:, j, :])
                last.then_inc(s["e8_done"], 1)
                wait_alone(dve, s["e8_done"], nth)
                for j in range(TPC):
                    last = v.max_index(gi[:, j, :], g8[:, j, :], sel[:, j, :])
                last.then_inc(s["ei_done"], 1)
                dve.wait_ge(s["ei_done"], c + 1)
                for k in range(TOP):
                    hk = hit[:, :, :].rearrange("p j (e k) -> p j e k", k=TOP)[:, :, :, k]
                    last = v.tensor_tensor(hk, _bc(gi[:, :, k], 2, E), _bc(iota[:, :], 1, TPC), ALU.is_equal)
                last.then_inc(s["ehit_done"], 1)
                dve.wait_ge(s["ehit_done"], c + 1)
                v.tensor_reduce(wf[:, :, :], hit[:, :, :].rearrange("p j (e k) -> p j e k", k=TOP), AX.X, ALU.add)\
                    .then_inc(s["cnt_done"], 1)
                dve.wait_ge(s["cnt_done"], c + 1)
                w2 = wf[:, :, :].rearrange("p j e -> p (j e)")
                v.scalar_tensor_tensor(out=w2, in0=w2, scalar=SCALE, in1=prob[:, :, :].rearrange("p j e -> p (j e)"),
                                       op0=ALU.mult, op1=ALU.mult).then_inc(s["wf_done"], 1)
                dve.wait_ge(s["wf_done"], c + 1)
                dve.wait_ge(s["hs_done"], c + 1)
                UN = 2 * (E + 1)

                def product(k):
                    e, half = divmod(k, 2)
                    dve.wait_ge(s["su_done"], UN * c + k + 1)
                    if k >= 2:
                        dve.wait_ge(s["y_mm"], 3 * (UN * c + k - 1))
                    v.scalar_tensor_tensor(out=ac[:, k % 2, :], in0=V[k % 2][:, 0:HT], scalar=bg[:, e:e + 1], in1=su[:, k % 2, :],
                                           op0=ALU.add, op1=ALU.mult).then_inc(s["ac_done"], 1)

                def collect(k):
                    e, half = divmod(k, 2)
                    for j in range(3):
                        n = 3 * k + j
                        dve.wait_ge(s["y_mm"], 3 * UN * c + n + 1)
                        if k >= 2:
                            dve.wait_ge(s["y_done"], 3 * UN * c + n - 5)
                        t = hc[:, 3 * half + j, :]
                        if e < E:
                            v.scalar_tensor_tensor(out=t, in0=O[n % 2][:, 0:D], scalar=wf[:, 3 * half + j, e:e + 1], in1=t,
                                                   op0=ALU.mult, op1=ALU.add).then_inc(s["y_done"], 1)
                        else:
                            v.tensor_tensor(t, O[n % 2][:, 0:D], t, ALU.add).then_inc(s["y_done"], 1)
                product(0)
                for k in range(1, UN):
                    product(k)
                    collect(k - 1)
                collect(UN - 1)

        @block.scalar
        def _(act):
            ac_ = nc.scalar
            act.wait_ge(s["weights"], NLOAD)
            for m, dst in enumerate((Gm, Hm)):
                for hh in range(NH):
                    n = m * NH + hh
                    act.wait_ge(s["gh_mm"], n + 1)
                    ac_.activation(dst[:, :, hh, :], O[n % 2][0:HD, 0:2 * D].rearrange("p (c d) -> p c d", c=2), ACT.Copy)\
                        .then_inc(s["gh_copied"], 1)
            for c in range(2):
                last = ac_.activation(wgtb[:, c, :, :], _bc(wgt[:, c, :], 2, HD), ACT.Copy)
            last.then_inc(s["wgtb_ready"], 1)
            for i in range(2):
                act.wait_ge(s["x0_tp"], i + 1)
                ac_.activation(x0T[:, :, i:STEPS:2], X[i][0:HD, 0:256].rearrange("p (c t) -> p c t", c=2)[:, :, 0:S0], ACT.Copy)\
                    .then_inc(s["x0_copied"], 1)
            for hh in range(NH):
                act.wait_ge(s["gate_mm"], hh + 1)
                if hh:
                    act.wait_ge(s["bt_scaled"], 3 * hh)
                ac_.activation(gate[:, :], O[0][0:HD, 0:STEPS], ACT.Sigmoid).then_inc(s["gate_ready"], 1)
                for c in range(2):
                    act.wait_ge(s["at_mm"], 4 * hh + c + 1)
                    dst = AT[:, c, :].rearrange("p (s k) -> p s k", k=NH)[:, :, hh]
                    ac_.activation(dst, U[c][0:HD, 0:STEPS], ACT.Copy).then_inc(s["at_copied"], 1)
            act.wait_ge(s["bt_scaled"], 3 * NH)
            act.wait_ge(s["at_copied"], 2 * NH)
            with act.Fori(0, CHUNKS) as c:
                act.wait_ge(s["ab_tp"], c)
                act.wait_ge(s["s_mm"], 2 * c)
                ac_.activation(ATc[:, :, :], AT[:, :, bass.ds(c * R, R)], ACT.Copy)
                ac_.activation(BTc[:, :, :], BT[:, :, bass.ds(c * R, R)], ACT.Copy).then_inc(s["abT_done"], 1)
                act.wait_ge(s["ab_tp"], c + 1)
                act.wait_ge(s["w_mm"], c)
                ac_.activation(Ac[:, :], V[1][0:R, 0:D], ACT.Copy, scale=DECAY ** CS)
                ac_.activation(Bc[:, :], V[1][0:R, D:2 * D], ACT.Copy).then_inc(s["ab_done"], 1)

                def evac_T(n):
                    for j in range(TPC):
                        act.wait_ge(s["xn_tp"], TPC * (2 * c + n) + j + 1)
                        ac_.activation(xnT[:, :, j * 128:(j + 1) * 128], X[j % 2][0:HD, 0:256].rearrange("p (c t) -> p c t", c=2),
                                       ACT.Copy).then_inc(s["xnT_done"], 1)
                act.wait_ge(s["y_mm"], 3 * 2 * (E + 1) * c)
                evac_T(0)
                act.wait_ge(s["o_mm"], TPC * (c + 1))
                evac_T(1)
                act.wait_ge(s["sub_done"], c + 1)
                ac_.activation(ex[:, :, :], lg[:, :, :], ACT.Exp).then_inc(s["ex_done"], 1)

                UN = 2 * (E + 1)
                for k in range(UN):
                    e, half = divmod(k, 2)
                    if k == UN - 2:
                        for n in range(2):
                            act.wait_ge(s["wT_tp"], 2 * c + n + 1)
                            ac_.activation(wT[:, n * HT:(n + 1) * HT], X[n][0:E, 0:HT], ACT.Copy).then_inc(s["wT_done"], 1)
                    act.wait_ge(s["up_mm"], UN * c + k + 1)
                    if k >= 2:
                        act.wait_ge(s["ac_done"], UN * c + k - 1)
                    ac_.activation(su[:, k % 2, :], U[k % 2][:, 0:HT], ACT.Silu, bias=bu[:, e:e + 1]).then_inc(s["su_done"], 1)

        @block.tensor
        def _(pe):
            mm = nc.tensor.matmul
            pe.wait_ge(s["weights"], NLOAD)
            for m, (left, right) in enumerate(((wk, wq), (wv, woT))):
                for hh in range(NH):
                    n = m * NH + hh
                    if n >= 2:
                        pe.wait_ge(s["gh_copied"], n - 1)
                    r = slice(64 * (hh % 2), 64 * (hh % 2) + 64)
                    for c in range(2):
                        last = mm(O[n % 2][0:HD, c * D:(c + 1) * D], left[r, hh // 2, c * HD:(c + 1) * HD], right[r, hh // 2, :],
                                  start=True, stop=True)
                    last.then_inc(s["gh_mm"], 1)
            pe.wait_ge(s["gh_copied"], 2 * NH)
            pe.wait_ge(s["wgtb_ready"], 1)
            pe.wait_ge(s["x0_norm"], 1)
            for i in range(2):
                for c in range(2):
                    last = nc.tensor.transpose(X[i][0:HD, c * 128:c * 128 + S0], x0n[:, i, c * HD:(c + 1) * HD], ident[0:S0, 0:S0])
                last.then_inc(s["x0_tp"], 1)
            pe.wait_ge(s["x0_copied"], 2)
            for hh in range(NH):
                if hh:
                    pe.wait_ge(s["gate_ready"], hh)
                for k in range(2):
                    last = mm(O[0][0:HD, 0:STEPS], wgtb[:, k, hh, :], x0T[:, k, :], start=(k == 0), stop=(k == 1))
                last.then_inc(s["gate_mm"], 1)
                for m, (w, bank) in enumerate(((Gm, U), (Hm, V))):
                    if hh:
                        if m == 0:
                            pe.wait_ge(s["at_copied"], 2 * hh)
                        else:
                            pe.wait_ge(s["bt_scaled"], 3 * hh)
                    for c in range(2):
                        for k in range(2):
                            last = mm(bank[c][0:HD, 0:STEPS], w[:, k, hh, c * HD:(c + 1) * HD], x0T[:, k, :], start=(k == 0), stop=(k == 1))
                        last.then_inc(s["at_mm"], 1)
            pe.wait_ge(s["at_copied"], 2 * NH)
            pe.wait_ge(s["bt_scaled"], 3 * NH)
            UN = 2 * (E + 1)
            with pe.Fori(0, CHUNKS) as c:
                pe.wait_ge(s["abT_done"], c + 1)
                pe.wait_ge(s["ac_done"], UN * c)
                for m, src in enumerate((ATc, BTc)):
                    for k in range(2):
                        last = nc.tensor.transpose(V[1][0:R, m * D + k * HD:m * D + (k + 1) * HD], src[:, k, :], ident[0:HD, 0:HD])
                last.then_inc(s["ab_tp"], 1)

                def transposes(n):
                    pe.wait_ge(s[f"xn_done_{'ab'[n]}"], c + 1)
                    for j in range(TPC):
                        if j >= 2:
                            pe.wait_ge(s["xnT_done"], TPC * (2 * c + n) + j - 1)
                        for k in range(2):
                            last = nc.tensor.transpose(X[j % 2][0:HD, k * 128:(k + 1) * 128], xn[:, j, k * HD:(k + 1) * HD], ident[:, :])
                        last.then_inc(s["xn_tp"], 1)
                pe.wait_ge(s["wT_done"], 2 * c)
                transposes(0)
                for g in range(2):
                    pe.wait_ge(s["xnT_done"], TPC * 2 * c + 3 * g + 3)
                    for k in range(2):
                        last = mm(U[g][0:R, 0:HT], ATc[:, k, :], xnT[:, k, g * HT:(g + 1) * HT], start=(k == 0), stop=(k == 1))
                    last.then_inc(s["s_mm"], 1)
                pe.wait_ge(s["ab_done"], c + 1)
                pe.wait_ge(s["W_ready"], c + 1)
                pe.wait_ge(s["y_done"], 3 * UN * c)
                for j in range(TPC):
                    pe.wait_ge(s["P_done"], 2 * c + j // 3 + 1)
                    if j >= 2:
                        pe.wait_ge(s["h1_done"], TPC * c + j - 1)
                    t = slice(j * 128, (j + 1) * 128)
                    for k in range(2):
                        mm(O[j % 2][:, 0:D], xnT[:, k, t], W[:, k, :], start=(k == 0), stop=False)
                    mm(O[j % 2][:, 0:D], P[:, t], Bc[:, :], start=False, stop=True).then_inc(s["o_mm"], 1)
                for k in range(2):
                    last = mm(V[0][0:HD, k * D:(k + 1) * D], Ac[:, k * HD:(k + 1) * HD], Bc[:, :], start=True, stop=True)
                last.then_inc(s["w_mm"], 1)
                transposes(1)
                pe.wait_ge(s["xnT_done"], TPC * (2 * c + 2))
                for j in range(TPC):
                    for k in range(2):
                        last = mm(X[0][:, j * E:(j + 1) * E], xnT[:, k, j * 128:(j + 1) * 128], gw[:, k, :], start=(k == 0), stop=(k == 1))
                last.then_inc(s["lg_mm"], 1)

                def up(k):
                    e, half = divmod(k, 2)
                    if k >= 2:
                        pe.wait_ge(s["ac_done"], UN * c + k - 1)
                    elif k == 0:
                        pe.wait_ge(s["P_done"], 2 * c + 2)
                        pe.wait_ge(s["W_ready"], c + 2)
                    for bank, w, sw in ((U, wu, swu), (V, wg, swg)):
                        for q in range(2):
                            lhs = w[:, q, e * HID:(e + 1) * HID] if e < E else sw[:, q, :]
                            last = mm(bank[k % 2][:, 0:HT], lhs, xnT[:, q, half * HT:(half + 1) * HT], start=(q == 0), stop=(q == 1))
                    last.then_inc(s["up_mm"], 1)

                def down(k):
                    e, half = divmod(k, 2)
                    pe.wait_ge(s["ac_done"], UN * c + k + 1)
                    for j in range(3):
                        n = 3 * k + j
                        if n >= 2:
                            pe.wait_ge(s["y_done"], 3 * UN * c + n - 1)
                        else:
                            pe.wait_ge(s["h1_done"], TPC * (c + 1))
                        t = slice(j * 128, (j + 1) * 128)
                        last = mm(O[n % 2][:, 0:D], ac[:, k % 2, t], wd[:, e, :] if e < E else swd[:, :], start=True, stop=(e < E))
                        if e == E:
                            pe.wait_ge(s["wT_done"], 2 * c + 2)
                            last = mm(O[n % 2][:, 0:D], wT[:, (3 * half + j) * 128:(3 * half + j + 1) * 128], bd[:, :], start=False, stop=True)
                        last.then_inc(s["y_mm"], 1)
                up(0)
                for k in range(1, UN):
                    up(k)
                    down(k - 1)
                    if k == 4:
                        pe.wait_ge(s["wf_done"], c + 1)
                        for n in range(2):
                            for j in range(3):
                                last = nc.tensor.transpose(X[n][0:E, j * 128:(j + 1) * 128], wf[:, 3 * n + j, :], ident[:, :])
                            last.then_inc(s["wT_tp"], 1)
                down(UN - 1)


_INS = ['x', 'L0_tok_gamma', 'L0_tok_beta', 'L0_tok_w', 'L0_tok_b', 'L0_attn_w_key', 'L0_attn_w_value', 'L0_attn_w_query',
        'L0_attn_w_gate', 'L0_attn_w_out', 'L0_ffn_gate_w', 'L0_ffn_gate_b', 'L0_ffn_bias', 'L0_ffn_Wu', 'L0_ffn_bu', 'L0_ffn_Wg',
        'L0_ffn_bg', 'L0_ffn_Wd', 'L0_ffn_bd', 'L0_ffn_sWu', 'L0_ffn_sbu', 'L0_ffn_sWg', 'L0_ffn_sbg', 'L0_ffn_sWd', 'L0_ffn_sbd']


_TURNED = ('L0_attn_w_gate', 'L0_attn_w_out', 'L0_ffn_bu', 'L0_ffn_bg')


def shape_constants():
    import numpy as np
    f = np.float32
    t = np.arange(STEPS)
    step = np.arange(R) // NH
    half = (np.arange(128) >= 64).astype(int)
    return {
        "c_ident": np.eye(128, dtype=f),
        "c_rowbase": (np.arange(B) * N).astype(f)[:, None],
        "c_mhalf": np.full((128, 128), -0.5, f),
        "c_wdec": np.tile((WRITE * DECAY ** (-(t % CS + 1.0))).astype(f), (HD, 1)),
        "c_causal": (step[:, None] < np.arange(CS)[None, :]).astype(f),
        "c_tdecay": (DECAY ** (2.0 * np.arange(TPC)[None, :] + half[:, None])).astype(f),
        "c_iota": np.tile(np.arange(E, dtype=f), (128, 1)),
    }


def kernel(**inputs):
    import numpy as np
    import concourse.bacc as bacc
    from concourse.bass_utils import run_bass_kernel_spmd

    nc = bacc.Bacc("TRN2", target_bir_lowering=False, num_devices=1)
    arrays, aps = {}, {}
    given = {n: np.ascontiguousarray(np.asarray(inputs[n]).T if n in _TURNED else inputs[n]) for n in _INS}
    given.update(shape_constants())
    for name, v in given.items():
        arrays[f"in_{name}"] = v
        aps[name] = nc.dram_tensor(f"in_{name}", v.shape, mybir.dt.from_np(v.dtype), kind="ExternalInput").ap()
    out = nc.dram_tensor("out_0", (B, KEEP, D), mybir.dt.float32, kind="ExternalOutput").ap()
    tower(nc, aps, out)
    return run_bass_kernel_spmd(nc, [arrays], core_ids=[0]).results[0]["out_0"]
```

```python
from contextlib import ExitStack

import concourse.bass as bass
from concourse import mybir

B, N, D = 64, 256, 192
KEEP = int(N * 0.7)
STEPS = KEEP + KEEP % 2
TILES = STEPS // 2
TPC = 5
CHUNKS = TILES // TPC
CS = 2 * TPC
NH, DK = 8, 64
E, G, HID = 16, 8, 128
TOP = 4
SCALE = 2.5
EPS = 1e-5
DECAY, WRITE = 0.95, 0.1
HD = D // 2
R = CS * NH
CT = TPC * 128
HT = CT // 2
ROUNDS = (STEPS + 7) // 8
XC = 8
XCHUNKS = 128 // XC
XBUF = 3
S0 = STEPS // 2
TOK = TILES * 128
BLK = 256
BT2 = BLK // 128
ROOM = TOK + BLK
BLOCKS = (TOK * TOP - E) // BLK + E
BLOCKS += -BLOCKS % 4
ROWLEN = D + 2 * E
SKIP = 1.0e7
AHEAD = 4
WAW = 2 * 2 * HID


def tower(nc, a, out):
    f32, u32, i32, bf16 = mybir.dt.float32, mybir.dt.uint32, mybir.dt.int32, mybir.dt.bfloat16
    ALU, ACT, AX = mybir.AluOpType, mybir.ActivationFunctionType, mybir.AxisListType
    es = ExitStack()
    with es:
        sb = lambda name, shape, dt=f32: es.enter_context(nc.sbuf_tensor(name, shape, dt))
        pb = lambda name, p, n: es.enter_context(nc.psum_tensor(name, [p, n], f32))
        sem = lambda name: es.enter_context(nc.semaphore(name))

        h = sb("h", [128, TILES * D])
        ident = sb("ident", [128, 128])
        wall = sb("wall", [128, E * WAW])
        wa = wall[0:HD, :]
        wd = sb("wd", [HID, E * D])
        swu = sb("swu", [HD, 2, HID])
        swg = sb("swg", [HD, 2, HID])
        swd = sb("swd", [HID, D])
        bu = sb("bu", [HID, E + 1])
        bg = sb("bg", [HID, E + 1])
        bd = sb("bd", [E + 1, D])
        tok4 = sb("tok4", [128, TILES])
        rank = sb("rank", [128, TOP])
        earlier = sb("earlier", [128, 128], bf16)
        earlier_in = sb("earlier_in", [128, 128])
        ones = sb("ones", [128, 128], bf16)
        carry = sb("carry", [128, E])
        base = sb("base", [128, E])
        blki = sb("blki", [1, BLOCKS])
        pad = sb("pad", [128, BT2, ROWLEN])
        epsc = sb("epsc", [128, 1])
        gw = sb("gw", [HD, 2, E])
        gb = sb("gb", [128, E])
        rb = sb("rb", [128, E])
        iota = sb("iota", [128, E])
        causal = sb("causal", [R, CS])
        tdecay = sb("tdecay", [128, TPC])
        kv = sb("kv", [128, 4 * STEPS * NH])
        AT = kv[0:HD, 0:2 * STEPS * NH].rearrange("p (c n) -> p c n", c=2)
        BT = kv[0:HD, 2 * STEPS * NH:4 * STEPS * NH].rearrange("p (c n) -> p c n", c=2)
        W = sb("W", [HD, 2, D])
        taken = [0]

        def in_kv(p, n):
            lo = taken[0]
            taken[0] += n
            assert taken[0] <= 4 * STEPS * NH
            return kv[0:p, lo:lo + n]

        mhalf = sb("mhalf", [128, 128])

        xin = h[:, 0:XBUF * XC * D].rearrange("p (i n) -> p i n", i=XBUF)
        xst = h[:, TILES * D - 128 * 6:TILES * D].rearrange("p (n k) -> p n k", k=6)
        xmean = in_kv(128, 128)
        xscr = in_kv(128, D)
        xdot = in_kv(128, 128)
        xtmp = in_kv(128, 128)
        xvar = in_kv(128, 128)
        xrs = in_kv(128, 128)
        gam = in_kv(128, D)
        bet = in_kv(128, D)
        tw = in_kv(128, D)
        gamw = in_kv(128, D)
        tb = sb("tb", [128, 1])
        tcon = sb("tcon", [128, 1])
        tcon2 = sb("tcon2", [128, 1])
        sc = in_kv(B, 2 * N).rearrange("p (k n) -> p k n", k=2)
        m8 = sb("m8", [B, 8])
        idx = sb("idx", [B, ROUNDS * 8], u32)
        rowbase = sb("rowbase", [B, 1])
        rowi = sb("rowi", [B, ROUNDS * 8], u32)
        odd = sb("odd", [B, TILES], u32)
        gidx = sb("gidx", [128, TILES + 2 * TPC], u32)
        kidx = sb("kidx", [S0, 2], u32)
        kone = sb("kone", [S0, 2, 1], u32)

        spare = [XBUF * XC * D]

        def in_h(p, x, y):
            lo = spare[0]
            spare[0] += x * y
            assert spare[0] <= TILES * D - 128 * 6
            return h[0:p, lo:lo + x * y].rearrange("p (x y) -> p x y", x=x)

        wk, wq, wv, woT = (in_h(128, 4, D) for _ in range(4))
        wgt = sb("wgt", [HD, 2, NH])
        wgtb = in_h(HD, 2, NH * HD).rearrange("p c (k d) -> p c k d", k=NH)
        Gm, Hm = (in_h(HD, 2, NH * D).rearrange("p c (k d) -> p c k d", k=NH) for _ in range(2))
        x0 = in_h(S0, 2, D)
        x0st = sb("x0st", [S0, 2, 6])
        x0mv = sb("x0mv", [S0, 2, 2])
        x0r = sb("x0r", [S0, 2])
        x0n = in_h(S0, 2, D)
        x0T = sb("x0T", [HD, 2, STEPS])
        wdec = sb("wdec", [HD, STEPS])
        gate = sb("gate", [HD, STEPS])

        gcur = [sb(f"gcur{u}", [128, TPC], u32) for u in range(2)]
        hin = [sb(f"hin{u}", [128, TPC, D]) for u in range(2)]
        rows = [sb(f"rows{u}", [128, TPC, ROWLEN]) for u in range(2)]
        slots = [sb(f"slots{u}", [128, TPC, TOP], u32) for u in range(2)]
        st = sb("st", [128, TPC, 6])
        mv = sb("mv", [128, TPC, 2])
        sd = sb("sd", [128, TPC])
        rs = sb("rs", [128, TPC])
        xn = {n: sb("xn_" + n, [128, TPC, D]) for n in "ab"}
        xnT = {n: sb("xnT_" + n, [HD, 2, CT]) for n in "ab"}
        P = sb("P", [R, CT])
        ATc = sb("ATc", [HD, 2, R])
        BTc = sb("BTc", [HD, 2, R])
        Ac = sb("Ac", [R, D])
        Bc = sb("Bc", [R, D])
        lg = sb("lg", [128, TPC, E])
        mx = sb("mx", [128, TPC])
        ex = sb("ex", [128, TPC, E])
        rsum = sb("rsum", [128, TPC])
        rinv = sb("rinv", [128, TPC])
        prob = sb("prob", [128, TPC, E])
        sel = sb("sel", [128, TPC, E])
        gs = sb("gs", [128, TPC, G])
        g8 = sb("g8", [128, TPC, 8])
        gi = sb("gi", [128, TPC, 8], u32)
        hit = sb("hit", [128, TPC, E * TOP])
        prod = sb("prod", [128, TPC, E * TOP])
        gm = sb("gm", [128, TPC, G])
        picked = sb("picked", [128, (TPC + 1) * E], bf16)
        slotrow = sb("slotrow", [128, TPC, E])
        wT = sb("wT", [E + 1, CT])
        su = sb("su", [HID, 2, HT])
        ac = sb("ac", [HID, 2, HT])

        cnt = sb("cnt", [1, E])
        cnti = sb("cnti", [1, E], i32)
        nblk = sb("nblk", [1, E])
        cum = sb("cum", [1, E])
        one1 = sb("one1", [1, E])
        skipd = sb("skipd", [1, E])
        carryi = sb("carryi", [1, E], i32)
        tabe = sb("tabe", [1, BLOCKS])
        tabr = sb("tabr", [1, BLOCKS])
        tabei = sb("tabei", [1, BLOCKS], i32)
        tabri = sb("tabri", [1, BLOCKS], i32)
        big = kv[0:1, 0:BLOCKS * E]

        taken[0] = 0
        xb = [in_kv(128, BT2 * ROWLEN).rearrange("p (t n) -> p t n", t=BT2) for u in range(4)]
        wac = [in_kv(HD, WAW) for u in range(2)]
        wdc = [in_kv(HID, D) for u in range(2)]
        xT = [in_kv(HD, 2 * BLK).rearrange("p (k n) -> p k n", k=2) for u in range(2)]
        sub = [in_kv(HID, BLK) for u in range(2)]
        acb = [in_kv(HID, BLK) for u in range(2)]
        yb = [rows[u % 2][:, :, :].rearrange("p j n -> p (j n)")[:, (u // 2) * BT2 * D:(u // 2 + 1) * BT2 * D]
              .rearrange("p (t n) -> p t n", t=BT2) for u in range(4)]
        wcur = [sb(f"wcur{u}", [128, BT2]) for u in range(4)]
        dcur = [sb(f"dcur{u}", [128, BT2], u32) for u in range(4)]
        bcur = [sb(f"bcur{u}", [128, 2]) for u in range(4)]

        YW = TPC * TOP * D
        yin = [wall[:, u * YW:(u + 1) * YW].rearrange("p (j n) -> p j n", j=TPC) for u in range(2)]
        fin = hin

        X = [pb("X0", 128, 512), pb("X1", 128, 512)]
        O = [pb("O0", 128, 512), pb("O1", 128, 512)]
        U = [pb("U0", 128, 512), pb("U1", 128, 512)]
        V = [pb("V0", 128, 512), pb("V1", 128, 512)]

        score_d = nc.dram_tensor("score_d", [128, 128], f32, kind="Internal").ap()
        lists = nc.dram_tensor("lists", [E * ROOM + BLK, ROWLEN], f32, kind="Internal").ap()
        yk = nc.dram_tensor("yk", [TOK * TOP, D], f32, kind="Internal").ap()
        row0_d = nc.dram_tensor("row0_d", [1, STEPS], u32, kind="Internal").ap()

        names = """weights x_loaded0 x_loaded1 x_loaded2 x_used stats_done mean_half mean_ready dot_done gamw_ready
        tcon_ready fold_ready var_ready rstd_ready score_ready score_out score_in top8 top8i top8r rowi_ready
        odd_ready odd_moved row0_out kidx_in kone_ready x0_in x0_stats x0_mv x0_rstd0 x0_rstd x0_norm x0_tp x0_copied
        wgtb_ready gh_mm gh_copied at_mm at_copied gate_mm gate_ready bt_scaled fills pad_ready pads table
        gath0 gath1 scat0 scat1 xl0 xl1 xl2 xl3 ysc0 ysc1 ysc2 ysc3 yl0 yl1 st0 st1 fin_done0 fin_done1 half_done0 half_done1 pair_done0 pair_done1 tables_set tail_mult""".split()
        per_chunk = dict(gcur_done=1, st_a=1, st_b=1, mv_a=1, mv_b=1, sd_a=1, sd_b=1, rs_a=1, rs_b=1, xn_a=1, xn_b=1,
                         tp_a=TPC, tp_b=TPC, xT_a=TPC, xT_b=TPC, hx_done=1, abT_done=1, ab_tp=1, ab_done=1, s_mm=2, P_done=2,
                         o_mm=TPC, h1_done=TPC, w_mm=1, W_done=1, lg_mm=1, lg_done=1, mx_done=1, sub_done=1, ex_done=1,
                         sum_done=1, inv_done=1, prob_done=1, sel_done=1, gs_done=1, g8_done=1, gi_done=1, ghit_done=1,
                         gm_done=1, pen_done=1, msk_done=1, e8_done=1, ei_done=1, ehit_done=1, picked_done=1, wf_done=1,
                         pos_mm=1, row_done=1, carry_done=1, prod_done=1, slots_done=1, rk_prod=1, rk_sum=1, dest_done=1,
                         rowx_done=1, wT_tp=1, wT_done=1, up_mm=2, su_done=2, ac_done=2, y_mm=TPC, h_done=TPC)
        per_block = dict(b_tp=1, b_xT=1, b_wa=1, b_wd=1, b_cur=1, b_up=1, b_su=1, b_ac=1, b_down=1, b_y=1)
        names += list(per_chunk) + list(per_block)
        s = {n: sem(n) for n in names}

        def reach(name, m, k=None):
            per = {**per_chunk, **per_block}[name]
            return per * (m + AHEAD) + (per if k is None else k)

        def wait(eng, name, m, k=None):
            eng.wait_ge(s[name], reach(name, m, k))

        def wait_reg(eng, name, m, k=None):
            wait_alone(eng, s[name], reach(name, m, k))

        def wait_alone(eng, what, count):
            register = eng.to_reg(count)
            eng.wait_ge(s["weights"], NLOAD)
            eng.wait_ge(what, register)

        def pipeline(eng, first, second, third):
            def ahead(i, r, d):
                return i + (r + d) // 4, (r + d) % 4

            def step(i, r, last=4):
                if r + 2 < last:
                    first(*ahead(i, r, 2))
                if r + 1 < last:
                    second(*ahead(i, r, 1))
                if third:
                    third(i, r)
            first(0, 0)
            first(0, 1)
            second(0, 0)
            with eng.Fori(0, BLOCKS // 4 - 1) as i:
                for r in range(4):
                    step(i, r, last=8)
            for r in range(4):
                step(BLOCKS // 4 - 1, r)

        def _bc(ap, pos, n):
            shape = list(ap.shape)
            u = ap.unsqueeze(pos)
            shape.insert(pos, n)
            return u.to_broadcast(shape)

        loads = []
        SCAT = 16 * TPC * TOP
        CREDIT = SCAT // 2
        YSC = 16 * BT2

        block = es.enter_context(nc.Block())

        @block.sync
        def _(sp):
            def load(dst, src):
                sp.dma_start(dst, src).then_inc(s["weights"], 16)
                loads.append(1)

            def xload(i):
                sp.dma_start(xin[:, i % XBUF, :], a["x"].rearrange("b (u n) d -> (b u) (n d)", u=2)
                             [:, i * XC * D:(i + 1) * XC * D]).then_inc(s[f"x_loaded{i % XBUF}"], 16)

            row = lambda v, p: v.rearrange("(a n) -> a n", a=1).to_broadcast([p, v.shape[0]])
            load(gam[:, :], row(a["L0_tok_gamma"], 128))
            load(tw[:, :], row(a["L0_tok_w"], 128))
            xload(0)
            xload(1)
            xload(2)
            load(bet[:, :], row(a["L0_tok_beta"], 128))
            load(tb[:, :], row(a["L0_tok_b"], 128))
            load(ident[:, :], a["c_ident"])
            load(rowbase[:, :], a["c_rowbase"])
            load(mhalf[:, :], a["c_mhalf"])
            load(wk[:, :, :], a["L0_attn_w_key"].rearrange("(c p) d -> p c d", p=128))
            load(wq[:, :, :], a["L0_attn_w_query"].rearrange("(c p) d -> p c d", p=128))
            load(wv[:, :, :], a["L0_attn_w_value"].rearrange("(c p) d -> p c d", p=128))
            load(woT[:, :, :], a["L0_attn_w_out"].rearrange("(c p) d -> p c d", p=128))
            load(wgt[:, :, :], a["L0_attn_w_gate"].rearrange("(c p) k -> p c k", p=HD))
            load(wdec[:, :], a["c_wdec"])
            load(causal[:, :], a["c_causal"])
            load(tdecay[:, :], a["c_tdecay"])
            load(iota[:, :], a["c_iota"])
            load(gw[:, :, :], a["L0_ffn_gate_w"].rearrange("(c p) e -> p c e", p=HD))
            load(gb[:, :], row(a["L0_ffn_gate_b"], 128))
            load(rb[:, :], row(a["L0_ffn_bias"], 128))
            load(bd[0:E, :], a["L0_ffn_bd"])
            load(bd[E:E + 1, :], row(a["L0_ffn_sbd"], 1))
            load(tok4[:, :], a["c_tok4"])
            load(rank[:, :], a["c_rank"])
            load(base[:, :], a["c_base"])
            load(blki[:, :], a["c_blki"])
            load(earlier_in[:, :], a["c_earlier"])
            load(bu[:, 0:E], a["L0_ffn_bu"])
            load(bg[:, 0:E], a["L0_ffn_bg"])
            load(bu[:, E:E + 1], a["L0_ffn_sbu"].rearrange("(h o) -> h o", o=1))
            load(bg[:, E:E + 1], a["L0_ffn_sbg"].rearrange("(h o) -> h o", o=1))
            wav = wa.rearrange("p (e m c n) -> p m c e n", e=E, m=2, c=2)
            for m, name in enumerate(("L0_ffn_Wu", "L0_ffn_Wg")):
                for c in range(2):
                    load(wav[:, m, c, :, :], a[name][:, c * HD:(c + 1) * HD, :].rearrange("e p n -> p e n"))
            load(wd[:, :].rearrange("p (e d) -> p e d", e=E), a["L0_ffn_Wd"].rearrange("e h d -> h e d"))
            load(swu[:, :, :], a["L0_ffn_sWu"].rearrange("(c p) n -> p c n", p=HD))
            load(swg[:, :, :], a["L0_ffn_sWg"].rearrange("(c p) n -> p c n", p=HD))
            load(swd[:, :], a["L0_ffn_sWd"])
            for i in range(XBUF, XCHUNKS):
                sp.wait_ge(s["x_used"], i - XBUF + 1)
                xload(i)
            sp.wait_ge(s["score_ready"], 1)
            sp.dma_start(score_d, xdot[:, :]).then_inc(s["score_out"], 16)
            sp.wait_ge(s["score_out"], 16)
            sp.dma_start(sc[:, 0, :], score_d.rearrange("(b u) n -> b (u n)", u=2)).then_inc(s["score_in"], 16)
            sp.wait_ge(s["odd_ready"], 1)
            sp.dma_start(row0_d, rowi[0:1, 0:STEPS]).then_inc(s["row0_out"], 16)
            sp.dma_start(gidx[64:128, 0:TILES], odd[:, :]).then_inc(s["odd_moved"], 16)
            sp.wait_ge(s["row0_out"], 16)
            sp.dma_start(kidx[:, :], row0_d.rearrange("a (p i) -> (a p) i", i=2)).then_inc(s["kidx_in"], 16)

            sp.wait_ge(s["table"], 1)
            for u in range(2):
                sp.wait_ge(s[f"scat{u}"], SCAT * (CHUNKS // 2) + CREDIT)
            for e in range(4, E):
                end = sp.value_load(carryi[0:1, e:e + 1], min_val=0, max_val=E * ROOM)
                sp.dma_start(lists[bass.ds(end, BLK), :].rearrange("(t p) d -> p t d", p=128), pad[:, :, :]).then_inc(s["pads"], 16)
            sp.wait_ge(s["pads"], 16 * (E - 4))
            for r in range(4):
                sp.wait_ge(s[f"ysc{r}"], YSC)
            sp.wait_ge(s["tables_set"], 1)
            with sp.Fori(0, BLOCKS // 4) as i:
                for r in range(4):
                    b = 4 * i + r
                    first = sp.value_load(tabri[0:1, bass.ds(b, 1)], min_val=0, max_val=E * ROOM)
                    wait(sp, "b_tp", b - 4)
                    wait(sp, "b_cur", b - 4)
                    sp.dma_start(xb[r][:, :, :], lists[bass.ds(first, BLK), :].rearrange("(t p) d -> p t d", p=128))\
                        .then_inc(s[f"xl{r}"], 16)
            for r in range(4):
                sp.wait_ge(s[f"ysc{r}"], YSC * (BLOCKS // 4 + 1))
            sp.wait_ge(s["b_wa"], BLOCKS + AHEAD)
            yrows = yk.rearrange("(t k) d -> t (k d)", k=TOP)

            def load_y(c, u):
                sp.dma_start(yin[u], yrows[bass.ds(c * (TPC * 128), TPC * 128), :].rearrange("(j p) n -> p j n", p=128))\
                    .then_inc(s[f"yl{u}"], 16)

            outp = out.rearrange("b t d -> b (t d)")

            def store(c, u, last=False):
                for half in range(2):
                    src = fin[u][64 * half:64 * half + 64, :, :]
                    if last and half:
                        sp.dma_start(out[:, c * CS + 1:c * CS + 2 * TPC - 2:2, :], src[:, 0:TPC - 1, :]).then_inc(s[f"st{u}"], 16)
                    else:
                        dst = outp[:, bass.ds(c * (CS * D), CS * D)].rearrange("b (j w d) -> b j w d", w=2, d=D)[:, :, half, :] \
                            if not last else out[:, c * CS:c * CS + CS - 1:2, :]
                        sp.dma_start(dst, src).then_inc(s[f"st{u}"], 16)

            load_y(0, 0)
            load_y(1, 1)
            with sp.Fori(1, CHUNKS // 2) as it:
                for u in range(2):
                    sp.wait_ge(s[f"fin_done{u}"], it)
                    load_y(2 * it + u, u)
                    store(2 * it - 2 + u, u)
            for u in range(2):
                sp.wait_ge(s[f"fin_done{u}"], CHUNKS // 2)
                store(CHUNKS - 2 + u, u, last=(u == 1))
            for u in range(2):
                sp.wait_ge(s[f"st{u}"], 32 * (CHUNKS // 2))

        NLOAD = 16 * len(loads)

        @block.gpsimd
        def _(pool):
            for name, per in {**per_chunk, **per_block}.items():
                pool.sem_inc(s[name], AHEAD * per)
            pool.wait_ge(s["weights"], NLOAD)
            pool.wait_ge(s["var_ready"], 1)
            nc.gpsimd.tensor_tensor(xrs[:, :], xvar[:, :], mhalf[:, :], ALU.pow).then_inc(s["rstd_ready"], 1)
            xrows = a["x"].rearrange("b n d -> (b n) d")
            pool.wait_ge(s["kone_ready"], 1)
            for i in range(2):
                pool.indirect_dma_start(out=x0[:, i, :], out_offset=None, in_=xrows,
                                        in_offset=bass.IndirectOffsetOnAxis(ap=kone[:, i, :], axis=0)).then_inc(s["x0_in"], 16)
            pool.wait_ge(s["x0_mv"], 1)
            nc.gpsimd.tensor_scalar(x0r[:, :], x0mv[:, :, 1], EPS, None, ALU.add).then_inc(s["x0_rstd0"], 1)
            pool.wait_ge(s["x0_rstd0"], 1)
            nc.gpsimd.tensor_tensor(x0r[:, :], x0r[:, :], mhalf[0:S0, 0:2], ALU.pow).then_inc(s["x0_rstd"], 1)

            def gather(u):
                for j in range(TPC):
                    pool.indirect_dma_start(out=hin[u][:, j, :], out_offset=None, in_=xrows,
                                            in_offset=bass.IndirectOffsetOnAxis(ap=gcur[u][:, j:j + 1], axis=0)).then_inc(s[f"gath{u}"], 16)
            pool.wait_ge(s["pad_ready"], 2)
            for u in range(2):
                pool.dma_start(lists[E * ROOM + 128 * u:E * ROOM + 128 * u + 128, :], pad[:, u, :]).then_inc(s[f"scat{u}"], CREDIT)
            for u in range(2):
                pool.wait_ge(s["gcur_done"], AHEAD + 1 + u)
                gather(u)
            with pool.Fori(0, CHUNKS // 2) as i:
                for u in range(2):
                    c = 2 * i + u
                    wait_reg(pool, "h1_done", c)
                    wait_reg(pool, "gcur_done", c + 2)
                    gather(u)
                    wait_reg(pool, "rowx_done", c)
                    wait_reg(pool, "slots_done", c)
                    for k in range(TOP):
                        for j in range(TPC):
                            pool.indirect_dma_start(out=lists, out_offset=bass.IndirectOffsetOnAxis(ap=slots[u][:, j, k:k + 1], axis=0),
                                                    in_=rows[u][:, j, :], in_offset=None).then_inc(s[f"scat{u}"], 16)
            pool.wait_ge(s["table"], 1)
            for u in range(2):
                pool.wait_ge(s[f"scat{u}"], SCAT * (CHUNKS // 2) + CREDIT)
            for e in range(4):
                end = pool.value_load(carryi[0:1, e:e + 1], min_val=0, max_val=E * ROOM)
                pool.dma_start(lists[bass.ds(end, BLK), :].rearrange("(t p) d -> p t d", p=128), pad[:, :, :]).then_inc(s[f"ysc{e}"], YSC)
            with pool.Fori(0, BLOCKS // 4) as i:
                for r in range(4):
                    wait_reg(pool, "b_y", 4 * i + r)
                    for t in range(BT2):
                        pool.indirect_dma_start(out=yk, out_offset=bass.IndirectOffsetOnAxis(ap=dcur[r][:, t:t + 1], axis=0),
                                                in_=yb[r][:, t, :], in_offset=None, bounds_check=TOK * TOP - 1,
                                                oob_is_err=False).then_inc(s[f"ysc{r}"], 16)
            for u in range(2):
                pool.wait_ge(s[f"gath{u}"], 16 * TPC * (CHUNKS // 2 + 1))
            with pool.Fori(1, CHUNKS // 2 + 1) as it:
                for u in range(2):
                    wait_alone(pool, s[f"yl{u}"], 16 * it)
                    y4 = yin[u].rearrange("p j (k d) -> p j k d", k=TOP)
                    nc.gpsimd.tensor_tensor(y4[:, :, 2, :], y4[:, :, 2, :], y4[:, :, 3, :], ALU.add).then_inc(s[f"half_done{u}"], 1)

        @block.vector
        def _(dve):
            v = nc.vector
            dve.wait_ge(s["weights"], NLOAD)
            v.tensor_tensor(gamw[:, :], gam[:, :], tw[:, :], ALU.mult).then_inc(s["gamw_ready"], 1)
            v.scalar_tensor_tensor(out=xscr[:, :], in0=bet[:, :], scalar=1.0, in1=tw[:, :], op0=ALU.mult, op1=ALU.mult,
                                   accum_out=tcon[:, :]).then_inc(s["tcon_ready"], 1)
            v.memset(pad[:, :, 0:D + E], 0.0).then_inc(s["pad_ready"], 1)
            v.memset(pad[:, :, D + E:ROWLEN], SKIP).then_inc(s["pad_ready"], 1)
            v.memset(W[:, :, :], 0.0).then_inc(s["fills"], 1)
            v.memset(picked[:, :], 0.0).then_inc(s["fills"], 1)
            v.memset(wT[:, :], 1.0).then_inc(s["fills"], 1)
            v.memset(ones[:, :], 1.0).then_inc(s["fills"], 1)
            v.memset(one1[:, :], 1.0).then_inc(s["fills"], 1)
            v.memset(epsc[:, :], EPS).then_inc(s["fills"], 1)
            v.memset(gidx[:, TILES:], 0).then_inc(s["fills"], 1)
            v.tensor_copy(carry[:, :], base[:, :]).then_inc(s["fills"], 1)
            v.tensor_copy(earlier[:, :], earlier_in[:, :]).then_inc(s["fills"], 1)
            dve.wait_ge(s["tcon_ready"], 1)
            v.tensor_tensor(tcon2[:, :], tcon[:, :], tb[:, :], ALU.add).then_inc(s["tcon_ready"], 1)
            dve.wait_ge(s["gamw_ready"], 1)
            for i in range(XCHUNKS):
                dve.wait_ge(s[f"x_loaded{i % XBUF}"], 16 * (i // XBUF + 1))
                for k in range(XC):
                    xt = xin[:, i % XBUF, k * D:(k + 1) * D]
                    last = v.bn_stats(xst[:, i * XC + k, :], xt)
                last.then_inc(s["stats_done"], 1)
                r = slice(i * XC, (i + 1) * XC)
                dve.wait_ge(s["stats_done"], i + 1)
                v.tensor_tensor(xtmp[:, r], xst[:, r, 1], xst[:, r, 4], ALU.add).then_inc(s["mean_half"], 1)
                dve.wait_ge(s["mean_half"], i + 1)
                v.tensor_scalar(xmean[:, r], xtmp[:, r], 0.5, None, ALU.mult).then_inc(s["mean_ready"], 1)
                dve.wait_ge(s["mean_ready"], i + 1)
                for k in range(XC):
                    xt = xin[:, i % XBUF, k * D:(k + 1) * D]
                    n = i * XC + k
                    last = v.scalar_tensor_tensor(out=xt, in0=xt, scalar=xmean[:, n:n + 1], in1=gamw[:, :],
                                                  op0=ALU.subtract, op1=ALU.mult, accum_out=xdot[:, n:n + 1])
                last.then_inc(s["x_used"], 1)
            v.tensor_tensor(xtmp[:, :], xst[:, :, 1], xst[:, :, 4], ALU.subtract).then_inc(s["fold_ready"], 1)
            v.tensor_tensor(xvar[:, :], xst[:, :, 2], xst[:, :, 5], ALU.add).then_inc(s["fold_ready"], 1)
            dve.wait_ge(s["fold_ready"], 2)
            v.tensor_tensor(xtmp[:, :], xtmp[:, :], xtmp[:, :], ALU.mult).then_inc(s["fold_ready"], 1)
            v.tensor_scalar(xvar[:, :], xvar[:, :], 1.0 / D, EPS, ALU.mult, ALU.add).then_inc(s["fold_ready"], 1)
            dve.wait_ge(s["fold_ready"], 4)
            v.scalar_tensor_tensor(out=xvar[:, :], in0=xtmp[:, :], scalar=0.25, in1=xvar[:, :], op0=ALU.mult, op1=ALU.add)\
                .then_inc(s["var_ready"], 1)
            dve.wait_ge(s["rstd_ready"], 1)
            dve.wait_ge(s["var_ready"], 1)
            v.tensor_tensor(xtmp[:, :], xrs[:, :], xrs[:, :], ALU.mult).then_inc(s["fold_ready"], 1)
            dve.wait_ge(s["fold_ready"], 5)
            v.tensor_tensor(xtmp[:, :], xtmp[:, :], xvar[:, :], ALU.mult).then_inc(s["fold_ready"], 1)
            dve.wait_ge(s["fold_ready"], 6)
            v.tensor_scalar(xtmp[:, :], xtmp[:, :], -0.5, 1.5, ALU.mult, ALU.add).then_inc(s["fold_ready"], 1)
            dve.wait_ge(s["x_used"], XCHUNKS)
            v.tensor_tensor(xdot[:, :], xdot[:, :], xrs[:, :], ALU.mult).then_inc(s["fold_ready"], 1)
            dve.wait_ge(s["fold_ready"], 8)
            v.tensor_tensor(xdot[:, :], xdot[:, :], xtmp[:, :], ALU.mult).then_inc(s["fold_ready"], 1)
            dve.wait_ge(s["fold_ready"], 9)
            dve.wait_ge(s["tcon_ready"], 2)
            v.tensor_scalar(xdot[:, :], xdot[:, :], tcon2[:, :], None, ALU.add).then_inc(s["score_ready"], 1)
            dve.wait_ge(s["score_in"], 16)
            for r in range(ROUNDS):
                cur, nxt = sc[:, r % 2, :], sc[:, (r + 1) % 2, :]
                if r:
                    dve.wait_ge(s["top8r"], r)
                v.max(m8[:, :], cur).then_inc(s["top8"], 1)
                dve.wait_ge(s["top8"], r + 1)
                v.max_index(idx[:, 8 * r:8 * r + 8], m8[:, :], cur).then_inc(s["top8i"], 1)
                v.match_replace(nxt, m8[:, :], cur, -3.0e38).then_inc(s["top8r"], 1)
            dve.wait_ge(s["top8i"], ROUNDS)
            v.tensor_scalar(rowi[:, :], idx[:, :], rowbase[:, :], None, ALU.add).then_inc(s["rowi_ready"], 1)
            dve.wait_ge(s["rowi_ready"], 1)
            v.tensor_copy(gidx[0:64, 0:TILES], rowi[:, 0:STEPS:2])
            v.tensor_copy(odd[:, :], rowi[:, 1:STEPS:2]).then_inc(s["odd_ready"], 1)
            dve.wait_ge(s["kidx_in"], 16)
            v.tensor_copy(kone[:, :, 0], kidx[:, :]).then_inc(s["kone_ready"], 1)

            dve.wait_ge(s["x0_in"], 32)
            for i in range(2):
                last = v.bn_stats(x0st[:, i, :], x0[:, i, :])
            last.then_inc(s["x0_stats"], 1)
            dve.wait_ge(s["x0_stats"], 1)
            for i in range(2):
                last = v.bn_aggr(x0mv[:, i, :], x0st[:, i, :])
            last.then_inc(s["x0_mv"], 1)
            dve.wait_ge(s["x0_mv"], 1)
            dve.wait_ge(s["x0_rstd"], 1)
            for i in range(2):
                last = v.tensor_scalar(x0n[:, i, :], x0[:, i, :], x0mv[:, i, 0:1], x0r[:, i:i + 1], ALU.subtract, ALU.mult)
            last.then_inc(s["x0_norm"], 1)
            for hh in range(NH):
                dve.wait_ge(s["gate_ready"], hh + 1)
                v.tensor_tensor(gate[:, :], gate[:, :], wdec[:, :], ALU.mult).then_inc(s["bt_scaled"], 1)
                dve.wait_ge(s["bt_scaled"], 3 * hh + 1)
                dve.wait_ge(s["at_mm"], 4 * hh + 4)
                for c in range(2):
                    dst = BT[:, c, :].rearrange("p (s k) -> p s k", k=NH)[:, :, hh]
                    v.tensor_tensor(dst, (V[c])[0:HD, 0:STEPS], gate[:, :], ALU.mult).then_inc(s["bt_scaled"], 1)

            def norm(hc, n, c):
                for j in range(TPC):
                    last = v.bn_stats(st[:, j, :], hc[:, j, :])
                last.then_inc(s["st_" + n], 1)
                wait_reg(dve, "st_" + n, c)
                for j in range(TPC):
                    last = v.bn_aggr(mv[:, j, :], st[:, j, :])
                last.then_inc(s["mv_" + n], 1)
                wait(dve, "sd_" + n, c)
                v.reciprocal(rs[:, :], sd[:, :]).then_inc(s["rs_" + n], 1)
                wait(dve, "rs_" + n, c)
                wait(dve, "tp_" + n, c - 1)
                if n == "b":
                    wait(dve, "rowx_done", c - 1)
                for j in range(TPC):
                    last = v.tensor_scalar(xn[n][:, j, :], hc[:, j, :], mv[:, j, 0:1], rs[:, j:j + 1], ALU.subtract, ALU.mult)
                last.then_inc(s["xn_" + n], 1)

            def resident(c):
                return h[:, bass.ds(c * (TPC * D), TPC * D)].rearrange("p (j d) -> p j d", d=D)

            def enter(i, u):
                c = 2 * i + u
                wait_alone(dve, s[f"gath{u}"], 16 * TPC * (i + 1))
                norm(hin[u], "a", c)
                wait(dve, "xn_a", c)
                v.tensor_tensor(hin[u][:, :, :], hin[u][:, :, :], xn["a"][:, :, :], ALU.add).then_inc(s["hx_done"], 1)

            def mask(c):
                for k in range(2):
                    wait(dve, "s_mm", c, k + 1)
                    wait(dve, "w_mm", c - 1)
                    dst = P[:, k * HT:(k + 1) * HT].rearrange("p (t b) -> p t b", b=64)
                    v.tensor_tensor(dst, U[k][0:R, 0:HT].rearrange("p (t b) -> p t b", b=64),
                                    _bc(causal[:, k * TPC:(k + 1) * TPC], 2, 64), ALU.mult).then_inc(s["P_done"], 1)

            def attend(i, u):
                c = 2 * i + u
                wait(dve, "hx_done", c)
                hc = resident(c)
                for j in range(TPC):
                    wait(dve, "o_mm", c, j + 1)
                    v.scalar_tensor_tensor(out=hc[:, j, :], in0=O[j % 2][:, 0:D], scalar=tdecay[:, j:j + 1], in1=hin[u][:, j, :],
                                           op0=ALU.mult, op1=ALU.add).then_inc(s["h1_done"], 1)

            def leave(c):
                wait(dve, "h1_done", c)
                wait(dve, "w_mm", c)
                wait(dve, "W_done", c - 1)
                Wf = W[:, :, :].rearrange("p c d -> p (c d)")
                v.scalar_tensor_tensor(out=Wf, in0=Wf, scalar=DECAY ** CS, in1=O[1][0:HD, 0:2 * D],
                                       op0=ALU.mult, op1=ALU.add).then_inc(s["W_done"], 1)
                norm(resident(c), "b", c)

            def route(i, u, mid):
                c = 2 * i + u
                wait(dve, "lg_mm", c)
                v.tensor_tensor(lg[:, :, :], O[0][:, 0:TPC * E].rearrange("p (j e) -> p j e", e=E), _bc(gb[:, :], 1, TPC), ALU.add)\
                    .then_inc(s["lg_done"], 1)
                wait(dve, "lg_done", c)
                v.tensor_reduce(mx[:, :], lg[:, :, :], AX.X, ALU.max).then_inc(s["mx_done"], 1)
                wait(dve, "mx_done", c)
                v.tensor_tensor(lg[:, :, :], lg[:, :, :], _bc(mx[:, :], 2, E), ALU.subtract).then_inc(s["sub_done"], 1)
                wait(dve, "ex_done", c)
                v.tensor_reduce(rsum[:, :], ex[:, :, :], AX.X, ALU.add).then_inc(s["sum_done"], 1)
                wait(dve, "sum_done", c)
                v.reciprocal(rinv[:, :], rsum[:, :]).then_inc(s["inv_done"], 1)
                wait(dve, "inv_done", c)
                v.tensor_tensor(prob[:, :, :], ex[:, :, :], _bc(rinv[:, :], 2, E), ALU.mult).then_inc(s["prob_done"], 1)
                wait(dve, "prob_done", c)
                v.tensor_tensor(sel[:, :, :], prob[:, :, :], _bc(rb[:, :], 1, TPC), ALU.add).then_inc(s["sel_done"], 1)
                wait(dve, "sel_done", c)
                pair = sel[:, :, :].rearrange("p j (g u) -> p j g u", u=2)
                v.tensor_tensor(gs[:, :, :], pair[:, :, :, 0], pair[:, :, :, 1], ALU.add).then_inc(s["gs_done"], 1)
                wait_reg(dve, "gs_done", c)
                for j in range(TPC):
                    last = v.max(g8[:, j, :], gs[:, j, :])
                last.then_inc(s["g8_done"], 1)
                wait_reg(dve, "g8_done", c)
                for j in range(TPC):
                    last = v.max_index(gi[:, j, :], g8[:, j, :], gs[:, j, :])
                last.then_inc(s["gi_done"], 1)
                wait(dve, "gi_done", c)
                hitg = hit[:, :, :].rearrange("p j (k g) -> p k j g", k=TOP)
                for k in range(TOP):
                    last = v.tensor_tensor(hitg[:, k, :, 0:G], _bc(gi[:, :, k], 2, G), _bc(iota[:, 0:G], 1, TPC), ALU.is_equal)
                last.then_inc(s["ghit_done"], 1)
                wait(dve, "ghit_done", c)
                v.tensor_reduce(gm[:, :, :], hit[:, :, :].rearrange("p j (k g) -> p j g k", k=TOP)[:, :, 0:G, :], AX.X, ALU.add)\
                    .then_inc(s["gm_done"], 1)
                wait(dve, "gm_done", c)
                v.tensor_scalar(gm[:, :, :], gm[:, :, :], -1.0, 1.0e30, ALU.add, ALU.mult).then_inc(s["pen_done"], 1)
                wait(dve, "pen_done", c)
                for w in range(2):
                    last = v.tensor_tensor(pair[:, :, :, w], pair[:, :, :, w], gm[:, :, :], ALU.add)
                last.then_inc(s["msk_done"], 1)
                wait_reg(dve, "msk_done", c)
                for j in range(TPC):
                    last = v.max(g8[:, j, :], sel[:, j, :])
                last.then_inc(s["e8_done"], 1)
                wait_reg(dve, "e8_done", c)
                for j in range(TPC):
                    last = v.max_index(gi[:, j, :], g8[:, j, :], sel[:, j, :])
                last.then_inc(s["ei_done"], 1)
                wait(dve, "ei_done", c)
                hit4 = hit[:, :, :].rearrange("p j (e k) -> p j e k", k=TOP)
                for k in range(TOP):
                    last = v.tensor_tensor(hit4[:, :, :, k], _bc(gi[:, :, k], 2, E), _bc(iota[:, :], 1, TPC), ALU.is_equal)
                last.then_inc(s["ehit_done"], 1)
                wait(dve, "ehit_done", c)
                wait(dve, "pos_mm", c - 1)
                pk = picked[:, 0:TPC * E].rearrange("p (j e) -> p j e", e=E)
                v.tensor_reduce(pk, hit4, AX.X, ALU.max).then_inc(s["picked_done"], 1)
                mid()
                wait(dve, "picked_done", c)
                dve.wait_ge(s[f"scat{u}"], SCAT * i + CREDIT)
                v.scalar_tensor_tensor(out=rows[u][:, :, D:D + E], in0=pk, scalar=SCALE,
                                       in1=prob[:, :, :], op0=ALU.mult, op1=ALU.mult).then_inc(s["wf_done"], 1)
                flat = prod[:, :, :].rearrange("p j (e k) -> p (j e) k", k=TOP)
                hflat = hit[:, :, :].rearrange("p j (e k) -> p (j e) k", k=TOP)
                wait(dve, "slots_done", c - 1)
                v.tensor_tensor(flat, hflat, _bc(rank[:, :], 1, TPC * E), ALU.mult).then_inc(s["rk_prod"], 1)
                wait(dve, "rk_prod", c)
                v.tensor_reduce(slotrow[:, :, :].rearrange("p j e -> p (j e)"), flat, AX.X, ALU.add).then_inc(s["rk_sum"], 1)
                wait(dve, "rk_sum", c)
                v.tensor_tensor(rows[u][:, :, D + E:ROWLEN], slotrow[:, :, :], _bc(tok4[:, bass.ds(c * TPC, TPC)], 2, E), ALU.add)\
                    .then_inc(s["dest_done"], 1)
                wait(dve, "pos_mm", c)
                wait(dve, "carry_done", c - 1)
                wait(dve, "dest_done", c)
                v.tensor_tensor(slotrow[:, :, :], V[1][:, HT:HT + TPC * E].rearrange("p (j e) -> p j e", e=E),
                                _bc(carry[:, :], 1, TPC), ALU.add).then_inc(s["row_done"], 1)
                wait(dve, "row_done", c)
                v.tensor_tensor(carry[:, :], V[1][:, HT + TPC * E:HT + (TPC + 1) * E], carry[:, :], ALU.add).then_inc(s["carry_done"], 1)
                v.tensor_tensor(flat, hflat, _bc(slotrow[:, :, :].rearrange("p j e -> p (j e)"), 2, TOP), ALU.mult)\
                    .then_inc(s["prod_done"], 1)
                wait(dve, "prod_done", c)
                with nc.allow_low_precision(reason="row numbers: whole, below 2 ** 24"):
                    v.tensor_reduce(slots[u][:, :, :], prod[:, :, :].rearrange("p j (e k) -> p j k e", k=TOP), AX.X, ALU.add)\
                        .then_inc(s["slots_done"], 1)

            def shared_product(c):
                for k in range(2):
                    wait(dve, "su_done", c, k + 1)
                    v.scalar_tensor_tensor(out=ac[:, k, :], in0=V[k][:, 0:HT], scalar=bg[:, E:E + 1], in1=su[:, k, :],
                                           op0=ALU.add, op1=ALU.mult).then_inc(s["ac_done"], 1)

            def shared_out(c):
                hc = resident(c)
                for j in range(TPC):
                    wait(dve, "y_mm", c, j + 1)
                    v.tensor_tensor(hc[:, j, :], O[j % 2][:, 0:D], hc[:, j, :], ALU.add).then_inc(s["h_done"], 1)

            def both(i, u):
                after = (i + 1, 0) if u else (i, 1)
                enter(*after)
                route(i, u, lambda: mask(2 * after[0] + after[1]))
                shared_product(2 * i + u)
                attend(*after)
                shared_out(2 * i + u)
                leave(2 * after[0] + after[1])

            dve.wait_ge(s["fills"], 9)
            enter(0, 0)
            mask(0)
            attend(0, 0)
            leave(0)
            with dve.Fori(0, CHUNKS // 2 - 1) as i:
                both(i, 0)
                both(i, 1)
            both(CHUNKS // 2 - 1, 0)
            route(CHUNKS // 2 - 1, 1, lambda: None)
            shared_product(CHUNKS - 1)
            shared_out(CHUNKS - 1)

            dve.wait_ge(s["carry_done"], CHUNKS + AHEAD)
            step = [0]

            def after(ins):
                step[0] += 1
                ins.then_inc(s["tail_mult"], 1)
                dve.wait_ge(s["tail_mult"], step[0])
            v.tensor_copy(carryi[:, :], carry[0:1, :]).then_inc(s["table"], 1)
            after(v.scalar_tensor_tensor(out=cnt[:, :], in0=carry[0:1, :], scalar=float(BLK - 1), in1=base[0:1, :], op0=ALU.add,
                                         op1=ALU.subtract))
            after(v.tensor_copy(cnti[:, :], cnt[:, :]))
            after(v.tensor_scalar(cnti[:, :], cnti[:, :], BLK.bit_length() - 1, None, ALU.logical_shift_right))
            after(v.tensor_copy(nblk[:, :], cnti[:, :]))
            after(v.tensor_tensor_scan(cum[:, :], one1[:, :], nblk[:, :], 0.0, ALU.mult, ALU.add))
            after(v.tensor_scalar(skipd[:, :], nblk[:, :], -float(BLK), float(ROOM), ALU.mult, ALU.add))
            past = big.rearrange("p (i e) -> p i e", e=E)
            after(v.tensor_tensor(past, _bc(cum[:, :], 1, BLOCKS), _bc(blki[:, :], 2, E), ALU.is_le))
            after(v.tensor_reduce(tabe[:, :], past, AX.X, ALU.add))
            after(v.tensor_tensor(past, past, _bc(skipd[:, :], 1, BLOCKS), ALU.mult))
            after(v.tensor_reduce(tabr[:, :], past, AX.X, ALU.add))
            after(v.scalar_tensor_tensor(out=tabr[:, :], in0=blki[:, :], scalar=float(BLK), in1=tabr[:, :], op0=ALU.mult, op1=ALU.add))
            after(v.tensor_scalar(tabri[:, :], tabr[:, :], float(E * ROOM), None, ALU.min))
            after(v.tensor_scalar(tabei[:, :], tabe[:, :], float(E - 1), None, ALU.min))
            v.engine_nop().then_inc(s["tables_set"], 1)

            def prepare(i, r):
                b = 4 * i + r
                e = dve.value_load(tabei[0:1, bass.ds(b, 1)], min_val=0, max_val=E - 1)
                wait(dve, "b_up", b - 2)
                v.tensor_copy(wac[r % 2][:, :], wa[:, bass.ds(e * WAW, WAW)]).then_inc(s["b_wa"], 1)
                dve.wait_ge(s[f"xl{r}"], 16 * (i + 1))
                dve.wait_ge(s[f"ysc{r}"], YSC * (i + 1))
                v.tensor_copy(dcur[r][:, :], xb[r][:, :, bass.ds(D + E + e, 1)].rearrange("p t o -> p (t o)"))
                v.tensor_copy(wcur[r][:, :], xb[r][:, :, bass.ds(D + e, 1)].rearrange("p t o -> p (t o)"))
                v.tensor_copy(bcur[r][:, 0:1], bu[:, bass.ds(e, 1)])
                v.tensor_copy(bcur[r][:, 1:2], bg[:, bass.ds(e, 1)]).then_inc(s["b_cur"], 1)

            def product(i, r):
                b = 4 * i + r
                wait(dve, "b_su", b)
                wait(dve, "b_cur", b)
                wait(dve, "b_down", b - 2)
                v.scalar_tensor_tensor(out=acb[r % 2][:, :], in0=U[r % 2][:, BLK:2 * BLK], scalar=bcur[r][:, 1:2],
                                       in1=sub[r % 2][:, :], op0=ALU.add, op1=ALU.mult).then_inc(s["b_ac"], 1)

            def scaled(i, r):
                wait(dve, "b_down", 4 * i + r)
                for t in range(BT2):
                    last = v.tensor_scalar(yb[r][:, t, :], O[r % 2][:, t * D:(t + 1) * D], wcur[r][:, t:t + 1], None, ALU.mult)
                last.then_inc(s["b_y"], 1)

            pipeline(dve, prepare, product, scaled)

            def finish(c, u, it, first):
                if not first:
                    dve.wait_ge(s[f"st{u}"], 32 * it - 32)
                dve.wait_ge(s[f"yl{u}"], 16 * it)
                y4 = yin[u].rearrange("p j (k d) -> p j k d", k=TOP)
                v.tensor_tensor(fin[u][:, :, :], y4[:, :, 0, :], y4[:, :, 1, :], ALU.add).then_inc(s[f"pair_done{u}"], 1)
                dve.wait_ge(s[f"pair_done{u}"], 2 * it - 1)
                v.tensor_tensor(fin[u][:, :, :], fin[u][:, :, :], h[:, bass.ds(c * (TPC * D), TPC * D)].rearrange("p (j d) -> p j d", d=D),
                                ALU.add).then_inc(s[f"pair_done{u}"], 1)
                dve.wait_ge(s[f"pair_done{u}"], 2 * it)
                dve.wait_ge(s[f"half_done{u}"], it)
                v.tensor_tensor(fin[u][:, :, :], fin[u][:, :, :], y4[:, :, 2, :], ALU.add).then_inc(s[f"fin_done{u}"], 1)
            for u in range(2):
                dve.wait_ge(s[f"gath{u}"], 16 * TPC * (CHUNKS // 2 + 1))
            for u in range(2):
                finish(u, u, 1, True)
            with dve.Fori(2, CHUNKS // 2 + 1) as it:
                for u in range(2):
                    finish(2 * it - 2 + u, u, it, False)

        @block.scalar
        def _(act):
            ac_ = nc.scalar
            act.wait_ge(s["weights"], NLOAD)
            for m, dst in enumerate((Gm, Hm)):
                for hh in range(NH):
                    n = m * NH + hh
                    act.wait_ge(s["gh_mm"], n + 1)
                    ac_.activation(dst[:, :, hh, :], O[n % 2][0:HD, 0:2 * D].rearrange("p (c d) -> p c d", c=2), ACT.Copy)\
                        .then_inc(s["gh_copied"], 1)
            for c in range(2):
                last = ac_.activation(wgtb[:, c, :, :], _bc(wgt[:, c, :], 2, HD), ACT.Copy)
            last.then_inc(s["wgtb_ready"], 1)
            for i in range(2):
                act.wait_ge(s["x0_tp"], i + 1)
                ac_.activation(x0T[:, :, i:STEPS:2], X[i][0:HD, 0:256].rearrange("p (c t) -> p c t", c=2)[:, :, 0:S0], ACT.Copy)\
                    .then_inc(s["x0_copied"], 1)
            for hh in range(NH):
                act.wait_ge(s["gate_mm"], hh + 1)
                if hh:
                    act.wait_ge(s["bt_scaled"], 3 * hh)
                ac_.activation(gate[:, :], O[0][0:HD, 0:STEPS], ACT.Sigmoid).then_inc(s["gate_ready"], 1)
                for c in range(2):
                    act.wait_ge(s["at_mm"], 4 * hh + c + 1)
                    dst = AT[:, c, :].rearrange("p (s k) -> p s k", k=NH)[:, :, hh]
                    ac_.activation(dst, U[c][0:HD, 0:STEPS], ACT.Copy).then_inc(s["at_copied"], 1)
            act.wait_ge(s["bt_scaled"], 3 * NH)
            act.wait_ge(s["at_copied"], 2 * NH)
            act.wait_ge(s["odd_moved"], 16)
            act.wait_ge(s["kone_ready"], 1)
            for u in range(2):
                ac_.activation(gcur[u][:, :], gidx[:, u * TPC:(u + 1) * TPC], ACT.Copy).then_inc(s["gcur_done"], 1)
            def spread(n, c):
                wait(act, "mv_" + n, c)
                ac_.activation(sd[:, :], mv[:, :, 1], ACT.Sqrt, bias=epsc[:, :]).then_inc(s["sd_" + n], 1)

            def evac_T(n, c):
                for j in range(TPC):
                    wait(act, "tp_" + n, c, j + 1)
                    ac_.activation(xnT[n][:, :, j * 128:(j + 1) * 128], X[j % 2][0:HD, 0:256].rearrange("p (c t) -> p c t", c=2),
                                   ACT.Copy).then_inc(s["xT_" + n], 1)

            def keys_in(i, u):
                c = 2 * i + u
                wait(act, "ab_tp", c - 1)
                wait(act, "s_mm", c - 1)
                ac_.activation(ATc[:, :, :], AT[:, :, bass.ds(c * R, R)], ACT.Copy)
                ac_.activation(BTc[:, :, :], BT[:, :, bass.ds(c * R, R)], ACT.Copy).then_inc(s["abT_done"], 1)
                act.wait_ge(s[f"gath{u}"], 16 * TPC * (i + 1))
                ac_.activation(gcur[u][:, :], gidx[:, bass.ds((c + 2) * TPC, TPC)], ACT.Copy).then_inc(s["gcur_done"], 1)

            def keys_out(c):
                wait(act, "ab_tp", c)
                wait(act, "w_mm", c - 1)
                ac_.activation(Ac[:, :], O[0][0:R, 0:D], ACT.Copy, scale=DECAY ** CS)
                ac_.activation(Bc[:, :], O[0][0:R, D:2 * D], ACT.Copy).then_inc(s["ab_done"], 1)

            def experts_in(i, u):
                c = 2 * i + u
                wait(act, "up_mm", c - 1)
                evac_T("b", c)
                act.wait_ge(s[f"scat{u}"], SCAT * i + CREDIT)
                ac_.activation(rows[u][:, :, 0:D], xn["b"][:, :, :], ACT.Copy).then_inc(s["rowx_done"], 1)
                wait(act, "sub_done", c)
                ac_.activation(ex[:, :, :], lg[:, :, :], ACT.Exp).then_inc(s["ex_done"], 1)
                for k in range(2):
                    wait(act, "up_mm", c, k + 1)
                    wait(act, "ac_done", c - 1)
                    ac_.activation(su[:, k, :], U[k][:, 0:HT], ACT.Silu, bias=bu[:, E:E + 1]).then_inc(s["su_done"], 1)

            def weights_out(c):
                wait(act, "wT_tp", c)
                wait(act, "y_mm", c - 1)
                ac_.activation(wT[0:E, 0:384], X[0][0:E, 0:384], ACT.Copy)
                ac_.activation(wT[0:E, 384:CT], X[1][0:E, 0:CT - 384], ACT.Copy).then_inc(s["wT_done"], 1)

            def both(i, u):
                after = (i + 1, 0) if u else (i, 1)
                c, n = 2 * i + u, 2 * after[0] + after[1]
                keys_in(*after)
                spread("a", n)
                experts_in(i, u)
                keys_out(n)
                wait(act, "o_mm", n - 1)
                evac_T("a", n)
                weights_out(c)
                spread("b", n)

            keys_in(0, 0)
            keys_out(0)
            spread("a", 0)
            evac_T("a", 0)
            spread("b", 0)
            with act.Fori(0, CHUNKS // 2 - 1) as i:
                both(i, 0)
                both(i, 1)
            both(CHUNKS // 2 - 1, 0)
            experts_in(CHUNKS // 2 - 1, 1)
            weights_out(CHUNKS - 1)

            act.wait_ge(s["tables_set"], 1)

            def prepare(i, r):
                b = 4 * i + r
                e = act.value_load(tabei[0:1, bass.ds(b, 1)], min_val=0, max_val=E - 1)
                wait(act, "b_tp", b)
                wait(act, "b_up", b - 2)
                ac_.activation(xT[r % 2][:, :, :].rearrange("p k (t n) -> p t k n", n=128),
                               X[r % 2][0:HD, :].rearrange("p (t k n) -> p t k n", t=2, k=2), ACT.Copy).then_inc(s["b_xT"], 1)
                wait(act, "b_down", b - 2)
                ac_.activation(wdc[r % 2][:, :], wd[:, bass.ds(e * D, D)], ACT.Copy).then_inc(s["b_wd"], 1)

            def silu(i, r):
                b = 4 * i + r
                wait(act, "b_cur", b)
                wait(act, "b_up", b)
                wait(act, "b_ac", b - 2)
                ac_.activation(sub[r % 2][:, :], U[r % 2][:, 0:BLK], ACT.Silu, bias=bcur[r][:, 0:1]).then_inc(s["b_su"], 1)

            pipeline(act, prepare, silu, None)

        @block.tensor
        def _(pe):
            mm = nc.tensor.matmul
            pe.wait_ge(s["weights"], NLOAD)
            for m, (left, right) in enumerate(((wk, wq), (wv, woT))):
                for hh in range(NH):
                    n = m * NH + hh
                    if n >= 2:
                        pe.wait_ge(s["gh_copied"], n - 1)
                    r = slice(64 * (hh % 2), 64 * (hh % 2) + 64)
                    for c in range(2):
                        last = mm(O[n % 2][0:HD, c * D:(c + 1) * D], left[r, hh // 2, c * HD:(c + 1) * HD], right[r, hh // 2, :],
                                  start=True, stop=True)
                    last.then_inc(s["gh_mm"], 1)
            pe.wait_ge(s["gh_copied"], 2 * NH)
            pe.wait_ge(s["wgtb_ready"], 1)
            pe.wait_ge(s["x0_norm"], 1)
            for i in range(2):
                for c in range(2):
                    last = nc.tensor.transpose(X[i][0:HD, c * 128:c * 128 + S0], x0n[:, i, c * HD:(c + 1) * HD], ident[0:S0, 0:S0])
                last.then_inc(s["x0_tp"], 1)
            pe.wait_ge(s["x0_copied"], 2)
            for hh in range(NH):
                if hh:
                    pe.wait_ge(s["gate_ready"], hh)
                for k in range(2):
                    last = mm(O[0][0:HD, 0:STEPS], wgtb[:, k, hh, :], x0T[:, k, :], start=(k == 0), stop=(k == 1))
                last.then_inc(s["gate_mm"], 1)
                for m, (w, bank) in enumerate(((Gm, U), (Hm, V))):
                    if hh:
                        if m == 0:
                            pe.wait_ge(s["at_copied"], 2 * hh)
                        else:
                            pe.wait_ge(s["bt_scaled"], 3 * hh)
                    for c in range(2):
                        for k in range(2):
                            last = mm(bank[c][0:HD, 0:STEPS], w[:, k, hh, c * HD:(c + 1) * HD], x0T[:, k, :], start=(k == 0), stop=(k == 1))
                        last.then_inc(s["at_mm"], 1)
            pe.wait_ge(s["at_copied"], 2 * NH)
            pe.wait_ge(s["bt_scaled"], 3 * NH)
            pe.wait_ge(s["fills"], 9)
            def keys(c):
                wait(pe, "abT_done", c)
                wait(pe, "h1_done", c - 1)
                wait(pe, "h_done", c - 2)
                for m, src in enumerate((ATc, BTc)):
                    for k in range(2):
                        last = nc.tensor.transpose(O[0][0:R, m * D + k * HD:m * D + (k + 1) * HD], src[:, k, :], ident[0:HD, 0:HD])
                last.then_inc(s["ab_tp"], 1)

            def transposes(n, c):
                wait(pe, "xn_" + n, c)
                for j in range(TPC):
                    if j >= 2:
                        wait(pe, "xT_" + n, c, j - 1)
                    elif n == "a":
                        wait(pe, "xT_b", c - 1)
                    for k in range(2):
                        last = nc.tensor.transpose(X[j % 2][0:HD, k * 128:(k + 1) * 128], xn[n][:, j, k * HD:(k + 1) * HD], ident[:, :])
                    last.then_inc(s["tp_" + n], 1)

            def scores(c):
                wait(pe, "su_done", c - 1)
                for g in range(2):
                    wait(pe, "xT_a", c, 3 if g == 0 else TPC)
                    for k in range(2):
                        last = mm(U[g][0:R, 0:HT], ATc[:, k, :], xnT["a"][:, k, g * HT:(g + 1) * HT], start=(k == 0), stop=(k == 1))
                    last.then_inc(s["s_mm"], 1)

            def outputs(c):
                wait(pe, "ab_done", c)
                wait(pe, "W_done", c - 1)
                for j in range(TPC):
                    wait(pe, "P_done", c, 1 if 128 * (j + 1) <= HT else 2)
                    if j >= 2:
                        wait(pe, "h1_done", c, j - 1)
                    t = slice(j * 128, (j + 1) * 128)
                    for k in range(2):
                        mm(O[j % 2][:, 0:D], xnT["a"][:, k, t], W[:, k, :], start=(k == 0), stop=False)
                    mm(O[j % 2][:, 0:D], P[:, t], Bc[:, :], start=False, stop=True).then_inc(s["o_mm"], 1)

            def state(c, shared):
                if shared:
                    wait(pe, "h_done", c - 1)
                wait(pe, "h1_done", c, TPC - 1)
                for k in range(2):
                    last = mm(O[1][0:HD, k * D:(k + 1) * D], Ac[:, k * HD:(k + 1) * HD], Bc[:, :], start=True, stop=True)
                last.then_inc(s["w_mm"], 1)

            def logits_up(c):
                wait(pe, "xT_b", c)
                wait(pe, "h_done", c - 1)
                for j in range(TPC):
                    for k in range(2):
                        last = mm(O[0][:, j * E:(j + 1) * E], xnT["b"][:, k, j * 128:(j + 1) * 128], gw[:, k, :],
                                  start=(k == 0), stop=(k == 1))
                last.then_inc(s["lg_mm"], 1)
                wait(pe, "ac_done", c - 1)
                wait(pe, "P_done", c)
                wait(pe, "carry_done", c - 1)
                for k in range(2):
                    for bank, w in ((U, swu), (V, swg)):
                        for r in range(2):
                            last = mm(bank[k][:, 0:HT], w[:, r, :], xnT["b"][:, r, k * HT:(k + 1) * HT], start=(r == 0), stop=(r == 1))
                    last.then_inc(s["up_mm"], 1)

            def places(c, u, later):
                wait(pe, "picked_done", c)
                mm(V[1][:, HT:HT + (TPC + 1) * E], earlier[:, :], picked[:, :], start=True, stop=False)
                for i in range(TPC):
                    n = TPC - i
                    last = mm(V[1][:, HT + (i + 1) * E:HT + (TPC + 1) * E].rearrange("p (n e) -> p n e", e=E), ones[:, :],
                              _bc(picked[:, i * E:(i + 1) * E], 1, n), start=False, stop=(i == TPC - 1))
                last.then_inc(s["pos_mm"], 1)
                wait(pe, "wf_done", c)
                if later:
                    wait(pe, "xT_a", c + 1)
                for j in range(TPC):
                    last = nc.tensor.transpose(X[j // 3][0:E, (j % 3) * 128:(j % 3 + 1) * 128], rows[u][:, j, D:D + E], ident[:, :])
                last.then_inc(s["wT_tp"], 1)

            def down(c, later):
                wait(pe, "wT_done", c)
                wait(pe, "ac_done", c)
                acf = ac[:, :, :].rearrange("p k n -> p (k n)")
                for j in range(TPC):
                    if j >= 2:
                        wait(pe, "h_done", c, j - 1)
                    elif later:
                        wait(pe, "h1_done", c + 1)
                    else:
                        wait(pe, "W_done", c)
                    mm(O[j % 2][:, 0:D], acf[:, j * 128:(j + 1) * 128], swd[:, :], start=True, stop=False)
                    mm(O[j % 2][:, 0:D], wT[:, j * 128:(j + 1) * 128], bd[:, :], start=False, stop=True).then_inc(s["y_mm"], 1)

            def both(i, u):
                c = 2 * i + u
                transposes("b", c)
                logits_up(c)
                keys_after(c + 1)
                transposes("a", c + 1)
                scores(c + 1)
                places(c, u, True)
                outputs(c + 1)
                down(c, True)
                state(c + 1, True)

            def keys_after(c):
                wait(pe, "W_done", c - 1)
                wait(pe, "lg_done", c - 1)
                keys(c)

            keys(0)
            transposes("a", 0)
            scores(0)
            outputs(0)
            state(0, False)
            with pe.Fori(0, CHUNKS // 2 - 1) as i:
                both(i, 0)
                both(i, 1)
            both(CHUNKS // 2 - 1, 0)
            transposes("b", CHUNKS - 1)
            logits_up(CHUNKS - 1)
            places(CHUNKS - 1, 1, False)
            down(CHUNKS - 1, False)

            pe.wait_ge(s["h_done"], TPC * (CHUNKS + AHEAD))

            def turn(i, r):
                b = 4 * i + r
                pe.wait_ge(s[f"xl{r}"], 16 * (i + 1))
                wait(pe, "b_xT", b - 2)
                for t in range(BT2):
                    for k in range(2):
                        last = nc.tensor.transpose(X[r % 2][0:HD, (2 * t + k) * 128:(2 * t + k + 1) * 128],
                                                   xb[r][:, t, k * HD:(k + 1) * HD], ident[:, :])
                last.then_inc(s["b_tp"], 1)

            def project(i, r):
                b = 4 * i + r
                wait(pe, "b_xT", b)
                wait(pe, "b_wa", b)
                wait(pe, "b_ac", b - 2)
                for m in range(2):
                    for k in range(2):
                        last = mm(U[r % 2][:, m * BLK:(m + 1) * BLK], wac[r % 2][:, (2 * m + k) * HID:(2 * m + k + 1) * HID],
                                  xT[r % 2][:, k, :], start=(k == 0), stop=(k == 1))
                last.then_inc(s["b_up"], 1)

            def project_down(i, r):
                b = 4 * i + r
                wait(pe, "b_wd", b)
                wait(pe, "b_ac", b)
                wait(pe, "b_y", b - 2)
                for t in range(BT2):
                    last = mm(O[r % 2][:, t * D:(t + 1) * D], acb[r % 2][:, t * 128:(t + 1) * 128], wdc[r % 2][:, :],
                              start=True, stop=True)
                last.then_inc(s["b_down"], 1)

            pipeline(pe, turn, project, project_down)


_INS = ['x', 'L0_tok_gamma', 'L0_tok_beta', 'L0_tok_w', 'L0_tok_b', 'L0_attn_w_key', 'L0_attn_w_value', 'L0_attn_w_query',
        'L0_attn_w_gate', 'L0_attn_w_out', 'L0_ffn_gate_w', 'L0_ffn_gate_b', 'L0_ffn_bias', 'L0_ffn_Wu', 'L0_ffn_bu', 'L0_ffn_Wg',
        'L0_ffn_bg', 'L0_ffn_Wd', 'L0_ffn_bd', 'L0_ffn_sWu', 'L0_ffn_sbu', 'L0_ffn_sWg', 'L0_ffn_sbg', 'L0_ffn_sWd', 'L0_ffn_sbd']


_TURNED = ('L0_attn_w_gate', 'L0_attn_w_out', 'L0_ffn_bu', 'L0_ffn_bg')


def shape_constants():
    import numpy as np
    f = np.float32
    t = np.arange(STEPS)
    step = np.arange(R) // NH
    half = (np.arange(128) >= 64).astype(int)
    return {
        "c_ident": np.eye(128, dtype=f),
        "c_rowbase": (np.arange(B) * N).astype(f)[:, None],
        "c_mhalf": np.full((128, 128), -0.5, f),
        "c_wdec": np.tile((WRITE * DECAY ** (-(t % CS + 1.0))).astype(f), (HD, 1)),
        "c_causal": (step[:, None] < np.arange(CS)[None, :]).astype(f),
        "c_tdecay": (DECAY ** (2.0 * np.arange(TPC)[None, :] + half[:, None])).astype(f),
        "c_tok4": (TOP * (np.arange(TILES)[None, :] * 128 + np.arange(128)[:, None])).astype(f),
        "c_rank": np.tile(np.arange(TOP, dtype=f), (128, 1)),
        "c_base": np.tile(np.arange(E, dtype=f) * ROOM, (128, 1)),
        "c_blki": np.arange(BLOCKS, dtype=f)[None, :],
        "c_earlier": np.triu(np.ones((128, 128), f), 1),
        "c_iota": np.tile(np.arange(E, dtype=f), (128, 1)),
    }


def kernel(**inputs):
    import numpy as np
    import concourse.bacc as bacc
    from concourse.bass_utils import run_bass_kernel_spmd

    nc = bacc.Bacc("TRN2", target_bir_lowering=False, num_devices=1)
    arrays, aps = {}, {}
    given = {n: np.ascontiguousarray(np.asarray(inputs[n]).T if n in _TURNED else inputs[n]) for n in _INS}
    given.update(shape_constants())
    for name, v in given.items():
        arrays[f"in_{name}"] = v
        aps[name] = nc.dram_tensor(f"in_{name}", v.shape, mybir.dt.from_np(v.dtype), kind="ExternalInput").ap()
    out = nc.dram_tensor("out_0", (B, KEEP, D), mybir.dt.float32, kind="ExternalOutput").ap()
    tower(nc, aps, out)
    return run_bass_kernel_spmd(nc, [arrays], core_ids=[0]).results[0]["out_0"]
```

```python
from contextlib import ExitStack

import concourse.bass as bass
from concourse import mybir

B, N, D = 64, 256, 192
KEEP = int(N * 0.7)
STEPS = KEEP + KEEP % 2
TILES = STEPS // 2
TPC = 5
CHUNKS = TILES // TPC
CS = 2 * TPC
NH, DK = 8, 64
E, G, HID = 16, 8, 128
TOP = 4
SCALE = 2.5
EPS = 1e-5
DECAY, WRITE = 0.95, 0.1
HD = D // 2
R = CS * NH
CT = TPC * 128
HT = CT // 2
ROUNDS = (STEPS + 7) // 8
XC = 8
XCHUNKS = 128 // XC
XA = 4
XBUF = 4
GROUPS = ((0, 64), (64, 96), (96, 112), (112, 128))
S0 = STEPS // 2
TOK = TILES * 128
BLK = 256
BT2 = BLK // 128
ROOM = TOK + BLK
BLOCKS = (TOK * TOP - E) // BLK + E
BLOCKS += -BLOCKS % 4
ROWLEN = D + E + 1
AHEAD = 4
WAW = 2 * 2 * HID


def tower(nc, a, out):
    f32, u32, i32, bf16 = mybir.dt.float32, mybir.dt.uint32, mybir.dt.int32, mybir.dt.bfloat16
    ALU, ACT, AX = mybir.AluOpType, mybir.ActivationFunctionType, mybir.AxisListType
    es = ExitStack()
    with es:
        sb = lambda name, shape, dt=f32: es.enter_context(nc.sbuf_tensor(name, shape, dt))
        pb = lambda name, p, n: es.enter_context(nc.psum_tensor(name, [p, n], f32))
        sem = lambda name: es.enter_context(nc.semaphore(name))

        h = sb("h", [128, TILES * D])
        ident = sb("ident", [128, 128])
        wall = sb("wall", [128, E * WAW])
        wa = wall[0:HD, :]
        wd = sb("wd", [HID, E * D])
        swu = sb("swu", [HD, 2, HID])
        swg = sb("swg", [HD, 2, HID])
        swd = sb("swd", [HID, D])
        bu = sb("bu", [HID, E + 1])
        bg = sb("bg", [HID, E + 1])
        bd = sb("bd", [E + 1, D])
        tok = sb("tok", [128, TILES])
        spare = sb("spare", [128, BT2])
        zero = sb("zero", [128, D])
        earlier = sb("earlier", [128, 128], bf16)
        earlier_in = sb("earlier_in", [128, 128])
        ones = sb("ones", [128, 128], bf16)
        carry = sb("carry", [128, E])
        base = sb("base", [128, E])
        blki = sb("blki", [1, BLOCKS])
        pad = sb("pad", [128, BT2, ROWLEN])
        epsc = sb("epsc", [128, 1])
        gw = sb("gw", [HD, 2, E])
        gb = sb("gb", [E, 1])
        rb = sb("rb", [128, E])
        iota = sb("iota", [128, E])
        causal = sb("causal", [R, CS])
        tdecay = sb("tdecay", [128, TPC])
        kv = sb("kv", [128, 4 * STEPS * NH])
        AT = kv[0:HD, 0:2 * STEPS * NH].rearrange("p (c n) -> p c n", c=2)
        BT = kv[0:HD, 2 * STEPS * NH:4 * STEPS * NH].rearrange("p (c n) -> p c n", c=2)
        W = sb("W", [HD, 2, D])
        taken = [0]

        def in_kv(p, n):
            lo = taken[0]
            taken[0] += n
            assert taken[0] <= 4 * STEPS * NH
            return kv[0:p, lo:lo + n]

        mhalf = sb("mhalf", [128, 128])

        xin = [h[:, i * XC * D:(i + 1) * XC * D] for i in range(XBUF - 1)] + [in_kv(128, XC * D)]
        xst = h[:, TILES * D - 128 * 6:TILES * D].rearrange("p (n k) -> p n k", k=6)
        xmean = in_kv(128, 128)
        xscr = in_kv(128, D)
        xpass = [in_kv(128, XA * D) for _ in range(2)]
        xdot = in_kv(128, 128)
        xtmp = in_kv(128, 128)
        xvar = in_kv(128, 128)
        xrs = in_kv(128, 128)
        gam = in_kv(128, D)
        bet = in_kv(128, D)
        tw = in_kv(128, D)
        gamw = in_kv(128, D)
        tb = sb("tb", [128, 1])
        tcon = sb("tcon", [128, 1])
        tcon2 = sb("tcon2", [128, 1])
        sc = in_kv(B, 2 * N).rearrange("p (k n) -> p k n", k=2)
        top = [sb(f"top{u}", [B, 8]) for u in range(2)]
        idx = sb("idx", [B, ROUNDS * 8], u32)
        rowbase = sb("rowbase", [B, 1])
        rowi = sb("rowi", [B, ROUNDS * 8], u32)
        odd = sb("odd", [B, TILES], u32)
        gidx = sb("gidx", [128, TILES + 2 * TPC], u32)
        kidx = sb("kidx", [S0, 2], u32)
        kone = sb("kone", [S0, 2, 1], u32)

        used = [(XBUF - 1) * XC * D]

        def in_h(p, x, y):
            lo = used[0]
            used[0] += x * y
            assert used[0] <= TILES * D - 128 * 6
            return h[0:p, lo:lo + x * y].rearrange("p (x y) -> p x y", x=x)

        wk, wq, wv, woT = (in_h(128, 4, D) for _ in range(4))
        wgt = sb("wgt", [HD, 2, NH])
        wgtb = in_h(HD, 2, NH * HD).rearrange("p c (k d) -> p c k d", k=NH)
        Gm, Hm = (in_h(HD, 2, NH * D).rearrange("p c (k d) -> p c k d", k=NH) for _ in range(2))
        x0 = in_h(S0, 2, D)
        x0st = sb("x0st", [S0, 2, 6])
        x0mv = sb("x0mv", [S0, 2, 2])
        x0r = sb("x0r", [S0, 2])
        x0n = in_h(S0, 2, D)
        x0T = sb("x0T", [HD, 2, STEPS])
        wdec = sb("wdec", [HD, STEPS])
        gate = sb("gate", [HD, STEPS])

        gcur = [sb(f"gcur{u}", [128, TPC], u32) for u in range(2)]
        hin = [sb(f"hin{u}", [128, TPC, D]) for u in range(2)]
        rows = [sb(f"rows{u}", [128, TPC, ROWLEN]) for u in range(2)]
        slots = [sb(f"slots{u}", [128, TPC, TOP], u32) for u in range(2)]
        st = sb("st", [128, TPC, 6])
        mv = {n: sb("mv_" + n, [128, TPC, 2]) for n in "ab"}
        sd = {n: sb("sd_" + n, [128, TPC]) for n in "ab"}
        rs = {n: sb("rs_" + n, [128, TPC]) for n in "ab"}
        shift = {n: sb("shift_" + n, [128, TPC]) for n in "ab"}
        rs1 = sb("rs1", [128, TPC])
        xn = sb("xn", [128, TPC, D])
        xnT = {n: sb("xnT_" + n, [HD, 2, CT]) for n in "ab"}
        P = sb("P", [R, CT])
        ATc = sb("ATc", [HD, 2, R])
        BTc = sb("BTc", [HD, 2, R])
        Ac = sb("Ac", [R, D])
        Bc = sb("Bc", [R, D])
        lgT = sb("lgT", [E, CT])
        lg = sb("lg", [128, TPC, E])
        mx = sb("mx", [128, TPC])
        ex = sb("ex", [128, TPC, E])
        rsum = sb("rsum", [128, TPC])
        rinv = sb("rinv", [128, TPC])
        prob = sb("prob", [128, TPC, E])
        sel = sb("sel", [128, TPC, E])
        gs = sb("gs", [128, TPC, G])
        g8 = sb("g8", [128, TPC, 8])
        gi = sb("gi", [128, TPC, 8], u32)
        hit = sb("hit", [128, TPC, E * TOP])
        prod = sb("prod", [128, TPC, E * TOP])
        gm = sb("gm", [128, TPC, G])
        picked = sb("picked", [128, (TPC + 1) * E], bf16)
        slotrow = sb("slotrow", [128, TPC, E])
        wT = sb("wT", [E + 1, CT])
        su = sb("su", [HID, 2, HT])
        ac = sb("ac", [HID, 2, HT])

        cnt = sb("cnt", [1, E])
        cnti = sb("cnti", [1, E], i32)
        nblk = sb("nblk", [1, E])
        cum = sb("cum", [1, E])
        one1 = sb("one1", [1, E])
        skipd = sb("skipd", [1, E])
        carryi = sb("carryi", [1, E], i32)
        tabe = sb("tabe", [1, BLOCKS])
        tabr = sb("tabr", [1, BLOCKS])
        tabei = sb("tabei", [1, BLOCKS], i32)
        tabri = sb("tabri", [1, BLOCKS], i32)
        big = kv[0:1, 0:BLOCKS * E]

        taken[0] = 0
        xb = [in_kv(128, BT2 * ROWLEN).rearrange("p (t n) -> p t n", t=BT2) for u in range(4)]
        wac = [in_kv(HD, WAW) for u in range(2)]
        wdc = [in_kv(HID, D) for u in range(2)]
        xT = [in_kv(HD, 2 * BLK).rearrange("p (k n) -> p k n", k=2) for u in range(2)]
        sub = [in_kv(HID, BLK) for u in range(2)]
        acb = [in_kv(HID, BLK) for u in range(2)]
        yb = [rows[u % 2][:, :, :].rearrange("p j n -> p (j n)")[:, (u // 2) * BT2 * D:(u // 2 + 1) * BT2 * D]
              .rearrange("p (t n) -> p t n", t=BT2) for u in range(4)]
        wcur = [sb(f"wcur{u}", [128, BT2]) for u in range(4)]
        dest = [sb(f"dest{u}", [128, BT2]) for u in range(4)]
        dcur = [sb(f"dcur{u}", [128, BT2], u32) for u in range(4)]
        bcur = [sb(f"bcur{u}", [128, 2]) for u in range(4)]

        YW = 2 * TPC * D
        yin = [wall[:, u * YW:(u + 1) * YW].rearrange("p (q j n) -> p q j n", q=2, j=TPC) for u in range(2)]
        fin = hin

        X = [pb("X0", 128, 512), pb("X1", 128, 512)]
        O = [pb("O0", 128, 512), pb("O1", 128, 512)]
        U = [pb("U0", 128, 512), pb("U1", 128, 512)]
        V = [pb("V0", 128, 512), pb("V1", 128, 512)]

        score_d = nc.dram_tensor("score_d", [128, 128], f32, kind="Internal").ap()
        lists = nc.dram_tensor("lists", [E * ROOM + BLK + 4 * 128, ROWLEN], f32, kind="Internal").ap()
        yk = [nc.dram_tensor(f"yk{q}", [TOK + BLK, D], f32, kind="Internal").ap() for q in range(2)]
        row0_d = nc.dram_tensor("row0_d", [1, STEPS], u32, kind="Internal").ap()

        names = """firsts weights x_loaded0 x_loaded1 x_loaded2 x_loaded3 x_used""".split()
        names += """act_mean act_var stats_done mean_half mean_ready gamw_ready tcon_ready fold_ready var_ready rstd_ready
            mhalf_ready score_ready score_out score_in top8 top8i top8r rowi_ready odd_ready odd_moved""".split()
        names += """row0_out kidx_in kone_ready x0_in x0_stats x0_mv x0_rstd0 x0_rstd x0_norm x0_tp x0_copied
            wgtb_ready gh_mm gh_copied at_mm at_copied gate_mm gate_ready bt_scaled""".split()
        names += "fills pad_ready pads table tables_set zero_ready zeroed".split()
        names += "gath0 gath1 scat0 scat1 xl0 xl1 xl2 xl3 ysc0 ysc1 ysc2 ysc3 yl0 yl1 st0 st1".split()
        names += "fin_done0 fin_done1 pair_done0 pair_done1 tail_mult".split()
        per_chunk = dict(
            gcur_done=1, st_a=1, st_b=1, mv_a=1, mv_b=1, sd_a=1, sd_b=1, rs_a=1, rs_b=1, shift_a=1, shift_b=1,
            xn_a=1, xn_b=1, tp_a=TPC, tp_b=TPC, xT_a=TPC, xT_b=TPC, hx_done=1,
            abT_done=1, ab_tp=1, ab_done=1, s_mm=2, P_done=2, o_mm=3, h1_done=2, w_mm=1, W_done=1,
            lgT_mm=2, lgT_done=2, lg_tp=1, mx_done=1, sub_done=1, ex_done=1, sum_done=1, inv_done=1, prob_done=1,
            sel_done=1, gs_done=1, g8_done=1, gi_done=1, ghit_done=1, gm_done=1, pen_done=1, msk_done=1, e8_done=1,
            ei_done=1, ehit_done=1, picked_done=1, wf_done=1,
            pos_mm=1, row_done=1, carry_done=1, prod_done=1, slots_done=1,
            wT_tp=1, wT_done=1, up_mm=2, su_done=2, ac_done=2, y_mm=3, h_done=1)
        per_block = dict(b_tp=1, b_xT=1, b_wa=1, b_wd=1, b_cur=1, b_up=1, b_su=1, b_ac=1, b_down=1, b_y=1)
        names += list(per_chunk) + list(per_block)
        s = {n: sem(n) for n in names}

        def reach(name, m, k=None):
            per = {**per_chunk, **per_block}[name]
            return per * (m + AHEAD) + (per if k is None else k)

        def wait(eng, name, m, k=None):
            eng.wait_ge(s[name], reach(name, m, k))

        def wait_reg(eng, name, m, k=None):
            wait_alone(eng, s[name], reach(name, m, k))

        def wait_alone(eng, what, count):
            register = eng.to_reg(count)
            eng.wait_ge(s["weights"], NLOAD)
            eng.wait_ge(what, register)

        def pipeline(eng, first, second, third):
            def ahead(i, r, d):
                return i + (r + d) // 4, (r + d) % 4

            def step(i, r, last=4):
                if r + 2 < last:
                    first(*ahead(i, r, 2))
                if r + 1 < last:
                    second(*ahead(i, r, 1))
                if third:
                    third(i, r)
            first(0, 0)
            first(0, 1)
            second(0, 0)
            with eng.Fori(0, BLOCKS // 4 - 1) as i:
                for r in range(4):
                    step(i, r, last=8)
            for r in range(4):
                step(BLOCKS // 4 - 1, r)

        def resident(c):
            return h[:, bass.ds(c * (TPC * D), TPC * D)].rearrange("p (j d) -> p j d", d=D)

        ATT, SHA = (O[0], O[1], X[0]), (V[0], V[1], O[1])

        def tile_out(banks, j):
            return banks[j // 2][:, (j % 2) * D:(j % 2 + 1) * D]

        def _bc(ap, pos, n):
            shape = list(ap.shape)
            u = ap.unsqueeze(pos)
            shape.insert(pos, n)
            return u.to_broadcast(shape)

        loads = []
        SCAT = 16 * TPC * TOP
        CREDIT = SCAT // 2
        YSC = 16 * BT2

        block = es.enter_context(nc.Block())

        @block.sync
        def _(sp):
            def load(dst, src):
                sp.dma_start(dst, src).then_inc(s["weights"], 16)
                loads.append(1)

            def xload(i):
                sp.dma_start(xin[i % XBUF][:, :], a["x"].rearrange("b (u n) d -> (b u) (n d)", u=2)
                             [:, i * XC * D:(i + 1) * XC * D]).then_inc(s[f"x_loaded{i % XBUF}"], 16)

            row = lambda v, p: v.rearrange("(a n) -> a n", a=1).to_broadcast([p, v.shape[0]])
            for dst, src in ((gam, a["L0_tok_gamma"]), (tw, a["L0_tok_w"]), (bet, a["L0_tok_beta"]), (tb, a["L0_tok_b"])):
                sp.dma_start(dst[:, :], row(src, 128)).then_inc(s["firsts"], 16)
            for i in range(XBUF):
                xload(i)
            wav = wa.rearrange("p (e m c n) -> p m c e n", e=E, m=2, c=2)
            weights = [
                (ident[:, :], a["c_ident"]),
                (rowbase[:, :], a["c_rowbase"]),
                (wk[:, :, :], a["L0_attn_w_key"].rearrange("(c p) d -> p c d", p=128)),
                (wq[:, :, :], a["L0_attn_w_query"].rearrange("(c p) d -> p c d", p=128)),
                (wv[:, :, :], a["L0_attn_w_value"].rearrange("(c p) d -> p c d", p=128)),
                (woT[:, :, :], a["L0_attn_w_out"].rearrange("(c p) d -> p c d", p=128)),
                (wgt[:, :, :], a["L0_attn_w_gate"].rearrange("(c p) k -> p c k", p=HD)),
                (wdec[:, :], a["c_wdec"]),
                (causal[:, :], a["c_causal"]),
                (tdecay[:, :], a["c_tdecay"]),
                (iota[:, :], a["c_iota"]),
                (gw[:, :, :], a["L0_ffn_gate_w"].rearrange("(c p) e -> p c e", p=HD)),
                (gb[:, :], a["L0_ffn_gate_b"].rearrange("(e o) -> e o", o=1)),
                (rb[:, :], row(a["L0_ffn_bias"], 128)),
                (bd[0:E, :], a["L0_ffn_bd"]),
                (bd[E:E + 1, :], row(a["L0_ffn_sbd"], 1)),
                (tok[:, :], a["c_tok"]),
                (spare[:, :], a["c_spare"]),
                (base[:, :], a["c_base"]),
                (blki[:, :], a["c_blki"]),
                (earlier_in[:, :], a["c_earlier"]),
                (bu[:, 0:E], a["L0_ffn_bu"]),
                (bg[:, 0:E], a["L0_ffn_bg"]),
                (bu[:, E:E + 1], a["L0_ffn_sbu"].rearrange("(h o) -> h o", o=1)),
                (bg[:, E:E + 1], a["L0_ffn_sbg"].rearrange("(h o) -> h o", o=1)),
                (wd[:, :].rearrange("p (e d) -> p e d", e=E), a["L0_ffn_Wd"].rearrange("e h d -> h e d")),
                (swu[:, :, :], a["L0_ffn_sWu"].rearrange("(c p) n -> p c n", p=HD)),
                (swg[:, :, :], a["L0_ffn_sWg"].rearrange("(c p) n -> p c n", p=HD)),
                (swd[:, :], a["L0_ffn_sWd"]),
            ]
            for m, name in enumerate(("L0_ffn_Wu", "L0_ffn_Wg")):
                for c in range(2):
                    weights.append((wav[:, m, c, :, :], a[name][:, c * HD:(c + 1) * HD, :].rearrange("e p n -> p e n")))
            share = -(-len(weights) // (XCHUNKS - XBUF))
            for i in range(XBUF, XCHUNKS):
                sp.wait_ge(s["x_used"], i - XBUF + 1)
                xload(i)
                for dst, src in weights[(i - XBUF) * share:(i - XBUF + 1) * share]:
                    load(dst, src)
            sp.wait_ge(s["score_ready"], 1)
            sp.dma_start(score_d, xdot[:, :]).then_inc(s["score_out"], 16)
            sp.wait_ge(s["score_out"], 16)
            sp.dma_start(sc[:, 0, :], score_d.rearrange("(b u) n -> b (u n)", u=2)).then_inc(s["score_in"], 16)
            sp.wait_ge(s["odd_ready"], 1)
            sp.dma_start(row0_d, rowi[0:1, 0:STEPS]).then_inc(s["row0_out"], 16)
            sp.dma_start(gidx[64:128, 0:TILES], odd[:, :]).then_inc(s["odd_moved"], 16)
            sp.wait_ge(s["row0_out"], 16)
            sp.dma_start(kidx[:, :], row0_d.rearrange("a (p i) -> (a p) i", i=2)).then_inc(s["kidx_in"], 16)

            sp.wait_ge(s["zero_ready"], 1)
            zeros = zero[:, :].unsqueeze(1)
            with sp.Fori(0, CHUNKS) as c:
                for q in range(2):
                    sp.dma_start(yk[q][bass.ds(c * (TPC * 128), TPC * 128), :].rearrange("(p j) d -> p j d", j=TPC),
                                 zeros.to_broadcast([128, TPC, D])).then_inc(s["zeroed"], 16)
            for q in range(2):
                sp.dma_start(yk[q][TOK:TOK + BLK, :].rearrange("(p j) d -> p j d", j=BT2), zeros.to_broadcast([128, BT2, D]))\
                    .then_inc(s["zeroed"], 16)

            sp.wait_ge(s["table"], 1)
            sp.wait_ge(s["pad_ready"], 2)
            for e in range(E):
                end = sp.value_load(carryi[0:1, e:e + 1], min_val=0, max_val=E * ROOM)
                sp.dma_start(lists[bass.ds(end, BLK), :].rearrange("(t p) d -> p t d", p=128), pad[:, :, :])\
                    .then_inc(s["pads"], 16)
            sp.wait_ge(s["pads"], 16 * E)
            for u in range(2):
                sp.wait_ge(s[f"scat{u}"], SCAT * (CHUNKS // 2) + CREDIT)
            sp.wait_ge(s["tables_set"], 1)
            with sp.Fori(0, BLOCKS // 4) as i:
                for r in range(4):
                    b = 4 * i + r
                    first = sp.value_load(tabri[0:1, bass.ds(b, 1)], min_val=0, max_val=E * ROOM)
                    wait(sp, "b_tp", b - 4)
                    wait(sp, "b_cur", b - 4)
                    sp.dma_start(xb[r][:, :, :], lists[bass.ds(first, BLK), :].rearrange("(t p) d -> p t d", p=128))\
                        .then_inc(s[f"xl{r}"], 16)
            for r in range(4):
                sp.wait_ge(s[f"ysc{r}"], YSC * (BLOCKS // 4 + 1))
            sp.wait_ge(s["b_wa"], BLOCKS + AHEAD)

            def load_y(c, u):
                for q in range(2):
                    sp.dma_start(yin[u][:, q, :, :], yk[q][bass.ds(c * (TPC * 128), TPC * 128), :].rearrange("(j p) n -> p j n", p=128))\
                        .then_inc(s[f"yl{u}"], 16)

            outp = out.rearrange("b t d -> b (t d)")

            def store(c, u, last=False):
                for half in range(2):
                    src = fin[u][64 * half:64 * half + 64, :, :]
                    if last and half:
                        sp.dma_start(out[:, c * CS + 1:c * CS + 2 * TPC - 2:2, :], src[:, 0:TPC - 1, :])\
                            .then_inc(s[f"st{u}"], 16)
                    else:
                        dst = outp[:, bass.ds(c * (CS * D), CS * D)].rearrange("b (j w d) -> b j w d", w=2, d=D)[:, :, half, :] \
                            if not last else out[:, c * CS:c * CS + CS - 1:2, :]
                        sp.dma_start(dst, src).then_inc(s[f"st{u}"], 16)

            load_y(0, 0)
            load_y(1, 1)
            with sp.Fori(1, CHUNKS // 2) as it:
                for u in range(2):
                    sp.wait_ge(s[f"fin_done{u}"], it)
                    load_y(2 * it + u, u)
                    store(2 * it - 2 + u, u)
            for u in range(2):
                sp.wait_ge(s[f"fin_done{u}"], CHUNKS // 2)
                store(CHUNKS - 2 + u, u, last=(u == 1))
            for u in range(2):
                sp.wait_ge(s[f"st{u}"], 32 * (CHUNKS // 2))

        NLOAD = 16 * len(loads)

        @block.gpsimd
        def _(pool):
            for name, per in {**per_chunk, **per_block}.items():
                pool.sem_inc(s[name], AHEAD * per)
            nc.gpsimd.memset(mhalf[:, :], -0.5).then_inc(s["mhalf_ready"], 1)
            pool.wait_ge(s["mhalf_ready"], 1)
            for g, (lo, hi) in enumerate(GROUPS):
                pool.wait_ge(s["var_ready"], 2 * (g + 1))
                nc.gpsimd.tensor_tensor(xrs[:, lo:hi], xvar[:, lo:hi], mhalf[:, lo:hi], ALU.pow)\
                    .then_inc(s["rstd_ready"], 1)
            pool.wait_ge(s["weights"], NLOAD)
            xrows = a["x"].rearrange("b n d -> (b n) d")
            pool.wait_ge(s["kone_ready"], 1)
            for i in range(2):
                pool.indirect_dma_start(out=x0[:, i, :], out_offset=None, in_=xrows,
                                        in_offset=bass.IndirectOffsetOnAxis(ap=kone[:, i, :], axis=0))\
                                            .then_inc(s["x0_in"], 16)
            pool.wait_ge(s["x0_mv"], 1)
            nc.gpsimd.tensor_scalar(x0r[:, :], x0mv[:, :, 1], EPS, None, ALU.add).then_inc(s["x0_rstd0"], 1)
            pool.wait_ge(s["x0_rstd0"], 1)
            nc.gpsimd.tensor_tensor(x0r[:, :], x0r[:, :], mhalf[0:S0, 0:2], ALU.pow).then_inc(s["x0_rstd"], 1)

            def gather(u):
                for j in range(TPC):
                    pool.indirect_dma_start(out=hin[u][:, j, :], out_offset=None, in_=xrows,
                                            in_offset=bass.IndirectOffsetOnAxis(ap=gcur[u][:, j:j + 1], axis=0))\
                                                .then_inc(s[f"gath{u}"], 16)
            pool.wait_ge(s["pad_ready"], 2)
            for u in range(2):
                pool.dma_start(lists[E * ROOM + 128 * u:E * ROOM + 128 * u + 128, :], pad[:, u, :])\
                    .then_inc(s[f"scat{u}"], CREDIT)
            for r in range(4):
                lo = E * ROOM + BLK + 128 * r
                pool.dma_start(lists[lo:lo + 128, :], pad[:, 0, :]).then_inc(s[f"ysc{r}"], YSC)

            def scatter(c, u):
                wait_reg(pool, "xn_b", c)
                wait_reg(pool, "slots_done", c)
                for k in range(TOP):
                    for j in range(TPC):
                        pool.indirect_dma_start(out=lists, out_offset=bass.IndirectOffsetOnAxis(ap=slots[u][:, j, k:k + 1], axis=0),
                                                in_=rows[u][:, j, :], in_offset=None).then_inc(s[f"scat{u}"], 16)

            for c in range(3):
                wait(pool, "gcur_done", c)
                if c == 2:
                    wait(pool, "hx_done", 0)
                gather(c % 2)
            with pool.Fori(0, CHUNKS // 2 - 1) as i:
                for u in range(2):
                    c = 2 * i + u
                    wait_reg(pool, "hx_done", c + 1)
                    wait_reg(pool, "gcur_done", c + 3)
                    gather(1 - u)
                    scatter(c, u)
            for u in range(2):
                scatter(CHUNKS - 2 + u, u)
            pool.wait_ge(s["zeroed"], 16 * 2 * (CHUNKS + 1))
            with pool.Fori(0, BLOCKS // 4) as i:
                for r in range(4):
                    wait_reg(pool, "b_y", 4 * i + r)
                    wait_alone(pool, s[f"ysc{(r + 2) % 4}"], YSC * (i + (2 if r >= 2 else 1)))
                    for t in range(BT2):
                        pool.indirect_dma_start(out=yk[r % 2], out_offset=bass.IndirectOffsetOnAxis(ap=dcur[r][:, t:t + 1], axis=0),
                                                in_=yb[r][:, t, :], in_offset=None, compute_op=ALU.add)\
                                                    .then_inc(s[f"ysc{r}"], 16)

        @block.vector
        def _(dve):
            v = nc.vector
            dve.wait_ge(s["firsts"], 64)
            v.tensor_tensor(gamw[:, :], gam[:, :], tw[:, :], ALU.mult).then_inc(s["gamw_ready"], 1)
            v.scalar_tensor_tensor(out=xscr[:, :], in0=bet[:, :], scalar=1.0, in1=tw[:, :], op0=ALU.mult, op1=ALU.mult,
                                   accum_out=tcon[:, :]).then_inc(s["tcon_ready"], 1)
            v.memset(pad[:, :, 0:D + E], 0.0).then_inc(s["pad_ready"], 1)
            v.memset(zero[:, :], 0.0).then_inc(s["zero_ready"], 1)
            v.memset(W[:, :, :], 0.0).then_inc(s["fills"], 1)
            v.memset(picked[:, :], 0.0).then_inc(s["fills"], 1)
            v.memset(wT[:, :], 1.0).then_inc(s["fills"], 1)
            v.memset(ones[:, :], 1.0).then_inc(s["fills"], 1)
            v.memset(one1[:, :], 1.0).then_inc(s["fills"], 1)
            v.memset(epsc[:, :], EPS).then_inc(s["fills"], 1)
            v.memset(gidx[:, TILES:], 0).then_inc(s["fills"], 1)
            dve.wait_ge(s["tcon_ready"], 1)
            v.tensor_tensor(tcon2[:, :], tcon[:, :], tb[:, :], ALU.add).then_inc(s["tcon_ready"], 1)
            dve.wait_ge(s["gamw_ready"], 1)

            def own(t, r, q=None):
                t = t[:, r] if q is None else t[:, r, q]
                return t.rearrange("p (i k) -> p i k", k=XC)[:, :, XA:]

            def fold(g, r):
                acts = xvar[:, r].rearrange("p (i k) -> p i k", k=XC)[:, :, 0:XA]
                v.tensor_tensor(own(xtmp, r), own(xst, r, 1), own(xst, r, 4), ALU.subtract).then_inc(s["fold_ready"], 1)
                v.tensor_tensor(own(xvar, r), own(xst, r, 2), own(xst, r, 5), ALU.add).then_inc(s["fold_ready"], 1)
                v.tensor_scalar(acts, acts, 1.0 / D, EPS, ALU.mult, ALU.add).then_inc(s["var_ready"], 1)
                dve.wait_ge(s["fold_ready"], 4 * g + 2)
                v.tensor_tensor(own(xtmp, r), own(xtmp, r), own(xtmp, r), ALU.mult).then_inc(s["fold_ready"], 1)
                v.tensor_scalar(own(xvar, r), own(xvar, r), 1.0 / D, EPS, ALU.mult, ALU.add).then_inc(s["fold_ready"], 1)
                dve.wait_ge(s["fold_ready"], 4 * g + 4)
                v.scalar_tensor_tensor(out=own(xvar, r), in0=own(xtmp, r), scalar=0.25, in1=own(xvar, r), op0=ALU.mult,
                                       op1=ALU.add).then_inc(s["var_ready"], 1)

            def stats(i, lo, hi):
                for k in range(lo, hi):
                    last = v.bn_stats(xst[:, i * XC + k, :], xin[i % XBUF][:, k * D:(k + 1) * D])
                return last

            def half(i):
                r = slice(i * XC + XA, (i + 1) * XC)
                dve.wait_ge(s["stats_done"], i + 1)
                v.tensor_tensor(xtmp[:, r], xst[:, r, 1], xst[:, r, 4], ALU.add).then_inc(s["mean_half"], 1)

            dve.wait_ge(s["x_loaded0"], 16)
            stats(0, XA, XC).then_inc(s["stats_done"], 1)
            half(0)
            for i in range(XCHUNKS):
                if i + 1 < XCHUNKS:
                    dve.wait_ge(s[f"x_loaded{(i + 1) % XBUF}"], 16 * ((i + 1) // XBUF + 1))
                    stats(i + 1, XA, XA + 1)
                r = slice(i * XC + XA, (i + 1) * XC)
                dve.wait_ge(s["mean_half"], i + 1)
                v.tensor_scalar(xmean[:, r], xtmp[:, r], 0.5, None, ALU.mult).then_inc(s["mean_ready"], 1)
                if i + 1 < XCHUNKS:
                    stats(i + 1, XA + 1, XC).then_inc(s["stats_done"], 1)
                dve.wait_ge(s["mean_ready"], i + 1)
                dve.wait_ge(s["act_var"], i + 1)
                for k in range(XC):
                    xt = xin[i % XBUF][:, k * D:(k + 1) * D]
                    n = i * XC + k
                    last = v.scalar_tensor_tensor(out=xt, in0=xt, scalar=xmean[:, n:n + 1], in1=gamw[:, :],
                                                  op0=ALU.subtract, op1=ALU.mult, accum_out=xdot[:, n:n + 1])
                last.then_inc(s["x_used"], 1)
                if i + 1 < XCHUNKS:
                    half(i + 1)
                for g, (lo, hi) in enumerate(GROUPS):
                    if hi == (i + 1) * XC:
                        fold(g, slice(lo, hi))
            dve.wait_ge(s["rstd_ready"], len(GROUPS))
            dve.wait_ge(s["var_ready"], 2 * len(GROUPS))
            folds = 4 * len(GROUPS)
            v.tensor_tensor(xtmp[:, :], xrs[:, :], xrs[:, :], ALU.mult).then_inc(s["fold_ready"], 1)
            dve.wait_ge(s["fold_ready"], folds + 1)
            v.tensor_tensor(xtmp[:, :], xtmp[:, :], xvar[:, :], ALU.mult).then_inc(s["fold_ready"], 1)
            dve.wait_ge(s["fold_ready"], folds + 2)
            v.tensor_scalar(xtmp[:, :], xtmp[:, :], -0.5, 1.5, ALU.mult, ALU.add).then_inc(s["fold_ready"], 1)
            dve.wait_ge(s["x_used"], XCHUNKS)
            v.tensor_tensor(xdot[:, :], xdot[:, :], xrs[:, :], ALU.mult).then_inc(s["fold_ready"], 1)
            dve.wait_ge(s["fold_ready"], folds + 4)
            v.tensor_tensor(xdot[:, :], xdot[:, :], xtmp[:, :], ALU.mult).then_inc(s["fold_ready"], 1)
            dve.wait_ge(s["fold_ready"], folds + 5)
            dve.wait_ge(s["tcon_ready"], 2)
            v.tensor_scalar(xdot[:, :], xdot[:, :], tcon2[:, :], None, ALU.add).then_inc(s["score_ready"], 1)
            dve.wait_ge(s["weights"], NLOAD)
            v.tensor_copy(carry[:, :], base[:, :]).then_inc(s["fills"], 1)
            v.tensor_copy(pad[:, :, D + E], spare[:, :]).then_inc(s["pad_ready"], 1)
            v.tensor_copy(earlier[:, :], earlier_in[:, :]).then_inc(s["fills"], 1)
            dve.wait_ge(s["score_in"], 16)
            for r in range(ROUNDS):
                cur, nxt, m8 = sc[:, r % 2, :], sc[:, (r + 1) % 2, :], top[r % 2]
                if r:
                    dve.wait_ge(s["top8r"], r)
                if r >= 2:
                    dve.wait_ge(s["top8i"], r - 1)
                v.max(m8[:, :], cur).then_inc(s["top8"], 1)
                dve.wait_ge(s["top8"], r + 1)
                if r:
                    dve.wait_ge(s["top8i"], r)
                v.match_replace(nxt, m8[:, :], cur, -3.0e38).then_inc(s["top8r"], 1)
                v.max_index(idx[:, 8 * r:8 * r + 8], m8[:, :], cur).then_inc(s["top8i"], 1)
            dve.wait_ge(s["top8i"], ROUNDS)
            v.tensor_scalar(rowi[:, :], idx[:, :], rowbase[:, :], None, ALU.add).then_inc(s["rowi_ready"], 1)
            dve.wait_ge(s["rowi_ready"], 1)
            v.tensor_copy(gidx[0:64, 0:TILES], rowi[:, 0:STEPS:2])
            v.tensor_copy(odd[:, :], rowi[:, 1:STEPS:2]).then_inc(s["odd_ready"], 1)
            dve.wait_ge(s["kidx_in"], 16)
            v.tensor_copy(kone[:, :, 0], kidx[:, :]).then_inc(s["kone_ready"], 1)

            dve.wait_ge(s["x0_in"], 32)
            for i in range(2):
                last = v.bn_stats(x0st[:, i, :], x0[:, i, :])
            last.then_inc(s["x0_stats"], 1)
            dve.wait_ge(s["x0_stats"], 1)
            for i in range(2):
                last = v.bn_aggr(x0mv[:, i, :], x0st[:, i, :])
            last.then_inc(s["x0_mv"], 1)
            dve.wait_ge(s["x0_mv"], 1)
            dve.wait_ge(s["x0_rstd"], 1)
            for i in range(2):
                last = v.tensor_scalar(x0n[:, i, :], x0[:, i, :], x0mv[:, i, 0:1], x0r[:, i:i + 1], ALU.subtract, ALU.mult)
            last.then_inc(s["x0_norm"], 1)
            for hh in range(NH):
                dve.wait_ge(s["gate_ready"], hh + 1)
                v.tensor_tensor(gate[:, :], gate[:, :], wdec[:, :], ALU.mult).then_inc(s["bt_scaled"], 1)
                dve.wait_ge(s["bt_scaled"], 3 * hh + 1)
                dve.wait_ge(s["at_mm"], 4 * hh + 4)
                for c in range(2):
                    dst = BT[:, c, :].rearrange("p (s k) -> p s k", k=NH)[:, :, hh]
                    v.tensor_tensor(dst, (V[c])[0:HD, 0:STEPS], gate[:, :], ALU.mult).then_inc(s["bt_scaled"], 1)

            def norm(hc, n, c):
                for j in range(TPC):
                    last = v.bn_stats(st[:, j, :], hc[:, j, :])
                last.then_inc(s["st_" + n], 1)
                wait_reg(dve, "st_" + n, c)
                for j in range(TPC):
                    last = v.bn_aggr(mv[n][:, j, :], st[:, j, :])
                last.then_inc(s["mv_" + n], 1)
                wait(dve, "sd_" + n, c)
                wait(dve, "hx_done" if n == "a" else "xn_b", c - 1)
                v.reciprocal(rs[n][:, :], sd[n][:, :]).then_inc(s["rs_" + n], 1)
                wait(dve, "rs_" + n, c)
                if n == "a":
                    v.tensor_scalar(rs1[:, :], rs[n][:, :], 1.0, None, ALU.add)
                v.scalar_tensor_tensor(out=shift[n][:, :], in0=mv[n][:, :, 0], scalar=-1.0, in1=rs[n][:, :], op0=ALU.mult, op1=ALU.mult)\
                    .then_inc(s["shift_" + n], 1)

            def enter(i, u):
                c = 2 * i + u
                wait_alone(dve, s[f"gath{u}"], 16 * TPC * (i + 1))
                norm(hin[u], "a", c)

            def mask(c):
                for k in range(2):
                    wait(dve, "s_mm", c, k + 1)
                    wait(dve, "w_mm", c - 1)
                    dst = P[:, k * HT:(k + 1) * HT].rearrange("p (t b) -> p t b", b=64)
                    v.tensor_tensor(dst, U[k][0:R, 0:HT].rearrange("p (t b) -> p t b", b=64),
                                    _bc(causal[:, k * TPC:(k + 1) * TPC], 2, 64), ALU.mult).then_inc(s["P_done"], 1)

            def attend(c, tiles):
                wait(dve, "hx_done", c)
                hc = resident(c)
                for j in tiles:
                    wait(dve, "o_mm", c, j // 2 + 1)
                    last = v.scalar_tensor_tensor(out=hc[:, j, :], in0=tile_out(ATT, j), scalar=tdecay[:, j:j + 1],
                                                  in1=hc[:, j, :], op0=ALU.mult, op1=ALU.add)
                last.then_inc(s["h1_done"], 1)

            def advance(c):
                wait(dve, "h1_done", c)
                wait(dve, "w_mm", c)
                wait(dve, "W_done", c - 1)
                Wf = W[:, :, :].rearrange("p c d -> p (c d)")
                v.scalar_tensor_tensor(out=Wf, in0=Wf, scalar=DECAY ** CS, in1=O[1][0:HD, 0:2 * D],
                                       op0=ALU.mult, op1=ALU.add).then_inc(s["W_done"], 1)

            pk = picked[:, 0:TPC * E].rearrange("p (j e) -> p j e", e=E)

            def choose(i, u, meanwhile):
                c = 2 * i + u
                logits = X[1][:, HT:HT + TPC * E].rearrange("p (j e) -> p j e", e=E)
                wait(dve, "lg_tp", c)
                v.tensor_reduce(mx[:, :], logits, AX.X, ALU.max).then_inc(s["mx_done"], 1)
                wait(dve, "mx_done", c)
                v.tensor_tensor(lg[:, :, :], logits, _bc(mx[:, :], 2, E), ALU.subtract).then_inc(s["sub_done"], 1)
                meanwhile()
                wait(dve, "ex_done", c)
                v.tensor_reduce(rsum[:, :], ex[:, :, :], AX.X, ALU.add).then_inc(s["sum_done"], 1)
                wait(dve, "sum_done", c)
                v.reciprocal(rinv[:, :], rsum[:, :]).then_inc(s["inv_done"], 1)
                wait(dve, "inv_done", c)
                v.tensor_tensor(prob[:, :, :], ex[:, :, :], _bc(rinv[:, :], 2, E), ALU.mult)\
                    .then_inc(s["prob_done"], 1)
                wait(dve, "prob_done", c)
                v.tensor_tensor(sel[:, :, :], prob[:, :, :], _bc(rb[:, :], 1, TPC), ALU.add)\
                    .then_inc(s["sel_done"], 1)
                wait(dve, "sel_done", c)
                pair = sel[:, :, :].rearrange("p j (g u) -> p j g u", u=2)
                v.tensor_tensor(gs[:, :, :], pair[:, :, :, 0], pair[:, :, :, 1], ALU.add).then_inc(s["gs_done"], 1)
                wait_reg(dve, "gs_done", c)
                for j in range(TPC):
                    last = v.max(g8[:, j, :], gs[:, j, :])
                last.then_inc(s["g8_done"], 1)
                wait_reg(dve, "g8_done", c)
                for j in range(TPC):
                    last = v.max_index(gi[:, j, :], g8[:, j, :], gs[:, j, :])
                last.then_inc(s["gi_done"], 1)
                wait(dve, "gi_done", c)
                hitg = hit[:, :, :].rearrange("p j (k g) -> p k j g", k=TOP)
                for k in range(TOP):
                    last = v.tensor_tensor(hitg[:, k, :, 0:G], _bc(gi[:, :, k], 2, G), _bc(iota[:, 0:G], 1, TPC), ALU.is_equal)
                last.then_inc(s["ghit_done"], 1)
                wait(dve, "ghit_done", c)
                v.tensor_reduce(gm[:, :, :], hit[:, :, :].rearrange("p j (k g) -> p j g k", k=TOP)[:, :, 0:G, :], AX.X, ALU.add)\
                    .then_inc(s["gm_done"], 1)
                wait(dve, "gm_done", c)
                v.tensor_scalar(gm[:, :, :], gm[:, :, :], -1.0, 1.0e30, ALU.add, ALU.mult).then_inc(s["pen_done"], 1)
                wait(dve, "pen_done", c)
                for w in range(2):
                    last = v.tensor_tensor(pair[:, :, :, w], pair[:, :, :, w], gm[:, :, :], ALU.add)
                last.then_inc(s["msk_done"], 1)
                wait_reg(dve, "msk_done", c)
                for j in range(TPC):
                    last = v.max(g8[:, j, :], sel[:, j, :])
                last.then_inc(s["e8_done"], 1)
                wait_reg(dve, "e8_done", c)
                for j in range(TPC):
                    last = v.max_index(gi[:, j, :], g8[:, j, :], sel[:, j, :])
                last.then_inc(s["ei_done"], 1)
                wait(dve, "ei_done", c)
                hit4 = hit[:, :, :].rearrange("p j (e k) -> p j e k", k=TOP)
                for k in range(TOP):
                    last = v.tensor_tensor(hit4[:, :, :, k], _bc(gi[:, :, k], 2, E), _bc(iota[:, :], 1, TPC), ALU.is_equal)
                last.then_inc(s["ehit_done"], 1)
                wait(dve, "ehit_done", c)
                wait(dve, "pos_mm", c - 1)
                v.tensor_reduce(pk, hit4, AX.X, ALU.max).then_inc(s["picked_done"], 1)

            def place(i, u):
                c = 2 * i + u
                wait(dve, "picked_done", c)
                dve.wait_ge(s[f"scat{u}"], SCAT * i + CREDIT)
                v.scalar_tensor_tensor(out=rows[u][:, :, D:D + E], in0=pk, scalar=SCALE,
                                       in1=prob[:, :, :], op0=ALU.mult, op1=ALU.mult).then_inc(s["wf_done"], 1)
                flat = prod[:, :, :].rearrange("p j (e k) -> p (j e) k", k=TOP)
                hflat = hit[:, :, :].rearrange("p j (e k) -> p (j e) k", k=TOP)
                wait(dve, "slots_done", c - 1)
                v.tensor_copy(rows[u][:, :, D + E], tok[:, bass.ds(c * TPC, TPC)])
                wait(dve, "pos_mm", c)
                wait(dve, "carry_done", c - 1)
                v.tensor_tensor(slotrow[:, :, :], V[1][:, HT:HT + TPC * E].rearrange("p (j e) -> p j e", e=E),
                                _bc(carry[:, :], 1, TPC), ALU.add).then_inc(s["row_done"], 1)
                wait(dve, "row_done", c)
                v.tensor_tensor(carry[:, :], V[1][:, HT + TPC * E:HT + (TPC + 1) * E], carry[:, :], ALU.add)\
                    .then_inc(s["carry_done"], 1)
                v.tensor_tensor(flat, hflat, _bc(slotrow[:, :, :].rearrange("p j e -> p (j e)"), 2, TOP), ALU.mult)\
                    .then_inc(s["prod_done"], 1)
                wait(dve, "prod_done", c)
                with nc.allow_low_precision(reason="row numbers: whole, below 2 ** 24"):
                    v.tensor_reduce(slots[u][:, :, :], prod[:, :, :].rearrange("p j (e k) -> p j k e", k=TOP), AX.X, ALU.add)\
                        .then_inc(s["slots_done"], 1)

            def shared_product(c):
                for k in range(2):
                    wait(dve, "su_done", c, k + 1)
                    v.scalar_tensor_tensor(out=ac[:, k, :], in0=V[k][:, 0:HT], scalar=bg[:, E:E + 1], in1=su[:, k, :],
                                           op0=ALU.add, op1=ALU.mult).then_inc(s["ac_done"], 1)

            def shared_out(c):
                hc = resident(c)
                for g in range(3):
                    wait(dve, "y_mm", c, g + 1)
                    part = hc[:, 2 * g:min(2 * g + 2, TPC), :].rearrange("p j d -> p (j d)")
                    last = v.tensor_tensor(part, SHA[g][:, 0:part.shape[1]], part, ALU.add)
                last.then_inc(s["h_done"], 1)

            def turn(i, u, enters=True, attends=True):
                c = 2 * i + u
                if enters:
                    enter(i + 1, u)
                if attends:
                    attend(c + 1, range(4))
                choose(i, u, (lambda: attend(c + 1, (4,))) if attends else (lambda: None))
                place(i, u)
                if not attends:
                    dve.wait_ge(s["carry_done"], CHUNKS + AHEAD)
                    v.tensor_copy(carryi[:, :], carry[0:1, :]).then_inc(s["table"], 1)
                shared_product(c)
                if attends:
                    norm(resident(c + 1), "b", c + 1)
                    advance(c + 1)
                if enters:
                    mask(c + 2)
                shared_out(c)

            dve.wait_ge(s["fills"], 9)
            enter(0, 0)
            mask(0)
            enter(0, 1)
            attend(0, range(4))
            attend(0, (4,))
            advance(0)
            mask(1)
            norm(resident(0), "b", 0)
            with dve.Fori(0, CHUNKS // 2 - 1) as i:
                turn(i, 0)
                turn(i, 1)
            turn(CHUNKS // 2 - 1, 0, enters=False)
            turn(CHUNKS // 2 - 1, 1, enters=False, attends=False)

            step = [0]

            def after(ins):
                step[0] += 1
                ins.then_inc(s["tail_mult"], 1)
                dve.wait_ge(s["tail_mult"], step[0])
            after(v.scalar_tensor_tensor(out=cnt[:, :], in0=carry[0:1, :], scalar=float(BLK - 1), in1=base[0:1, :], op0=ALU.add,
                                         op1=ALU.subtract))
            after(v.tensor_copy(cnti[:, :], cnt[:, :]))
            after(v.tensor_scalar(cnti[:, :], cnti[:, :], BLK.bit_length() - 1, None, ALU.logical_shift_right))
            after(v.tensor_copy(nblk[:, :], cnti[:, :]))
            after(v.tensor_tensor_scan(cum[:, :], one1[:, :], nblk[:, :], 0.0, ALU.mult, ALU.add))
            after(v.tensor_scalar(skipd[:, :], nblk[:, :], -float(BLK), float(ROOM), ALU.mult, ALU.add))
            past = big.rearrange("p (i e) -> p i e", e=E)
            after(v.tensor_tensor(past, _bc(cum[:, :], 1, BLOCKS), _bc(blki[:, :], 2, E), ALU.is_le))
            after(v.tensor_reduce(tabe[:, :], past, AX.X, ALU.add))
            after(v.tensor_tensor(past, past, _bc(skipd[:, :], 1, BLOCKS), ALU.mult))
            after(v.tensor_reduce(tabr[:, :], past, AX.X, ALU.add))
            after(v.scalar_tensor_tensor(out=tabr[:, :], in0=blki[:, :], scalar=float(BLK), in1=tabr[:, :], op0=ALU.mult, op1=ALU.add))
            after(v.tensor_scalar(tabri[:, :], tabr[:, :], float(E * ROOM), None, ALU.min))
            after(v.tensor_scalar(tabei[:, :], tabe[:, :], float(E - 1), None, ALU.min))
            v.engine_nop().then_inc(s["tables_set"], 1)

            def prepare(i, r):
                b = 4 * i + r
                e = dve.value_load(tabei[0:1, bass.ds(b, 1)], min_val=0, max_val=E - 1)
                wait(dve, "b_up", b - 2)
                v.tensor_copy(wac[r % 2][:, :], wa[:, bass.ds(e * WAW, WAW)]).then_inc(s["b_wa"], 1)
                dve.wait_ge(s[f"xl{r}"], 16 * (i + 1))
                wait(dve, "b_y", b - 4)
                v.tensor_copy(dest[r][:, :], xb[r][:, :, D + E])
                v.tensor_copy(wcur[r][:, :], xb[r][:, :, bass.ds(D + e, 1)].rearrange("p t o -> p (t o)"))
                v.tensor_copy(bcur[r][:, 0:1], bu[:, bass.ds(e, 1)])
                v.tensor_copy(bcur[r][:, 1:2], bg[:, bass.ds(e, 1)]).then_inc(s["b_cur"], 1)

            def product(i, r):
                b = 4 * i + r
                wait(dve, "b_su", b)
                wait(dve, "b_cur", b)
                wait(dve, "b_down", b - 2)
                v.scalar_tensor_tensor(out=acb[r % 2][:, :], in0=U[r % 2][:, BLK:2 * BLK], scalar=bcur[r][:, 1:2],
                                       in1=sub[r % 2][:, :], op0=ALU.add, op1=ALU.mult).then_inc(s["b_ac"], 1)

            def scaled(i, r):
                b = 4 * i + r
                dve.wait_ge(s[f"ysc{r}"], YSC * (i + 1))
                v.tensor_copy(dcur[r][:, :], dest[r][:, :])
                wait(dve, "b_down", b)
                for t in range(BT2):
                    last = v.tensor_scalar(yb[r][:, t, :], O[r % 2][:, t * D:(t + 1) * D], wcur[r][:, t:t + 1], None, ALU.mult)
                last.then_inc(s["b_y"], 1)

            pipeline(dve, prepare, product, scaled)

            def finish(c, u, it, first):
                if not first:
                    dve.wait_ge(s[f"st{u}"], 32 * it - 32)
                dve.wait_ge(s[f"yl{u}"], 32 * it)
                v.tensor_tensor(fin[u][:, :, :], yin[u][:, 0, :, :], h[:, bass.ds(c * (TPC * D), TPC * D)].rearrange("p (j d) -> p j d", d=D),
                                ALU.add).then_inc(s[f"pair_done{u}"], 1)
                dve.wait_ge(s[f"pair_done{u}"], it)
                v.tensor_tensor(fin[u][:, :, :], fin[u][:, :, :], yin[u][:, 1, :, :], ALU.add)\
                    .then_inc(s[f"fin_done{u}"], 1)
            dve.wait_ge(s["gath0"], 16 * TPC * (CHUNKS // 2 + 1))
            for u in range(2):
                finish(u, u, 1, True)
            with dve.Fori(2, CHUNKS // 2 + 1) as it:
                for u in range(2):
                    finish(2 * it - 2 + u, u, it, False)

        @block.scalar
        def _(act):
            ac_ = nc.scalar
            for i in range(XCHUNKS):
                act.wait_ge(s[f"x_loaded{i % XBUF}"], 16 * (i // XBUF + 1))
                for k in range(XA):
                    n = i * XC + k
                    last = ac_.activation(xpass[0][:, k * D:(k + 1) * D], xin[i % XBUF][:, k * D:(k + 1) * D], ACT.Copy, scale=1.0 / D,
                                          accum_out=xmean[:, n:n + 1])
                last.then_inc(s["act_mean"], 1)
                act.wait_ge(s["act_mean"], i + 1)
                if i:
                    act.wait_ge(s["act_var"], i)
                for k in range(XA):
                    n = i * XC + k
                    last = ac_.activation(xpass[1][:, k * D:(k + 1) * D], xin[i % XBUF][:, k * D:(k + 1) * D], ACT.Square, scale=-1.0,
                                          bias=xmean[:, n:n + 1], accum_out=xvar[:, n:n + 1])
                last.then_inc(s["act_var"], 1)
            act.wait_ge(s["weights"], NLOAD)
            for m, dst in enumerate((Gm, Hm)):
                for hh in range(NH):
                    n = m * NH + hh
                    act.wait_ge(s["gh_mm"], n + 1)
                    ac_.activation(dst[:, :, hh, :], O[n % 2][0:HD, 0:2 * D].rearrange("p (c d) -> p c d", c=2), ACT.Copy)\
                        .then_inc(s["gh_copied"], 1)
            for c in range(2):
                last = ac_.activation(wgtb[:, c, :, :], _bc(wgt[:, c, :], 2, HD), ACT.Copy)
            last.then_inc(s["wgtb_ready"], 1)
            act.wait_ge(s["odd_moved"], 16)
            act.wait_ge(s["kone_ready"], 1)
            for u in range(2):
                ac_.activation(gcur[u][:, :], gidx[:, u * TPC:(u + 1) * TPC], ACT.Copy).then_inc(s["gcur_done"], 1)
            for i in range(2):
                act.wait_ge(s["x0_tp"], i + 1)
                ac_.activation(x0T[:, :, i:STEPS:2], X[i][0:HD, 0:256].rearrange("p (c t) -> p c t", c=2)[:, :, 0:S0], ACT.Copy)\
                    .then_inc(s["x0_copied"], 1)
            for hh in range(NH):
                act.wait_ge(s["gate_mm"], hh + 1)
                if hh:
                    act.wait_ge(s["bt_scaled"], 3 * hh)
                ac_.activation(gate[:, :], O[0][0:HD, 0:STEPS], ACT.Sigmoid).then_inc(s["gate_ready"], 1)
                for c in range(2):
                    act.wait_ge(s["at_mm"], 4 * hh + c + 1)
                    dst = AT[:, c, :].rearrange("p (s k) -> p s k", k=NH)[:, :, hh]
                    ac_.activation(dst, U[c][0:HD, 0:STEPS], ACT.Copy).then_inc(s["at_copied"], 1)
            act.wait_ge(s["bt_scaled"], 3 * NH)
            act.wait_ge(s["at_copied"], 2 * NH)

            def spread(n, c):
                wait(act, "mv_" + n, c)
                ac_.activation(sd[n][:, :], mv[n][:, :, 1], ACT.Sqrt, bias=epsc[:, :]).then_inc(s["sd_" + n], 1)

            def apply(dst, src, scale, n):
                for j in range(TPC):
                    last = ac_.activation(dst[:, j, 0:D], src[:, j, :], ACT.Identity, scale=scale[:, j:j + 1], bias=shift[n][:, j:j + 1])
                return last

            def normed(i, u):
                c = 2 * i + u
                wait(act, "shift_a", c)
                wait(act, "tp_a", c - 1)
                apply(xn, hin[u], rs["a"], "a").then_inc(s["xn_a"], 1)

            def residual(i, u):
                c = 2 * i + u
                apply(resident(c), hin[u], rs1, "a").then_inc(s["hx_done"], 1)

            def experts_rows(i, u):
                c = 2 * i + u
                scaled, scattered = act.to_reg(reach("shift_b", c)), act.to_reg(SCAT * i + CREDIT)
                act.wait_ge(s["weights"], NLOAD)
                act.wait_ge(s["shift_b"], scaled)
                act.wait_ge(s[f"scat{u}"], scattered)
                apply(rows[u], resident(c), rs["b"], "b").then_inc(s["xn_b"], 1)

            def evac_T(n, c, beside=lambda j: None):
                for j in range(TPC):
                    wait(act, "tp_" + n, c, j + 1)
                    ac_.activation(xnT[n][:, :, j * 128:(j + 1) * 128], X[j % 2][0:HD, 0:256].rearrange("p (c t) -> p c t", c=2),
                                   ACT.Copy).then_inc(s["xT_" + n], 1)
                    beside(j)

            def keys_in(c):
                wait(act, "ab_tp", c - 1)
                wait(act, "s_mm", c - 1)
                ac_.activation(ATc[:, :, :], AT[:, :, bass.ds(c * R, R)], ACT.Copy)
                ac_.activation(BTc[:, :, :], BT[:, :, bass.ds(c * R, R)], ACT.Copy).then_inc(s["abT_done"], 1)

            def indices(i, u):
                act.wait_ge(s[f"gath{u}"], 16 * TPC * i)
                ac_.activation(gcur[u][:, :], gidx[:, bass.ds((2 * i + u) * TPC, TPC)], ACT.Copy)\
                    .then_inc(s["gcur_done"], 1)

            def keys_out(c):
                wait(act, "ab_tp", c)
                wait(act, "w_mm", c - 1)
                ac_.activation(Ac[:, :], O[0][0:R, 0:D], ACT.Copy, scale=DECAY ** CS)
                ac_.activation(Bc[:, :], O[0][0:R, D:2 * D], ACT.Copy).then_inc(s["ab_done"], 1)

            def logits_out(c):
                for k in range(2):
                    wait(act, "lgT_mm", c, k + 1)
                    wait(act, "lg_tp", c - 1)
                    ac_.activation(lgT[:, k * HT:(k + 1) * HT], X[k][0:E, 0:HT], ACT.Identity, bias=gb[:, :])\
                        .then_inc(s["lgT_done"], 1)

            def softmax(c):
                wait(act, "sub_done", c)
                ac_.activation(ex[:, :, :], lg[:, :, :], ACT.Exp).then_inc(s["ex_done"], 1)

            def shared(c, k):
                wait(act, "up_mm", c, k + 1)
                wait(act, "ac_done", c - 1)
                ac_.activation(su[:, k, :], U[k][:, 0:HT], ACT.Silu, bias=bu[:, E:E + 1]).then_inc(s["su_done"], 1)

            def weights_out(c):
                wait(act, "wT_tp", c)
                wait(act, "y_mm", c - 1)
                ac_.activation(wT[0:E, 0:384], X[0][0:E, 0:384], ACT.Copy)
                ac_.activation(wT[0:E, 384:CT], X[1][0:E, 0:CT - 384], ACT.Copy).then_inc(s["wT_done"], 1)

            def turn(i, u, enters=True, attends=True):
                c = 2 * i + u
                if enters:
                    indices(i + 1 + u, 1 - u)
                wait(act, "up_mm", c - 1)
                evac_T("b", c, lambda j: spread("a", c + 2) if enters and j == 2 else None)
                logits_out(c)
                if enters:
                    normed(i + 1, u)
                softmax(c)
                if enters:
                    keys_in(c + 2)
                    residual(i + 1, u)
                shared(c, 0)
                if enters:
                    keys_out(c + 2)
                    wait(act, "o_mm", c + 1)
                    evac_T("a", c + 2)
                shared(c, 1)
                weights_out(c)
                if attends:
                    spread("b", c + 1)
                if attends:
                    experts_rows(i + u, 1 - u)

            keys_in(0)
            spread("a", 0)
            normed(0, 0)
            residual(0, 0)
            keys_out(0)
            evac_T("a", 0)
            indices(1, 0)
            keys_in(1)
            spread("a", 1)
            normed(0, 1)
            residual(0, 1)
            keys_out(1)
            wait(act, "o_mm", 0)
            evac_T("a", 1)
            spread("b", 0)
            experts_rows(0, 0)
            with act.Fori(0, CHUNKS // 2 - 1) as i:
                turn(i, 0)
                turn(i, 1)
            turn(CHUNKS // 2 - 1, 0, enters=False)
            turn(CHUNKS // 2 - 1, 1, enters=False, attends=False)

            act.wait_ge(s["tables_set"], 1)

            def prepare(i, r):
                b = 4 * i + r
                e = act.value_load(tabei[0:1, bass.ds(b, 1)], min_val=0, max_val=E - 1)
                wait(act, "b_tp", b)
                wait(act, "b_up", b - 2)
                ac_.activation(xT[r % 2][:, :, :].rearrange("p k (t n) -> p t k n", n=128),
                               X[r % 2][0:HD, :].rearrange("p (t k n) -> p t k n", t=2, k=2), ACT.Copy)\
                                   .then_inc(s["b_xT"], 1)
                wait(act, "b_down", b - 2)
                ac_.activation(wdc[r % 2][:, :], wd[:, bass.ds(e * D, D)], ACT.Copy).then_inc(s["b_wd"], 1)

            def silu(i, r):
                b = 4 * i + r
                wait(act, "b_cur", b)
                wait(act, "b_up", b)
                wait(act, "b_ac", b - 2)
                ac_.activation(sub[r % 2][:, :], U[r % 2][:, 0:BLK], ACT.Silu, bias=bcur[r][:, 0:1])\
                    .then_inc(s["b_su"], 1)

            pipeline(act, prepare, silu, None)

        @block.tensor
        def _(pe):
            mm = nc.tensor.matmul
            pe.wait_ge(s["weights"], NLOAD)
            for m, (left, right) in enumerate(((wk, wq), (wv, woT))):
                for hh in range(NH):
                    n = m * NH + hh
                    if n >= 2:
                        pe.wait_ge(s["gh_copied"], n - 1)
                    r = slice(64 * (hh % 2), 64 * (hh % 2) + 64)
                    for c in range(2):
                        last = mm(O[n % 2][0:HD, c * D:(c + 1) * D], left[r, hh // 2, c * HD:(c + 1) * HD], right[r, hh // 2, :],
                                  start=True, stop=True)
                    last.then_inc(s["gh_mm"], 1)
            pe.wait_ge(s["gh_copied"], 2 * NH)
            pe.wait_ge(s["wgtb_ready"], 1)
            pe.wait_ge(s["x0_norm"], 1)
            for i in range(2):
                for c in range(2):
                    last = nc.tensor.transpose(X[i][0:HD, c * 128:c * 128 + S0], x0n[:, i, c * HD:(c + 1) * HD], ident[0:S0, 0:S0])
                last.then_inc(s["x0_tp"], 1)
            pe.wait_ge(s["x0_copied"], 2)
            for hh in range(NH):
                if hh:
                    pe.wait_ge(s["gate_ready"], hh)
                for k in range(2):
                    last = mm(O[0][0:HD, 0:STEPS], wgtb[:, k, hh, :], x0T[:, k, :], start=(k == 0), stop=(k == 1))
                last.then_inc(s["gate_mm"], 1)
                for m, (w, bank) in enumerate(((Gm, U), (Hm, V))):
                    if hh:
                        if m == 0:
                            pe.wait_ge(s["at_copied"], 2 * hh)
                        else:
                            pe.wait_ge(s["bt_scaled"], 3 * hh)
                    for c in range(2):
                        for k in range(2):
                            last = mm(bank[c][0:HD, 0:STEPS], w[:, k, hh, c * HD:(c + 1) * HD], x0T[:, k, :], start=(k == 0), stop=(k == 1))
                        last.then_inc(s["at_mm"], 1)
            pe.wait_ge(s["at_copied"], 2 * NH)
            pe.wait_ge(s["bt_scaled"], 3 * NH)
            pe.wait_ge(s["fills"], 9)

            def keys(c):
                wait(pe, "abT_done", c)
                wait(pe, "h1_done", c - 1)
                for m, src in enumerate((ATc, BTc)):
                    for k in range(2):
                        last = nc.tensor.transpose(O[0][0:R, m * D + k * HD:m * D + (k + 1) * HD], src[:, k, :], ident[0:HD, 0:HD])
                last.then_inc(s["ab_tp"], 1)

            def transposes(src, n, c, beside=lambda j: None):
                wait(pe, "xn_" + n, c)
                for j in range(TPC):
                    if j >= 2:
                        wait(pe, "xT_" + n, c, j - 1)
                    elif n == "a":
                        wait(pe, "h1_done", c - 1)
                        wait(pe, "sub_done", c - 2)
                    for k in range(2):
                        last = nc.tensor.transpose(X[j % 2][0:HD, k * 128:(k + 1) * 128], src[:, j, k * HD:(k + 1) * HD], ident[:, :])
                    last.then_inc(s["tp_" + n], 1)
                    beside(j)

            def scores(c):
                wait(pe, "su_done", c - 2)
                for g in range(2):
                    wait(pe, "xT_a", c, 3 if g == 0 else TPC)
                    for k in range(2):
                        last = mm(U[g][0:R, 0:HT], ATc[:, k, :], xnT["a"][:, k, g * HT:(g + 1) * HT], start=(k == 0), stop=(k == 1))
                    last.then_inc(s["s_mm"], 1)

            def outputs(c, tiles):
                wait(pe, "ab_done", c)
                wait(pe, "W_done", c - 1)
                for j in tiles:
                    if j == 2:
                        wait(pe, "h_done", c - 2)
                    wait(pe, "P_done", c, 1 if 128 * (j + 1) <= HT else 2)
                    t = slice(j * 128, (j + 1) * 128)
                    for k in range(2):
                        mm(tile_out(ATT, j), xnT["a"][:, k, t], W[:, k, :], start=(k == 0), stop=False)
                    last = mm(tile_out(ATT, j), P[:, t], Bc[:, :], start=False, stop=True)
                    if j % 2 or j == TPC - 1:
                        last.then_inc(s["o_mm"], 1)

            def state(c):
                wait(pe, "h1_done", c)
                for k in range(2):
                    last = mm(O[1][0:HD, k * D:(k + 1) * D], Ac[:, k * HD:(k + 1) * HD], Bc[:, :], start=True, stop=True)
                last.then_inc(s["w_mm"], 1)

            def logits(c):
                wait(pe, "xT_b", c)
                for k in range(2):
                    for r in range(2):
                        last = mm(X[k][0:E, 0:HT], gw[:, r, :], xnT["b"][:, r, k * HT:(k + 1) * HT], start=(r == 0), stop=(r == 1))
                    last.then_inc(s["lgT_mm"], 1)

            def logits_back(c):
                wait_reg(pe, "lgT_done", c)
                for j in range(TPC):
                    last = nc.tensor.transpose(X[1][:, HT + j * E:HT + (j + 1) * E], lgT[:, j * 128:(j + 1) * 128], ident[0:E, 0:E])
                last.then_inc(s["lg_tp"], 1)

            def shared(c, attends):
                wait(pe, "ac_done", c - 1)
                wait(pe, "h_done", c - 1)
                wait(pe, "P_done", c + 1 if attends else c)
                wait(pe, "carry_done", c - 1)
                shared_half(c, 0)

            def shared_half(c, k):
                for part in range(4):
                    shared_part(c, k, part)

            def shared_part(c, k, part):
                bank, w = ((U, swu), (V, swg))[part // 2]
                r = part % 2
                last = mm(bank[k][:, 0:HT], w[:, r, :], xnT["b"][:, r, k * HT:(k + 1) * HT], start=(r == 0), stop=(r == 1))
                if part == 3:
                    last.then_inc(s["up_mm"], 1)

            def places(c):
                wait(pe, "picked_done", c)
                mm(V[1][:, HT:HT + (TPC + 1) * E], earlier[:, :], picked[:, :], start=True, stop=False)
                for i in range(TPC):
                    n = TPC - i
                    last = mm(V[1][:, HT + (i + 1) * E:HT + (TPC + 1) * E].rearrange("p (n e) -> p n e", e=E), ones[:, :],
                              _bc(picked[:, i * E:(i + 1) * E], 1, n), start=False, stop=(i == TPC - 1))
                last.then_inc(s["pos_mm"], 1)

            def weights(c, u, enters):
                wait(pe, "wf_done", c)
                if enters:
                    wait(pe, "xT_a", c + 2)
                for j in range(TPC):
                    last = nc.tensor.transpose(X[j // 3][0:E, (j % 3) * 128:(j % 3 + 1) * 128], rows[u][:, j, D:D + E], ident[:, :])
                last.then_inc(s["wT_tp"], 1)

            def down(c, attends):
                wait(pe, "wT_done", c)
                wait(pe, "ac_done", c)
                wait(pe, "carry_done", c)
                acf = ac[:, :, :].rearrange("p k n -> p (k n)")
                for j in range(TPC):
                    if attends and j == TPC - 1:
                        wait(pe, "W_done", c + 1)
                    mm(tile_out(SHA, j), acf[:, j * 128:(j + 1) * 128], swd[:, :], start=True, stop=False)
                    last = mm(tile_out(SHA, j), wT[:, j * 128:(j + 1) * 128], bd[:, :], start=False, stop=True)
                    if j % 2 or j == TPC - 1:
                        last.then_inc(s["y_mm"], 1)

            def turn(i, u, enters=True, attends=True):
                c = 2 * i + u
                if attends:
                    outputs(c + 1, (0,))
                transposes(rows[u], "b", c, lambda j: outputs(c + 1, (1,)) if attends and j == 1 else None)
                logits(c)
                if attends:
                    outputs(c + 1, (2, 3))
                logits_back(c)
                if attends:
                    outputs(c + 1, (4,))
                shared(c, attends)
                if attends:
                    state(c + 1)
                if enters:
                    keys(c + 2)
                    transposes(xn, "a", c + 2, lambda j: shared_part(c, 1, j) if j < 4 else None)
                else:
                    shared_half(c, 1)
                places(c)
                weights(c, u, enters)
                if enters:
                    scores(c + 2)
                down(c, attends)

            keys(0)
            transposes(xn, "a", 0)
            scores(0)
            outputs(0, range(TPC))
            state(0)
            keys(1)
            transposes(xn, "a", 1)
            scores(1)
            wait(pe, "ab_done", 1)
            with pe.Fori(0, CHUNKS // 2 - 1) as i:
                turn(i, 0)
                turn(i, 1)
            turn(CHUNKS // 2 - 1, 0, enters=False)
            turn(CHUNKS // 2 - 1, 1, enters=False, attends=False)

            pe.wait_ge(s["h_done"], CHUNKS + AHEAD)

            def flip(i, r):
                b = 4 * i + r
                pe.wait_ge(s[f"xl{r}"], 16 * (i + 1))
                wait(pe, "b_xT", b - 2)
                for t in range(BT2):
                    for k in range(2):
                        last = nc.tensor.transpose(X[r % 2][0:HD, (2 * t + k) * 128:(2 * t + k + 1) * 128],
                                                   xb[r][:, t, k * HD:(k + 1) * HD], ident[:, :])
                last.then_inc(s["b_tp"], 1)

            def project(i, r):
                b = 4 * i + r
                wait(pe, "b_xT", b)
                wait(pe, "b_wa", b)
                wait(pe, "b_ac", b - 2)
                for m in range(2):
                    for k in range(2):
                        last = mm(U[r % 2][:, m * BLK:(m + 1) * BLK], wac[r % 2][:, (2 * m + k) * HID:(2 * m + k + 1) * HID],
                                  xT[r % 2][:, k, :], start=(k == 0), stop=(k == 1))
                last.then_inc(s["b_up"], 1)

            def project_down(i, r):
                b = 4 * i + r
                wait(pe, "b_wd", b)
                wait(pe, "b_ac", b)
                wait(pe, "b_y", b - 2)
                for t in range(BT2):
                    last = mm(O[r % 2][:, t * D:(t + 1) * D], acb[r % 2][:, t * 128:(t + 1) * 128], wdc[r % 2][:, :],
                              start=True, stop=True)
                last.then_inc(s["b_down"], 1)

            pipeline(pe, flip, project, project_down)


_INS = ['x', 'L0_tok_gamma', 'L0_tok_beta', 'L0_tok_w', 'L0_tok_b', 'L0_attn_w_key', 'L0_attn_w_value', 'L0_attn_w_query',
        'L0_attn_w_gate', 'L0_attn_w_out', 'L0_ffn_gate_w', 'L0_ffn_gate_b', 'L0_ffn_bias', 'L0_ffn_Wu', 'L0_ffn_bu', 'L0_ffn_Wg',
        'L0_ffn_bg', 'L0_ffn_Wd', 'L0_ffn_bd', 'L0_ffn_sWu', 'L0_ffn_sbu', 'L0_ffn_sWg', 'L0_ffn_sbg', 'L0_ffn_sWd', 'L0_ffn_sbd']


_TURNED = ('L0_attn_w_gate', 'L0_attn_w_out', 'L0_ffn_bu', 'L0_ffn_bg')


def shape_constants():
    import numpy as np
    f = np.float32
    t = np.arange(STEPS)
    step = np.arange(R) // NH
    half = (np.arange(128) >= 64).astype(int)
    return {
        "c_ident": np.eye(128, dtype=f),
        "c_rowbase": (np.arange(B) * N).astype(f)[:, None],
        "c_wdec": np.tile((WRITE * DECAY ** (-(t % CS + 1.0))).astype(f), (HD, 1)),
        "c_causal": (step[:, None] < np.arange(CS)[None, :]).astype(f),
        "c_tdecay": (DECAY ** (2.0 * np.arange(TPC)[None, :] + half[:, None])).astype(f),
        "c_tok": (np.arange(TILES)[None, :] * 128 + np.arange(128)[:, None]).astype(f),
        "c_spare": (TOK + np.arange(BT2)[None, :] * 128 + np.arange(128)[:, None]).astype(f),
        "c_base": np.tile(np.arange(E, dtype=f) * ROOM, (128, 1)),
        "c_blki": np.arange(BLOCKS, dtype=f)[None, :],
        "c_earlier": np.triu(np.ones((128, 128), f), 1),
        "c_iota": np.tile(np.arange(E, dtype=f), (128, 1)),
    }


def kernel(**inputs):
    import numpy as np
    import concourse.bacc as bacc
    from concourse.bass_utils import run_bass_kernel_spmd

    nc = bacc.Bacc("TRN2", target_bir_lowering=False, num_devices=1)
    arrays, aps = {}, {}
    given = {n: np.ascontiguousarray(np.asarray(inputs[n]).T if n in _TURNED else inputs[n]) for n in _INS}
    given.update(shape_constants())
    for name, v in given.items():
        arrays[f"in_{name}"] = v
        aps[name] = nc.dram_tensor(f"in_{name}", v.shape, mybir.dt.from_np(v.dtype), kind="ExternalInput").ap()
    out = nc.dram_tensor("out_0", (B, KEEP, D), mybir.dt.float32, kind="ExternalOutput").ap()
    tower(nc, aps, out)
    return run_bass_kernel_spmd(nc, [arrays], core_ids=[0]).results[0]["out_0"]
```
